# Optimizing a Trainium2 kernel written in Bass

```python
import numpy as np
import jax
import jax.numpy as jnp

def _softmax(x, axis=-1):
    return jax.nn.softmax(x, axis=axis)

def _gelu(x):
    return jax.nn.gelu(x, approximate=True)

def _silu(x):
    return jax.nn.silu(x)

def _sigmoid(x):
    return jax.nn.sigmoid(x)

def _layernorm(x, axis=-1, eps=1e-05):
    m = jnp.mean(x, axis=axis, keepdims=True)
    v = jnp.var(x, axis=axis, keepdims=True)
    return (x - m) / jnp.sqrt(v + eps)

def _scatter_add(tgt, idx, src, axis=0):
    return tgt.at[idx].add(src)

def _segment_sum(src, seg, n):
    return jax.ops.segment_sum(src, seg, n)
kernel_name = 'mk_vit_tower_cls_d1_tok_img1024_r4_4e689e'

def setup_inputs(seed: int=0):
    np.random.seed(seed)
    _w = jnp.asarray

    def _rec_inputs():
        import jax
        import jax.numpy as jnp
        _rk = jax.random.key(seed)
        x = -0.000169711 + 1.00022 * jax.random.normal(jax.random.fold_in(_rk, 1), (128, 3, 168, 168), jnp.float32)
        cls_tok = 0.02 * jax.random.normal(jax.random.fold_in(_rk, 5), (1, 1, 256), jnp.float32)
        return (x, cls_tok)
    x, cls_tok = _rec_inputs()

    def _L0_tok_setup():
        import jax, jax.numpy as jnp
        import numpy as np
        C = 256
        H8 = 8
        DH = C // H8
        PS = 14
        CS = 3
        IMG = 168
        B = 4

        def _ln(x, g, b):
            mu = jnp.mean(x, axis=-1, keepdims=True)
            xc = x - mu
            var = jnp.mean(xc * xc, axis=-1, keepdims=True)
            return xc * jax.lax.rsqrt(var + 1e-05) * g + b

        def _forward(pixel_values, conv_w, class_emb, la_ln_q_g, la_ln_q_b, la_wq, la_ln_kv_g, la_ln_kv_b, la_wkv, la_proj_w, la_proj_b, ga_ln_q_g, ga_ln_q_b, ga_wq, ga_ln_kv_g, ga_ln_kv_b, ga_wkv, ga_proj_w, ga_proj_b, mod_w, mod_b):
            b = pixel_values.shape[0]
            pe = jax.lax.conv_general_dilated(pixel_values, conv_w, (PS, PS), 'VALID', dimension_numbers=('NCHW', 'OIHW', 'NCHW'))
            HP = pe.shape[2]
            h = HP // CS
            hw, N = (h * h, CS * CS)
            scale = C ** (-0.5)
            grid = pe.reshape(b, C, h, CS, h, CS)
            red = grid.mean(axis=(3, 5)).reshape(b, C, hw).transpose(0, 2, 1)
            win = grid.transpose(0, 2, 4, 3, 5, 1).reshape(b, hw, N, C)
            q = _ln(red, la_ln_q_g, la_ln_q_b) @ la_wq
            q = q.reshape(b, hw, H8, DH).transpose(0, 2, 1, 3)
            kv = _ln(win, la_ln_kv_g, la_ln_kv_b) @ la_wkv
            kv = kv.reshape(b, hw, N, 2, H8, DH).transpose(3, 0, 4, 1, 2, 5)
            k_, v_ = (kv[0], kv[1])
            attn = jax.nn.softmax(jnp.einsum('bhnd,bhnkd->bhnk', q * scale, k_), axis=-1)
            agg = jnp.einsum('bhnk,bhnkd->bhnd', attn, v_)
            agg = agg.transpose(0, 2, 1, 3).reshape(b, hw, C)
            local_out = red + agg @ la_proj_w + la_proj_b
            cls = jnp.broadcast_to(class_emb, (b, 1, C))
            gq = (_ln(cls, ga_ln_q_g, ga_ln_q_b) @ ga_wq).reshape(b, H8, DH)
            gkv = _ln(local_out, ga_ln_kv_g, ga_ln_kv_b) @ ga_wkv
            gkv = gkv.reshape(b, hw, 2, H8, DH).transpose(2, 0, 3, 1, 4)
            gk, gv = (gkv[0], gkv[1])
            gattn = jax.nn.softmax(jnp.einsum('bhd,bhnd->bhn', gq * scale, gk), axis=-1)
            gagg = jnp.einsum('bhn,bhnd->bhd', gattn, gv).reshape(b, 1, C)
            cls_out = cls + gagg @ ga_proj_w + ga_proj_b
            patch_out = local_out @ mod_w + mod_b
            return jnp.concatenate([patch_out, cls_out], axis=1)
        key = jax.random.key(seed)
        ks = jax.random.split(key, 16)
        nrm = lambda k, shape: jax.random.normal(k, shape, jnp.float32) * 0.02
        return {'pixel_values': jax.random.normal(ks[0], (B, 3, IMG, IMG), jnp.float32), 'pixel_masks': jnp.ones((B, 1, IMG, IMG), jnp.float32), 'conv_w': nrm(ks[1], (C, 3, PS, PS)), 'class_emb': nrm(ks[2], (C,)), 'la_ln_q_g': jnp.ones((C,)), 'la_ln_q_b': jnp.zeros((C,)), 'la_wq': nrm(ks[3], (C, C)), 'la_ln_kv_g': jnp.ones((C,)), 'la_ln_kv_b': jnp.zeros((C,)), 'la_wkv': nrm(ks[4], (C, 2 * C)), 'la_proj_w': nrm(ks[5], (C, C)), 'la_proj_b': jnp.zeros((C,)), 'ga_ln_q_g': jnp.ones((C,)), 'ga_ln_q_b': jnp.zeros((C,)), 'ga_wq': nrm(ks[6], (C, C)), 'ga_ln_kv_g': jnp.ones((C,)), 'ga_ln_kv_b': jnp.zeros((C,)), 'ga_wkv': nrm(ks[7], (C, 2 * C)), 'ga_proj_w': nrm(ks[8], (C, C)), 'ga_proj_b': jnp.zeros((C,)), 'mod_w': nrm(ks[9], (C, C)), 'mod_b': jnp.zeros((C,))}
    _L0_tok_all = _L0_tok_setup()
    _L0_tok_in = {k: v for k, v in _L0_tok_all.items() if k in ('pixel_masks', 'conv_w', 'class_emb', 'la_ln_q_g', 'la_ln_q_b', 'la_wq', 'la_ln_kv_g', 'la_ln_kv_b', 'la_wkv', 'la_proj_w', 'la_proj_b', 'ga_ln_q_g', 'ga_ln_q_b', 'ga_wq', 'ga_ln_kv_g', 'ga_ln_kv_b', 'ga_wkv', 'ga_proj_w', 'ga_proj_b', 'mod_w', 'mod_b')}
    del _L0_tok_all

    def _L0_attn_setup():
        import jax, jax.numpy as jnp
        import numpy as np
        B, S, D = (8, 512, 256)
        key = jax.random.key(seed)
        x = jax.random.normal(key, (B, S, D), dtype=jnp.float32)
        return {'x': x}
    _L0_attn_all = _L0_attn_setup()
    _L0_attn_in = {k: v for k, v in _L0_attn_all.items() if k in ()}
    del _L0_attn_all

    def _L0_ffn_setup():
        import jax, jax.numpy as jnp
        import numpy as np
        E = 16
        K = 2
        LOAD = 1.0

        def _dispatch(xb, pb, cap):
            T, C = xb.shape
            top_k_probs, ei = jax.lax.top_k(pb, K)
            flat = ei.swapaxes(0, 1).ravel()
            one_hot = jax.nn.one_hot(flat, E, dtype=jnp.int32)
            pos = jnp.cumsum(one_hot, axis=0) * one_hot
            pos = pos.reshape(K, T, E).swapaxes(0, 1)
            pos = jnp.max(pos, axis=-1) - 1
            ei2 = flat.reshape(K, T).swapaxes(0, 1)
            xr = jnp.repeat(xb, K, axis=0)
            buf = jnp.zeros((E, cap, C), xb.dtype)
            buf = buf.at[ei2.ravel(), pos.ravel()].set(xr, mode='drop')
            return (top_k_probs, pos, ei2, buf)

        def _collect(eo_b, ei_b, pos_b, tk_b):
            out = eo_b[ei_b, pos_b]
            return jnp.sum(tk_b[..., None] * out, axis=1)
        key = jax.random.key(seed)
        k1, k2, k3, k4, k5 = jax.random.split(key, 5)
        B, T, C, H = (8, 1024, 256, 128)
        n_layer = 12
        x = jax.random.normal(k1, (B, T, C), dtype=jnp.float32)
        w_router = jax.random.normal(k2, (C, E), dtype=jnp.float32) * 0.02
        w_fc = jax.random.normal(k3, (E, C, H), dtype=jnp.float32) * 0.02
        w_gate = jax.random.normal(k4, (E, C, H), dtype=jnp.float32) * 0.02
        w_proj = jax.random.normal(k5, (E, H, C), dtype=jnp.float32) * (0.02 * (2 * n_layer) ** (-0.5))
        return {'x': x, 'w_router': w_router, 'w_fc': w_fc, 'w_gate': w_gate, 'w_proj': w_proj}
    _L0_ffn_all = _L0_ffn_setup()
    _L0_ffn_in = {k: v for k, v in _L0_ffn_all.items() if k in ('w_router', 'w_fc', 'w_gate', 'w_proj')}
    del _L0_ffn_all
    return {'x': x, 'cls_tok': cls_tok, 'L0_tok_pixel_masks': _L0_tok_in['pixel_masks'], 'L0_tok_conv_w': _L0_tok_in['conv_w'], 'L0_tok_class_emb': _L0_tok_in['class_emb'], 'L0_tok_la_ln_q_g': _L0_tok_in['la_ln_q_g'], 'L0_tok_la_ln_q_b': _L0_tok_in['la_ln_q_b'], 'L0_tok_la_wq': _L0_tok_in['la_wq'], 'L0_tok_la_ln_kv_g': _L0_tok_in['la_ln_kv_g'], 'L0_tok_la_ln_kv_b': _L0_tok_in['la_ln_kv_b'], 'L0_tok_la_wkv': _L0_tok_in['la_wkv'], 'L0_tok_la_proj_w': _L0_tok_in['la_proj_w'], 'L0_tok_la_proj_b': _L0_tok_in['la_proj_b'], 'L0_tok_ga_ln_q_g': _L0_tok_in['ga_ln_q_g'], 'L0_tok_ga_ln_q_b': _L0_tok_in['ga_ln_q_b'], 'L0_tok_ga_wq': _L0_tok_in['ga_wq'], 'L0_tok_ga_ln_kv_g': _L0_tok_in['ga_ln_kv_g'], 'L0_tok_ga_ln_kv_b': _L0_tok_in['ga_ln_kv_b'], 'L0_tok_ga_wkv': _L0_tok_in['ga_wkv'], 'L0_tok_ga_proj_w': _L0_tok_in['ga_proj_w'], 'L0_tok_ga_proj_b': _L0_tok_in['ga_proj_b'], 'L0_tok_mod_w': _L0_tok_in['mod_w'], 'L0_tok_mod_b': _L0_tok_in['mod_b'], 'L0_ffn_w_router': _L0_ffn_in['w_router'], 'L0_ffn_w_fc': _L0_ffn_in['w_fc'], 'L0_ffn_w_gate': _L0_ffn_in['w_gate'], 'L0_ffn_w_proj': _L0_ffn_in['w_proj']}

def reference(x, cls_tok, L0_tok_pixel_masks, L0_tok_conv_w, L0_tok_class_emb, L0_tok_la_ln_q_g, L0_tok_la_ln_q_b, L0_tok_la_wq, L0_tok_la_ln_kv_g, L0_tok_la_ln_kv_b, L0_tok_la_wkv, L0_tok_la_proj_w, L0_tok_la_proj_b, L0_tok_ga_ln_q_g, L0_tok_ga_ln_q_b, L0_tok_ga_wq, L0_tok_ga_ln_kv_g, L0_tok_ga_ln_kv_b, L0_tok_ga_wkv, L0_tok_ga_proj_w, L0_tok_ga_proj_b, L0_tok_mod_w, L0_tok_mod_b, L0_ffn_w_router, L0_ffn_w_fc, L0_ffn_w_gate, L0_ffn_w_proj):
    import jax
    import jax.numpy as jnp

    def _L0_tok_ref(pixel_values, pixel_masks, conv_w, class_emb, la_ln_q_g, la_ln_q_b, la_wq, la_ln_kv_g, la_ln_kv_b, la_wkv, la_proj_w, la_proj_b, ga_ln_q_g, ga_ln_q_b, ga_wq, ga_ln_kv_g, ga_ln_kv_b, ga_wkv, ga_proj_w, ga_proj_b, mod_w, mod_b):
        import jax, jax.numpy as jnp
        import numpy as np
        C = 256
        H8 = 8
        DH = C // H8
        PS = 14
        CS = 3
        IMG = 168
        B = 4

        def _ln(x, g, b):
            mu = jnp.mean(x, axis=-1, keepdims=True)
            xc = x - mu
            var = jnp.mean(xc * xc, axis=-1, keepdims=True)
            return xc * jax.lax.rsqrt(var + 1e-05) * g + b

        def _forward(pixel_values, conv_w, class_emb, la_ln_q_g, la_ln_q_b, la_wq, la_ln_kv_g, la_ln_kv_b, la_wkv, la_proj_w, la_proj_b, ga_ln_q_g, ga_ln_q_b, ga_wq, ga_ln_kv_g, ga_ln_kv_b, ga_wkv, ga_proj_w, ga_proj_b, mod_w, mod_b):
            b = pixel_values.shape[0]
            pe = jax.lax.conv_general_dilated(pixel_values, conv_w, (PS, PS), 'VALID', dimension_numbers=('NCHW', 'OIHW', 'NCHW'))
            HP = pe.shape[2]
            h = HP // CS
            hw, N = (h * h, CS * CS)
            scale = C ** (-0.5)
            grid = pe.reshape(b, C, h, CS, h, CS)
            red = grid.mean(axis=(3, 5)).reshape(b, C, hw).transpose(0, 2, 1)
            win = grid.transpose(0, 2, 4, 3, 5, 1).reshape(b, hw, N, C)
            q = _ln(red, la_ln_q_g, la_ln_q_b) @ la_wq
            q = q.reshape(b, hw, H8, DH).transpose(0, 2, 1, 3)
            kv = _ln(win, la_ln_kv_g, la_ln_kv_b) @ la_wkv
            kv = kv.reshape(b, hw, N, 2, H8, DH).transpose(3, 0, 4, 1, 2, 5)
            k_, v_ = (kv[0], kv[1])
            attn = jax.nn.softmax(jnp.einsum('bhnd,bhnkd->bhnk', q * scale, k_), axis=-1)
            agg = jnp.einsum('bhnk,bhnkd->bhnd', attn, v_)
            agg = agg.transpose(0, 2, 1, 3).reshape(b, hw, C)
            local_out = red + agg @ la_proj_w + la_proj_b
            cls = jnp.broadcast_to(class_emb, (b, 1, C))
            gq = (_ln(cls, ga_ln_q_g, ga_ln_q_b) @ ga_wq).reshape(b, H8, DH)
            gkv = _ln(local_out, ga_ln_kv_g, ga_ln_kv_b) @ ga_wkv
            gkv = gkv.reshape(b, hw, 2, H8, DH).transpose(2, 0, 3, 1, 4)
            gk, gv = (gkv[0], gkv[1])
            gattn = jax.nn.softmax(jnp.einsum('bhd,bhnd->bhn', gq * scale, gk), axis=-1)
            gagg = jnp.einsum('bhn,bhnd->bhd', gattn, gv).reshape(b, 1, C)
            cls_out = cls + gagg @ ga_proj_w + ga_proj_b
            patch_out = local_out @ mod_w + mod_b
            return jnp.concatenate([patch_out, cls_out], axis=1)
        del pixel_masks
        return _forward(pixel_values, conv_w, class_emb, la_ln_q_g, la_ln_q_b, la_wq, la_ln_kv_g, la_ln_kv_b, la_wkv, la_proj_w, la_proj_b, ga_ln_q_g, ga_ln_q_b, ga_wq, ga_ln_kv_g, ga_ln_kv_b, ga_wkv, ga_proj_w, ga_proj_b, mod_w, mod_b)

    def _L0_attn_ref(x):
        import jax, jax.numpy as jnp
        import numpy as np
        B, S, D = (8, 512, 256)
        scores = jnp.einsum('bid,bjd->bij', x, x)
        attn = jax.nn.softmax(scores, axis=1)
        context = jnp.einsum('bij,bjd->bid', attn, x)
        return context

    def _L0_ffn_ref(x, w_router, w_fc, w_gate, w_proj):
        import jax, jax.numpy as jnp
        import numpy as np
        E = 16
        K = 2
        LOAD = 1.0

        def _dispatch(xb, pb, cap):
            T, C = xb.shape
            top_k_probs, ei = jax.lax.top_k(pb, K)
            flat = ei.swapaxes(0, 1).ravel()
            one_hot = jax.nn.one_hot(flat, E, dtype=jnp.int32)
            pos = jnp.cumsum(one_hot, axis=0) * one_hot
            pos = pos.reshape(K, T, E).swapaxes(0, 1)
            pos = jnp.max(pos, axis=-1) - 1
            ei2 = flat.reshape(K, T).swapaxes(0, 1)
            xr = jnp.repeat(xb, K, axis=0)
            buf = jnp.zeros((E, cap, C), xb.dtype)
            buf = buf.at[ei2.ravel(), pos.ravel()].set(xr, mode='drop')
            return (top_k_probs, pos, ei2, buf)

        def _collect(eo_b, ei_b, pos_b, tk_b):
            out = eo_b[ei_b, pos_b]
            return jnp.sum(tk_b[..., None] * out, axis=1)
        B, T, C = x.shape
        cap = int(LOAD * K * max(1, T / E))
        g = jnp.einsum('btc,ce->bte', x, w_router)
        gate_probs = jax.nn.softmax(g, axis=-1)
        top_k_probs, positions, indices, expert_inputs = jax.vmap(lambda xb, pb: _dispatch(xb, pb, cap))(x, gate_probs)
        expert_inputs = jnp.swapaxes(expert_inputs, 0, 1).reshape(E, B * cap, C)
        gg = jnp.einsum('enc,ech->enh', expert_inputs, w_gate)
        h = jnp.einsum('enc,ech->enh', expert_inputs, w_fc)
        h = jax.nn.silu(gg) * h
        o = jnp.einsum('enh,ehc->enc', h, w_proj)
        expert_outputs = jnp.swapaxes(o.reshape(E, B, cap, C), 0, 1)
        y = jax.vmap(_collect)(expert_outputs, indices, positions, top_k_probs)
        return y
    h = _L0_tok_ref(x, L0_tok_pixel_masks, L0_tok_conv_w, L0_tok_class_emb, L0_tok_la_ln_q_g, L0_tok_la_ln_q_b, L0_tok_la_wq, L0_tok_la_ln_kv_g, L0_tok_la_ln_kv_b, L0_tok_la_wkv, L0_tok_la_proj_w, L0_tok_la_proj_b, L0_tok_ga_ln_q_g, L0_tok_ga_ln_q_b, L0_tok_ga_wq, L0_tok_ga_ln_kv_g, L0_tok_ga_ln_kv_b, L0_tok_ga_wkv, L0_tok_ga_proj_w, L0_tok_ga_proj_b, L0_tok_mod_w, L0_tok_mod_b)
    h = jnp.concatenate([jnp.broadcast_to(cls_tok, (h.shape[0], 1, h.shape[2])), h], axis=1)
    h = h + _L0_attn_ref(_layernorm(h, axis=-1))
    h = h + _L0_ffn_ref(_layernorm(h, axis=-1), L0_ffn_w_router, L0_ffn_w_fc, L0_ffn_w_gate, L0_ffn_w_proj)
    return h

_drawn_inputs = setup_inputs


def setup_inputs(seed=0):
    import zlib

    import numpy as np

    out = dict(_drawn_inputs(seed))
    spreads = {'L0_tok_pixel_masks': (1.0, 0.2),
     'L0_tok_la_ln_q_g': (1.0, 0.6),
     'L0_tok_la_ln_q_b': (0.0, 0.8),
     'L0_tok_la_ln_kv_g': (1.0, 0.6),
     'L0_tok_la_ln_kv_b': (0.0, 0.267),
     'L0_tok_la_proj_b': (0.0, 0.1),
     'L0_tok_ga_ln_q_g': (1.0, 0.6),
     'L0_tok_ga_ln_q_b': (0.0, 0.8),
     'L0_tok_ga_ln_kv_g': (1.0, 0.6),
     'L0_tok_ga_ln_kv_b': (0.0, 0.349),
     'L0_tok_ga_proj_b': (0.0, 0.1),
     'L0_tok_mod_b': (0.0, 0.1)}
    factors = {'L0_tok_la_wq': 8.0,
     'L0_tok_ga_wq': 8.0,
     'L0_ffn_w_router': 8.0,
     'L0_ffn_w_fc': 8.0,
     'L0_ffn_w_gate': 8.0,
     'L0_ffn_w_proj': 8.0}
    for name, (base, spread) in spreads.items():
        noise = np.random.default_rng([zlib.crc32(name.encode()), seed]).standard_normal(out[name].shape)
        drawn = base * np.exp(spread * noise) if base else spread * noise
        out[name] = jnp.asarray(drawn.astype(out[name].dtype))
    for name, factor in factors.items():
        out[name] = (out[name] * factor).astype(out[name].dtype)
    return out
```

```python
from contextlib import ExitStack

import concourse.bass as bass
from concourse import mybir

F32 = mybir.dt.float32
I32 = mybir.dt.int32
ALU = mybir.AluOpType
ACT = mybir.ActivationFunctionType
AX_X = mybir.AxisListType.X

P = 128
EPS = 1e-5
IMGS, CH, IMG, PS, CS = 128, 3, 168, 14, 3
C = 256
HEADS, DH = 8, 32
SIDE = IMG // PS // CS
WIN = SIDE * SIDE
KEYS = CS * CS
PIX = CH * PS * PS
KFULL = PIX // P
KREST = PIX - KFULL * P
KPAD = -(-KREST // 16) * 16
GI = 8
NG = IMGS // GI
GW = GI * WIN
GT = GW * KEYS
BLK = GT // 3
NBLK = GT // BLK
HALF = 8 * KEYS
NH = GT // HALF
SCALE = C ** -0.5

TOK = WIN + 2
TI = 7
R = TI * TOK
NT = -(-IMGS // TI)
LASTR = (IMGS - (NT - 1) * TI) * TOK
E, CAP, H = 16, 2, 128
TS = TI * CAP
SLOTS = NT * TS
ES = E * TS
EH = ES // 2
NEG = 1e30
COLS = ("la_ln_q_g", "la_ln_q_b", "la_ln_kv_g", "la_ln_kv_b", "la_proj_b",
        "ga_ln_q_g", "ga_ln_q_b", "ga_ln_kv_g", "ga_ln_kv_b", "class_emb")


def tower(nc, a, out):
    with ExitStack() as ctx:
        def sb(name, shape):
            return ctx.enter_context(nc.sbuf_tensor(name, shape, F32))

        def sem(name):
            return ctx.enter_context(nc.semaphore(name))

        scratch = nc.dram_tensor("tower_rows", [IMGS * TOK, C], F32, kind="Internal").ap()
        scratch_img = scratch.rearrange("(b t) c -> b t c", t=TOK)

        ident = sb("ident", [P, P])
        mean_ones = sb("mean_ones", [P, P])
        own_window = sb("own_window", [P, 8])
        own_image = sb("own_image", [P, GI])
        own_seq = sb("own_seq", [P, TI])
        same_seq = sb("same_seq", [P, R])
        earlier = sb("earlier", [P, R])
        neg_mask = sb("neg_mask", [P, R])
        rank_w = sb("rank_w", [P, E])
        w_conv = sb("w_conv", [P, KFULL + 1, C])
        wq = sb("wq", [P, 2, C])
        wkv = sb("wkv", [P, 2, 2 * C])
        proj = sb("proj", [P, 2, C])
        gwq = sb("gwq", [P, 2, C])
        gwkv = sb("gwkv", [P, 2, 2 * C])
        gproj = sb("gproj", [P, 2, C])
        mod_w = sb("mod_w", [P, 2, C])
        router = sb("router", [P, 2, E])
        col_vectors = sb("col_vectors", [P, len(COLS), 2])
        cols = {n: col_vectors[:, i, :] for i, n in enumerate(COLS)}
        ROWS = ["la_ln_kv_g", "ga_ln_kv_g", "mod_b", "class_emb", "ga_proj_b"]
        rows = {n: sb("row_" + n, [P, C]) for n in ROWS}
        wk_fold = sb("wk_fold", [P, 2, C])
        wv_fold = sb("wv_fold", [P, 2, C])
        gwk_fold = sb("gwk_fold", [P, 2, C])
        gwv_fold = sb("gwv_fold", [P, 2, C])
        v_bias = sb("v_bias", [P, 2])
        gv_bias = sb("gv_bias", [P, 2])
        gq_block = sb("gq_block", [P, 2, HEADS])
        gqk = sb("gqk", [P, 2, HEADS])
        small = sb("small", [P, 16])
        newton = sb("newton", [P, 2, 32])
        var = sb("var", [P, 32])

        xs = sb("xs", [P, 2, KFULL + 1, GT])
        arena = sb("arena", [P, 2 * 2 * GT + NH * C + 2 * HEADS * P * 2])
        o1 = 4 * GT
        o2 = o1 + NH * C
        o3 = o2 + 2 * HEADS * P
        pe_t = arena[:, 0:o1].rearrange("p (s m t) -> p s m t", s=2, m=2)
        tok = arena[:, o1:o2].rearrange("p (t c) -> p t c", t=NH)
        qk = arena[:, o2:o3].rearrange("p (m h w) -> p m h w", m=2, h=HEADS)
        ctxv = arena[:, o3:o3 + 2 * HEADS * P].rearrange("p (m h w) -> p m h w", m=2, h=HEADS)
        gv_all = sb("gv_all", [P, NG, C])
        gs_all = sb("gs_all", [P, NG, HEADS])
        lo_var = sb("lo_var", [P, NG])
        lo_rstd = sb("lo_rstd", [P, NG])
        red_sum = sb("red_sum", [P, 2, P])
        red_hat = sb("red_hat", [P, C])
        red_hat_t = sb("red_hat_t", [P, 2, P])
        q_t = sb("q_t", [P, 2, P])
        stats = sb("stats", [P, NH, 6])
        tmp16 = sb("tmp16", [P, 3, NH])
        rstd = sb("rstd", [P, NH])
        masked = sb("masked", [P, NH * HEADS, 8])
        score = sb("score", [P, NH, HEADS])
        soft = sb("soft", [P, 8, KEYS])
        soft_max = sb("soft_max", [P, 8])
        soft_sum = sb("soft_sum", [P, 8])
        attn = sb("attn", [P, NH, HEADS])
        spread = sb("spread", [P, NH * HEADS, 8])
        agg_t = sb("agg_t", [P, 2, P])
        lo_t = sb("lo_t", [P, 2, P])
        lo_part = sb("lo_part", [P, 2, P])
        st6 = sb("st6", [P, 6])
        mv = sb("mv", [P, 2])
        patch = sb("patch", [P, C])

        XB = 2 * E * SLOTS
        slots_t = sb("slots_t", [P, XB])
        xb = slots_t[:, :].rearrange("p (m t e s) -> p m t e s", m=2, t=NT, e=E)
        xflat = xs[:, :, :, :].rearrange("p a b c -> p (a b c)")
        w_gate = xflat[:, 0:E * C].rearrange("p (e m h) -> p e m h", e=E, m=2)
        w_fc = xflat[:, E * C:2 * E * C].rearrange("p (e m h) -> p e m h", e=E, m=2)
        w_proj = gv_all[:, :, :]
        h_rows = arena[:, 0:NT * C].rearrange("p (t c) -> p t c", t=NT)
        n_rows = arena[:, NT * C:2 * NT * C].rearrange("p (t c) -> p t c", t=NT)
        g0 = 2 * NT * C
        assert g0 + 6 * NT * E <= o3 + 2 * HEADS * P
        logit = arena[:, g0:g0 + NT * E].rearrange("p (t e) -> p t e", t=NT)
        hot = arena[:, g0 + NT * E:g0 + 3 * NT * E].rearrange("p (k t e) -> p k t e", k=2, t=NT)
        gt1 = arena[:, g0 + 3 * NT * E:g0 + 4 * NT * E].rearrange("p (t e) -> p t e", t=NT)
        gt2 = arena[:, g0 + 4 * NT * E:g0 + 5 * NT * E].rearrange("p (t e) -> p t e", t=NT)
        gt3 = arena[:, g0 + 5 * NT * E:g0 + 6 * NT * E].rearrange("p (t e) -> p t e", t=NT)
        gcol = sb("gcol", [P, NT])
        stat6 = masked[:, 0:NT, :][:, :, 0:6]
        row_mv = masked[:, NT:2 * NT, :][:, :, 0:2]
        row_var = tmp16[:, :, :].rearrange("p a b -> p (a b)")[:, 0:NT]
        g1 = g0 + 6 * NT * E
        take = arena[:, g1:g1 + NT * E * CAP].rearrange("p (a s) -> p a s", s=CAP)
        give = arena[:, g1 + NT * E * CAP:g1 + 2 * NT * E * CAP].rearrange("p (a s) -> p a s", s=CAP)
        assert g1 + 2 * NT * E * CAP <= o3 + 2 * HEADS * P
        s_mat = sb("s_mat", [P, P])
        x0 = 2 * E * C

        def behind(n):
            nonlocal x0
            x0 += n
            assert x0 <= 2 * (KFULL + 1) * GT
            return xflat[:, x0 - n:x0]

        disp = behind(ES).rearrange("p (e b s) -> p e b s", e=E, b=TI)
        comb = behind(ES).rearrange("p (e b s) -> p e b s", e=E, b=TI)
        comb_t = behind(2 * R).rearrange("p (k r) -> p k r", k=2)
        nt_t = behind(2 * R).rearrange("p (k r) -> p k r", k=2)
        o_rows = behind(2 * C).rearrange("p (k c) -> p k c", k=2)
        y_rows = behind(2 * C).rearrange("p (k c) -> p k c", k=2)
        hid = behind(2 * SLOTS).rearrange("p (k s) -> p k s", k=2)

        ps = ctx.enter_context(nc.psum_tensor("ps", [P, 8, 512], F32))

        masks_made = sem("masks_made")
        weights_in = sem("weights_in")
        rows_in = sem("rows_in")
        x_in = [sem("x_in_even"), sem("x_in_odd")]
        conv_done = sem("conv_done")
        conv_moved = sem("conv_moved")
        pe_step = sem("pe_step")
        act_step = sem("act_step")
        dve_step = sem("dve_step")
        tok_turned = sem("tok_turned")
        tok_moved = sem("tok_moved")
        ctx_done = sem("ctx_done")
        ctx_moved = sem("ctx_moved")
        attn_turned = sem("attn_turned")
        patch_out = sem("patch_out")
        group_kept = sem("group_kept")
        cls_tok_out = sem("cls_tok_out")
        cls_out = sem("cls_out")
        pre = sem("pre")
        pre_v = sem("pre_v")
        ffn_in = sem("ffn_in")
        p2 = sem("p2")
        p2v = sem("p2v")
        p2a = sem("p2a")
        h_in = sem("h_in")
        pad_zero = sem("pad_zero")
        out_sem = [sem("out_even"), sem("out_odd")]

        block = ctx.enter_context(nc.Block())

        def mpn(ap):
            return ap.rearrange("(m p) n -> p m n", p=P)

        NPE = 13
        NACT = 10
        NR = 11
        RED_HAT = 2 + 1 + 5 + NR + 1
        QK_MOVED = RED_HAT + 2
        SCORED = QK_MOVED + NH + 5 + NR + 5
        SUBTRACTED = SCORED + 2
        SOFTMAXED = SUBTRACTED + 3
        SPREAD = SOFTMAXED + 2
        LOCAL = SPREAD + 1
        LO_STATS = LOCAL + 1
        PATCHED = LO_STATS + 5
        NDVE = PATCHED + 1
        SQ_DONE = 4 + 2 * 5 + 2 + 2 + 3
        QHAT_DONE = SQ_DONE + 1 + NR + 3
        GQ_DONE = QHAT_DONE + HEADS
        SETUP_V = GQ_DONE + 2
        CLASS_V = SETUP_V + NR
        MASKS = 8 + 8 + 2 + E
        LN1_DONE = 2 * NT + 1 + NR + NT
        NV = 5
        LN2_DONE = LN1_DONE + NV * NT + 2 * NT + 1 + NR + NT
        GATE_MAX = LN2_DONE + 2
        HOT_DONE = GATE_MAX + 4 + 5 + 2 + 5
        DISP_V = HOT_DONE + 6 + 4 + 1
        HID_AT = DISP_V + NT
        COMB_V = HID_AT + E
        DISP_AT = 5 * NT + 2
        EXP_AT = DISP_AT + NT
        COMB_AT = EXP_AT + 2 * E

        W_DMAS = 2 + 8 + len(ROWS) + 1

        @block.sync
        def _(sp):
            def load(g, slot):
                sp.dma_start(xs[:, slot, 0:KFULL, :], a["x"][g, 0:KFULL * P, :].rearrange("(k p) t -> p k t", p=P))\
                    .then_inc(x_in[slot], 16)
                sp.dma_start(xs[0:KPAD, slot, KFULL, :], a["x"][g, KFULL * P:KFULL * P + KPAD, :])\
                    .then_inc(x_in[slot], 16)

            load(0, 0)
            load(1, 1)
            sp.dma_start(scratch_img[:, 0:1, :], a["cls_tok"].broadcast_to([IMGS, 1, C])).then_inc(cls_tok_out, 16)

            def step(g, slot, more):
                if more:
                    sp.wait_ge(conv_done, g * 2 * NBLK + 2 * NBLK)
                    load(g + 2, slot)
                sp.wait_ge(dve_step, g * NDVE + PATCHED)
                sp.dma_start(scratch_img[bass.ds(g * GI, GI), 1:1 + WIN, :], patch[:, :])\
                    .then_inc(patch_out, 16)

            step(0, 0, True)
            with sp.Fori(0, NG // 2 - 2) as r:
                step(2 * r + 1, 1, True)
                step(2 * r + 2, 0, True)
            step(NG - 3, 1, True)
            step(NG - 2, 0, False)
            step(NG - 1, 1, False)
            sp.wait_ge(conv_done, NG * 2 * NBLK)
            sp.dma_start(w_gate, a["w_gate"].rearrange("e (m p) h -> p e m h", p=P)).then_inc(ffn_in, 16)
            sp.dma_start(w_fc, a["w_fc"].rearrange("e (m p) h -> p e m h", p=P)).then_inc(ffn_in, 16)
            sp.wait_ge(pre, 12)
            sp.dma_start(w_proj, a["w_proj"].rearrange("e h c -> h e c")).then_inc(ffn_in, 16)
            sp.wait_ge(pre_v, CLASS_V + 9)
            sp.dma_start(scratch_img[:, 1 + WIN, :], patch[:, :]).then_inc(cls_out, 16)
            sp.wait_ge(cls_tok_out, 16)
            sp.wait_ge(patch_out, 16 * NG)
            sp.wait_ge(cls_out, 16)
            sp.wait_ge(pad_zero, 1)
            for t in range(NT - 1):
                sp.dma_start(h_rows[0:R, t, :], scratch[t * R:(t + 1) * R, :]).then_inc(h_in, 16)
            sp.dma_start(h_rows[0:LASTR, NT - 1, :], scratch[(NT - 1) * R:IMGS * TOK, :]).then_inc(h_in, 16)
            for t in range(NT):
                sp.wait_ge(p2v, COMB_V + 3 * t + 2)
                n = R if t < NT - 1 else LASTR
                sp.dma_start(out[t * R:t * R + n, :], y_rows[0:n, t % 2, :]).then_inc(out_sem[t % 2], 16)
            sp.wait_ge(out_sem[0], 16 * ((NT + 1) // 2))
            sp.wait_ge(out_sem[1], 16 * (NT // 2))

        @block.gpsimd
        def _(pool):
            pool.memset(ident[:, :], 0.0).then_inc(masks_made, 1)
            pool.memset(mean_ones[:, :], 1.0 / C).then_inc(masks_made, 1)
            for m in (own_window, own_image, own_seq, same_seq):
                pool.memset(m[:, :], 1.0).then_inc(masks_made, 1)
            pool.memset(gq_block[:, :, :], 0.0).then_inc(masks_made, 1)
            n = 7
            pool.wait_ge(masks_made, n)
            pool.affine_select(out=ident[:, :], in_=ident[:, :], compare_op=ALU.not_equal, fill=1.0, base=0,
                               pattern=[[-1, P]], channel_multiplier=1).then_inc(masks_made, 1)
            n += 1
            for m, size, pat in ((own_window, KEYS, [[-KEYS, 8]]), (own_image, WIN, [[-WIN, GI]]),
                                 (own_seq, TOK, [[-TOK, TI]]), (same_seq, TOK, [[-TOK, TI], [0, TOK]])):
                up = [[-s, k] for s, k in pat]
                pool.affine_select(out=m[:, :], in_=m[:, :], compare_op=ALU.is_ge, fill=0.0, base=0,
                                   pattern=pat, channel_multiplier=1).then_inc(masks_made, 1)
                n += 1
                pool.wait_ge(masks_made, n)
                pool.affine_select(out=m[:, :], in_=m[:, :], compare_op=ALU.is_ge, fill=0.0, base=size - 1,
                                   pattern=up, channel_multiplier=-1).then_inc(masks_made, 1)
                n += 1
                pool.wait_ge(masks_made, n)
            pool.affine_select(out=earlier[:, :], in_=same_seq[:, :], compare_op=ALU.is_ge, fill=0.0, base=-1,
                               pattern=[[1, R]], channel_multiplier=-1).then_inc(masks_made, 1)
            pool.tensor_scalar(neg_mask[:, :], same_seq[:, :], -1.0, NEG, ALU.add, ALU.mult).then_inc(masks_made, 1)
            for e in range(E):
                pool.memset(rank_w[:, e:e + 1], float(E - e)).then_inc(masks_made, 1)
            n += 2 + E
            assert n == MASKS
            pool.wait_ge(pre_v, CLASS_V + 9)
            pool.memset(h_rows[:, NT - 1, :], 0.0).then_inc(pad_zero, 1)

        @block.scalar
        def _(act):
            act.dma_start(w_conv[:, 0:KFULL, :], a["conv_w"][0:KFULL * P, :].rearrange("(k p) c -> p k c", p=P))\
                .then_inc(weights_in, 16)
            act.dma_start(w_conv[0:KPAD, KFULL, :], a["conv_w"][KFULL * P:KFULL * P + KPAD, :])\
                .then_inc(weights_in, 16)
            for t, n in ((wkv, "la_wkv"), (wq, "la_wq"), (gwkv, "ga_wkv"), (gwq, "ga_wq"), (proj, "la_proj_w"),
                         (gproj, "ga_proj_w"), (mod_w, "mod_w"), (router, "w_router")):
                act.dma_start(t[:, :, :], mpn(a[n])).then_inc(weights_in, 16)
            for n in ROWS:
                act.dma_start(rows[n][:, :], a[n].rearrange("(o c) -> o c", o=1).broadcast_to([P, C]))\
                    .then_inc(weights_in, 16)
            act.dma_start(col_vectors[:, :, :], a["cols"]).then_inc(weights_in, 16)

            def conv_move(g, slot, n):
                act.wait_ge(conv_done, g * 2 * NBLK + n + 1)
                act.activation(pe_t[:, slot, n % 2, BLK * (n // 2):BLK * (n // 2 + 1)], ps[:, n % 2, 0:BLK], ACT.Copy)\
                    .then_inc(conv_moved, 1)

            def chain(g, slot, nxt):
                conv = (lambda n: conv_move(g + 1, 1 - slot, n)) if nxt else (lambda n: None)
                conv(0)
                act.wait_ge(pe_step, g * NPE + 2)
                for m in range(2):
                    act.activation(red_hat_t[:, m, :], ps[:, 7, P * m:P * m + P], ACT.Identity,
                                   bias=cols["la_ln_q_b"][:, m:m + 1], scale=cols["la_ln_q_g"][:, m:m + 1])\
                        .then_inc(act_step, 1)
                conv(1)
                act.wait_ge(pe_step, g * NPE + 3)
                act.activation(q_t[:, :, :], ps[:, 6, 0:C], ACT.Copy).then_inc(act_step, 1)
                act.wait_ge(pe_step, g * NPE + 4)
                for j in range(2):
                    act.activation(qk[:, :, j:HEADS:4, :],
                                   ps[:, 2 + j, :].rearrange("p (m h w) -> p m h w", m=2, h=2), ACT.Copy)\
                        .then_inc(act_step, 1)
                for k in range(NH // 2):
                    act.wait_ge(tok_turned, g * (NH // 2) + k + 1)
                    act.activation(tok[0:HALF, 2 * k:2 * k + 2, :], ps[0:HALF, 2 + k % 2, :], ACT.Copy)\
                        .then_inc(tok_moved, 1)
                    if k == 1:
                        conv(2)
                    if k == 5:
                        conv(3)
                conv(4)
                act.wait_ge(dve_step, g * NDVE + SUBTRACTED)
                act.activation(soft[:, :, :], soft[:, :, :], ACT.Exp).then_inc(act_step, 1)
                for k in range(4):
                    m, half = k // 2, k % 2
                    act.wait_ge(ctx_done, g * 4 + k + 1)
                    act.activation(ctxv[:, m, :, 64 * half:64 * half + 64].rearrange("p h (t w) -> p t h w", w=8),
                                   ps[:, 4 + k % 2, :].rearrange("p (t h w) -> p t h w", t=8, h=8), ACT.Copy)\
                        .then_inc(ctx_moved, 1)
                act.wait_ge(pe_step, g * NPE + 8)
                for m in range(2):
                    act.activation(agg_t[:, m, :], ps[:, 6, P * m:P * m + P], ACT.Identity,
                                   bias=v_bias[:, m:m + 1]).then_inc(act_step, 1)
                act.wait_ge(pe_step, g * NPE + 9)
                for m in range(2):
                    act.activation(lo_part[:, m, :], ps[:, 7, P * m:P * m + P], ACT.Identity,
                                   bias=cols["la_proj_b"][:, m:m + 1]).then_inc(act_step, 1)
                conv(5)
                act.wait_ge(pe_step, g * NPE + 12)
                act.activation(gv_all[:, bass.ds(g, 1), :], ps[:, 6, 0:C], ACT.Copy).then_inc(group_kept, 1)

            act.wait_ge(pre_v, SETUP_V)
            for n in range(2 * NBLK):
                conv_move(0, 0, n)
            chain(0, 0, True)
            with act.Fori(0, NG // 2 - 1) as r:
                chain(2 * r + 1, 1, True)
                chain(2 * r + 2, 0, True)
            chain(NG - 1, 1, False)

            act.wait_ge(pre_v, CLASS_V + 3)
            act.activation(s_mat[:, 0:P], s_mat[:, 0:P], ACT.Exp).then_inc(p2a, 1)
            act.wait_ge(pre, 12)
            for m in range(2):
                act.activation(agg_t[:, m, :], ps[:, 1, P * m:P * m + P], ACT.Identity,
                               bias=gv_bias[:, m:m + 1]).then_inc(p2a, 1)
            na = 3
            for t in range(NT):
                act.wait_ge(p2, 3 * t + 1)
                act.activation(nt_t[:, :, :], ps[:, 0, 0:2 * R], ACT.Copy).then_inc(p2a, 1)
                act.wait_ge(p2v, LN1_DONE + NV * t + 2)
                act.activation(s_mat[0:R, 0:R], s_mat[0:R, 0:R], ACT.Exp, bias=small[0:R, 4:5],
                               accum_out=small[0:R, 5:6]).then_inc(p2a, 1)
            for t in range(NT):
                act.wait_ge(p2, 3 * NT + 2 * t + 1)
                act.activation(nt_t[:, :, :], ps[:, 0, 0:2 * R], ACT.Copy).then_inc(p2a, 1)
                act.wait_ge(p2, 3 * NT + 2 * t + 2)
                act.activation(logit[0:R, t, :], ps[0:R, 3, 0:E], ACT.Copy).then_inc(p2a, 1)
            na += 4 * NT
            act.wait_ge(p2v, GATE_MAX)
            act.activation(gt1[0:R, :, :], gt1[0:R, :, :], ACT.Exp).then_inc(p2a, 1)
            na += 1
            for t in range(NT):
                act.wait_ge(p2, DISP_AT + t)
                for m in range(2):
                    act.activation(xb[:, m, t, :, :], ps[:, t % 2, ES * m:ES * m + ES], ACT.Copy)\
                        .then_inc(p2a, 1)
            na += 2 * NT
            for e in range(E):
                b = 3 * (e % 2)
                act.wait_ge(p2, EXP_AT + 2 * e)
                if e >= 1:
                    act.wait_ge(p2v, HID_AT + e - 1)
                act.activation(hid[:, 0, :], ps[:, b, 0:SLOTS], ACT.Silu).then_inc(p2a, 1)
                act.wait_ge(p2, EXP_AT + 2 * e + 1)
                act.activation(xb[:, 0, :, e, :], ps[:, b + 2, 0:SLOTS].rearrange("p (t s) -> p t s", t=NT), ACT.Copy).then_inc(p2a, 1)
                act.activation(xb[:, 1, :, e, :], ps[:, 6 + e % 2, 0:SLOTS].rearrange("p (t s) -> p t s", t=NT), ACT.Copy).then_inc(p2a, 1)
            na += 3 * E
            for t in range(NT):
                act.wait_ge(p2, COMB_AT + 2 * t)
                act.activation(o_rows[0:EH, :, :], ps[0:EH, 0, :], ACT.Copy).then_inc(p2a, 1)

        @block.tensor
        def _(pe):
            pe.wait_ge(weights_in, 16 * W_DMAS)
            pe.wait_ge(masks_made, MASKS)
            for b, w in enumerate((wkv, gwkv)):
                for hc in range(2):
                    for m in range(2):
                        last = pe.transpose(ps[:, b, C * hc + P * m:C * hc + P * m + P], w[:, m, P * hc:P * hc + P],
                                            ident[:, :])
                last.then_inc(pre, 1)
            pe.wait_ge(pre_v, 4)
            for b, w in enumerate((wv_fold, gwv_fold)):
                for m in range(2):
                    last = pe.matmul(ps[:, 2 + b, 0:C], mean_ones[:, :], w[:, m, :], start=(m == 0), stop=(m == 1))
                last.then_inc(pre, 1)
            for i, (w, bc) in enumerate(((wkv, "la_ln_kv_b"), (gwkv, "ga_ln_kv_b"))):
                for hc in range(2):
                    for m in range(2):
                        last = pe.matmul(ps[:, 4, 2 * i + hc:2 * i + hc + 1], w[:, m, C + P * hc:C + P * hc + P],
                                         cols[bc][:, m:m + 1], start=(m == 0), stop=(m == 1))
            last.then_inc(pre, 1)
            for m in range(2):
                last = pe.matmul(ps[:, 5, 0:1], mean_ones[:, :], cols["class_emb"][:, m:m + 1],
                                 start=(m == 0), stop=(m == 1))
            last.then_inc(pre, 1)
            pe.wait_ge(pre_v, SQ_DONE)
            for m in range(2):
                last = pe.matmul(ps[:, 5, 1:2], mean_ones[:, :], small[:, 4 + m:5 + m], start=(m == 0), stop=(m == 1))
            last.then_inc(pre, 1)
            pe.wait_ge(pre_v, QHAT_DONE)
            for hc in range(2):
                for m in range(2):
                    last = pe.matmul(ps[:, 5, 2 + hc:3 + hc], gwq[:, m, P * hc:P * hc + P], small[:, 8 + m:9 + m],
                                     start=(m == 0), stop=(m == 1))
            last.then_inc(pre, 1)
            pe.wait_ge(pre_v, GQ_DONE)
            for m in range(2):
                for hc in range(2):
                    last = pe.matmul(ps[:, 5, 8 + 8 * m:16 + 8 * m], gwk_fold[:, hc, P * m:P * m + P],
                                     gq_block[:, hc, :], start=(hc == 0), stop=(hc == 1))
            last.then_inc(pre, 1)
            pe.wait_ge(pre_v, SETUP_V)

            def conv_part(g, slot, first, count, start=False):
                for u in range(first, first + count):
                    n, k = u // (KFULL + 1), u % (KFULL + 1)
                    m, j = n % 2, n // 2
                    if u == 0:
                        pe.wait_ge(x_in[slot], g * 16 + 32 - 16 * slot)
                    if k == 0 and not (start and n < 2):
                        pe.wait_ge(conv_moved, g * 2 * NBLK + n - 1)
                    kk = P if k < KFULL else KREST
                    mm = pe.matmul(ps[:, m, 0:BLK], w_conv[0:kk, k, P * m:P * m + P],
                                   xs[0:kk, slot, k, BLK * j:BLK * (j + 1)], start=(k == 0), stop=(k == KFULL))
                    if k == KFULL:
                        mm.then_inc(conv_done, 1)

            def chain(g, slot, nxt, begun=True):
                at = 0

                def conv(n):
                    nonlocal at
                    if nxt:
                        conv_part(g + 1, 1 - slot, at, n)
                        at += n

                conv(4)
                pe.wait_ge(dve_step, g * NDVE + 2)
                if begun:
                    pe.wait_ge(group_kept, g)
                for m in range(2):
                    last = pe.transpose(ps[:, 6, P * m:P * m + P], red_sum[:, m, :], ident[:, :])
                last.then_inc(pe_step, 1)
                conv(3)
                pe.wait_ge(dve_step, g * NDVE + RED_HAT)
                for m in range(2):
                    last = pe.transpose(ps[:, 7, P * m:P * m + P], red_hat[:, P * m:P * m + P], ident[:, :])
                last.then_inc(pe_step, 1)
                conv(2)
                pe.wait_ge(act_step, g * NACT + 2)
                for hc in range(2):
                    for m in range(2):
                        last = pe.matmul(ps[:, 6, P * hc:P * hc + P], wq[:, m, P * hc:P * hc + P], red_hat_t[:, m, :],
                                         start=(m == 0), stop=(m == 1))
                last.then_inc(pe_step, 1)
                conv(2)
                pe.wait_ge(act_step, g * NACT + 3)
                if begun:
                    pe.wait_ge(ctx_moved, g * 4)
                for m in range(2):
                    for hc in range(2):
                        for j in range(4):
                            o = P * (2 * m + hc)
                            last = pe.matmul(ps[:, 2 + j, o:o + P], wk_fold[32 * j:32 * j + 32, hc, P * m:P * m + P],
                                             q_t[32 * j:32 * j + 32, hc, :], start=True, stop=True)
                last.then_inc(pe_step, 1)
                conv(2)
                pe.wait_ge(act_step, g * NACT + 5)
                pe.wait_ge(dve_step, g * NDVE + QK_MOVED)
                for k in range(NH // 2):
                    if k >= 2:
                        pe.wait_ge(tok_moved, g * (NH // 2) + k - 1)
                    for t in (2 * k, 2 * k + 1):
                        for m in range(2):
                            o = C * (t % 2) + P * m
                            last = pe.transpose(ps[0:HALF, 2 + k % 2, o:o + P],
                                                pe_t[:, slot, m, HALF * t:HALF * t + HALF], ident[:, :])
                    last.then_inc(tok_turned, 1)
                    for t in (2 * k, 2 * k + 1):
                        for m in range(2):
                            last = pe.matmul(ps[0:HALF, 4 + t // 8, 64 * (t % 8):64 * (t % 8) + 64],
                                             pe_t[:, slot, m, HALF * t:HALF * t + HALF], qk[:, m, :, 8 * t:8 * t + 8],
                                             start=(m == 0), stop=(m == 1))
                    if k in (3, 7):
                        last.then_inc(pe_step, 1)
                    conv(1)
                conv(2)
                pe.wait_ge(dve_step, g * NDVE + SCORED)
                pe.transpose(ps[:, 6, 0:HALF], score[0:HALF, :, :], ident[0:HALF, 0:HALF]).then_inc(pe_step, 1)
                conv(2)
                pe.wait_ge(dve_step, g * NDVE + SOFTMAXED)
                pe.transpose(ps[0:HALF, 7, 0:P], soft[:, :, :], ident[:, :]).then_inc(attn_turned, 1)
                conv(2)
                pe.wait_ge(dve_step, g * NDVE + SPREAD)
                pe.wait_ge(tok_moved, (g + 1) * (NH // 2))
                for k in range(4):
                    m, half = k // 2, k % 2
                    if k >= 2:
                        pe.wait_ge(ctx_moved, g * 4 + k - 1)
                    for t in range(8 * half, 8 * half + 8):
                        last = pe.matmul(ps[:, 4 + k % 2, 64 * (t % 8):64 * (t % 8) + 64],
                                         tok[0:HALF, t, P * m:P * m + P], spread[0:HALF, 8 * t:8 * t + 8, :],
                                         start=True, stop=True)
                    last.then_inc(ctx_done, 1)
                conv(1)
                pe.wait_ge(ctx_moved, g * 4 + 4)
                for hc in range(2):
                    for j in range(4):
                        h = 4 * hc + j
                        for m in range(2):
                            last = pe.matmul(ps[32 * j:32 * j + 32, 6, P * hc:P * hc + P],
                                             wv_fold[:, m, DH * h:DH * h + DH], ctxv[:, m, h, :],
                                             start=(m == 0), stop=(m == 1))
                last.then_inc(pe_step, 1)
                conv(1)
                pe.wait_ge(act_step, g * NACT + 8)
                for m in range(2):
                    for hc in range(2):
                        last = pe.matmul(ps[:, 7, P * m:P * m + P], proj[:, hc, P * m:P * m + P], agg_t[:, hc, :],
                                         start=(hc == 0), stop=(hc == 1))
                last.then_inc(pe_step, 1)
                conv(1)
                pe.wait_ge(dve_step, g * NDVE + LOCAL)
                for m in range(2):
                    last = pe.transpose(ps[:, 6, C + P * m:C + P * m + P], lo_t[:, m, :], ident[:, :])
                last.then_inc(pe_step, 1)
                for m in range(2):
                    last = pe.matmul(ps[:, 7, 0:C], lo_t[:, m, :], mod_w[:, m, :], start=(m == 0), stop=(m == 1))
                last.then_inc(pe_step, 1)
                pe.wait_ge(dve_step, g * NDVE + LO_STATS)
                for m in range(2):
                    last = pe.matmul(ps[:, 6, 0:C], lo_t[:, m, :], gwv_fold[:, m, :], start=(m == 0), stop=(m == 1))
                last.then_inc(pe_step, 1)
                pe.wait_ge(dve_step, g * NDVE + PATCHED)
                for m in range(2):
                    last = pe.matmul(ps[:, 7, 0:HEADS], lo_t[:, m, :], gqk[:, m, :], start=(m == 0), stop=(m == 1))
                last.then_inc(pe_step, 1)
                assert not nxt or at == 2 * NBLK * (KFULL + 1), at

            conv_part(0, 0, 0, 2 * NBLK * (KFULL + 1), start=True)
            chain(0, 0, True, begun=False)
            with pe.Fori(0, NG // 2 - 1) as r:
                chain(2 * r + 1, 1, True)
                chain(2 * r + 2, 0, True)
            chain(NG - 1, 1, False)

            pe.wait_ge(pre_v, CLASS_V + 1)
            pe.transpose(ps[:, 0, 0:P], gs_all[:, :, :], ident[:, :]).then_inc(pre, 1)
            pe.wait_ge(pre_v, CLASS_V + 6)
            pe.transpose(ps[:, 0, P:2 * P], s_mat[:, 0:P], ident[:, :]).then_inc(pre, 1)
            pe.wait_ge(pre_v, CLASS_V + 8)
            for g in range(NG):
                for hc in range(2):
                    last = pe.matmul(ps[:, 1, P * hc + GI * g:P * hc + GI * g + GI],
                                     gv_all[:, g, P * hc:P * hc + P], own_image[:, :], start=True, stop=True)
            last.then_inc(pre, 1)
            pe.wait_ge(p2a, 3)
            for hc in range(2):
                last = pe.matmul(ps[:, 2, 0:C], agg_t[:, hc, :], gproj[:, hc, :], start=(hc == 0), stop=(hc == 1))
            last.then_inc(pre, 1)

            np_ = 0
            for t in range(NT):
                if t == 0:
                    pe.wait_ge(p2v, LN1_DONE)
                else:
                    pe.wait_ge(p2a, 3 + 2 * t)
                for m in range(2):
                    last = pe.transpose(ps[:, 0, R * m:R * m + R], n_rows[0:R, t, P * m:P * m + P], ident[0:R, 0:R])
                last.then_inc(p2, 1)
                pe.wait_ge(p2a, 3 + 2 * t + 1)
                for m in range(2):
                    last = pe.matmul(ps[0:R, 1, 0:R], nt_t[:, m, :], nt_t[:, m, :], start=(m == 0), stop=(m == 1))
                last.then_inc(p2, 1)
                pe.wait_ge(p2v, LN1_DONE + NV * t + 4)
                pe.matmul(ps[0:R, 2, 0:C], s_mat[0:R, 0:R], n_rows[0:R, t, :], start=True, stop=True).then_inc(p2, 1)
            pe.wait_ge(p2v, LN2_DONE)
            for t in range(NT):
                if t:
                    pe.wait_ge(p2a, 3 + 2 * NT + 2 * t)
                for m in range(2):
                    last = pe.transpose(ps[:, 0, R * m:R * m + R], n_rows[0:R, t, P * m:P * m + P], ident[0:R, 0:R])
                last.then_inc(p2, 1)
                pe.wait_ge(p2a, 3 + 2 * NT + 2 * t + 1)
                for m in range(2):
                    last = pe.matmul(ps[0:R, 3, 0:E], nt_t[:, m, :], router[:, m, :], start=(m == 0), stop=(m == 1))
                last.then_inc(p2, 1)
            np_ += 5 * NT
            pe.wait_ge(p2v, HOT_DONE)
            pe.matmul(ps[0:R, 4, 0:NT * E], earlier[0:R, :], hot[0:R, 0, :, :], start=True, stop=True)
            pe.matmul(ps[0:R, 5, 0:NT * E], same_seq[0:R, :], hot[0:R, 0, :, :], start=True, stop=False)
            pe.matmul(ps[0:R, 5, 0:NT * E], earlier[0:R, :], hot[0:R, 1, :, :], start=False, stop=True).then_inc(p2, 1)
            np_ += 1
            assert np_ + 1 == DISP_AT
            for t in range(NT):
                pe.wait_ge(p2v, DISP_V + t)
                if t >= 2:
                    pe.wait_ge(p2a, 3 + 4 * NT + 1 + 2 * (t - 1))
                for m in range(2):
                    last = pe.matmul(ps[:, t % 2, ES * m:ES * m + ES], n_rows[0:R, t, P * m:P * m + P],
                                     disp[0:R, :, :, :], start=True, stop=True)
                last.then_inc(p2, 1)
            np_ += NT
            pe.wait_ge(ffn_in, 48)
            A0 = 3 + 4 * NT + 1 + 2 * NT
            pe.wait_ge(p2a, A0)
            for e in range(E):
                b = 3 * (e % 2)
                if e >= 2:
                    pe.wait_ge(p2a, A0 + 3 * (e - 1))
                for i, w in enumerate((w_gate, w_fc)):
                    for m in range(2):
                        last = pe.matmul(ps[:, b + i, 0:SLOTS], w[:, e, m, :], xb[:, m, :, e, :],
                                         start=(m == 0), stop=(m == 1))
                last.then_inc(p2, 1)
                pe.wait_ge(p2v, HID_AT + e)
                pe.matmul(ps[:, b + 2, 0:SLOTS], w_proj[:, e, 0:P], hid[:, 1, :], start=True, stop=True)
                pe.matmul(ps[:, 6 + e % 2, 0:SLOTS], w_proj[:, e, P:C], hid[:, 1, :], start=True, stop=True)\
                    .then_inc(p2, 1)
            np_ += 2 * E
            assert np_ + 1 == COMB_AT - 0
            A1 = A0 + 3 * E
            pe.wait_ge(p2a, A1)
            for t in range(NT):
                pe.wait_ge(p2v, COMB_V + 3 * t)
                if t:
                    pe.wait_ge(p2a, A1 + t)
                for half in range(2):
                    for m in range(2):
                        pe.transpose(ps[0:EH, 0, C * half + P * m:C * half + P * m + P],
                                     xb[:, m, t, 8 * half:8 * half + 8, :], ident[:, :])
                for half in range(2):
                    last = pe.transpose(ps[0:EH, 1, P * half:P * half + R],
                                        comb[0:R, 8 * half:8 * half + 8, :, :], ident[0:R, 0:R])
                last.then_inc(p2, 1)
                pe.wait_ge(p2v, COMB_V + 3 * t + 1)
                pe.wait_ge(p2a, A1 + t + 1)
                for half in range(2):
                    last = pe.matmul(ps[0:R, 2, 0:C], comb_t[0:EH, half, :], o_rows[0:EH, half, :],
                                     start=(half == 0), stop=(half == 1))
                last.then_inc(p2, 1)

        @block.vector
        def _(dve):
            def rsqrt(step, settled, v, y, n):
                p = v.shape[0]
                a, b = newton[0:p, 0, 0:n], newton[0:p, 1, 0:n]
                step(dve.tensor_scalar(a.bitcast(I32), v.bitcast(I32), 1, None, ALU.logical_shift_right))
                settled()
                step(dve.tensor_scalar(y.bitcast(I32), a.bitcast(I32), -1.0, float(0x5f3759df), ALU.mult, ALU.add))
                for _ in range(3):
                    settled()
                    step(dve.tensor_tensor(a, y, y, ALU.mult))
                    settled()
                    step(dve.scalar_tensor_tensor(out=b, in0=a, scalar=-0.5, in1=v, op0=ALU.mult, op1=ALU.mult))
                    settled()
                    step(dve.scalar_tensor_tensor(out=y, in0=b, scalar=1.5, in1=y, op0=ALU.add, op1=ALU.mult))

            made = 0

            def first(ins):
                nonlocal made
                made += 1
                ins.then_inc(pre_v, 1)

            def first_settled():
                dve.wait_ge(pre_v, made)

            dve.wait_ge(masks_made, MASKS)
            dve.wait_ge(weights_in, 16 * W_DMAS)
            for w, f, gn in ((wkv, wv_fold, "la_ln_kv_g"), (gwkv, gwv_fold, "ga_ln_kv_g")):
                for m in range(2):
                    first(dve.tensor_scalar(f[:, m, :], w[:, m, C:2 * C], cols[gn][:, m:m + 1], None, ALU.mult))
            for b, (f, gn) in enumerate(((wk_fold, "la_ln_kv_g"), (gwk_fold, "ga_ln_kv_g"))):
                dve.wait_ge(pre, b + 1)
                first(dve.tensor_tensor(f[:, :, :], ps[:, b, :].rearrange("p (h c) -> p h c", h=2),
                                        rows[gn][:, :].unsqueeze(1).broadcast_to([P, 2, C]), ALU.mult))
                dve.wait_ge(pre_v, made)
                first(dve.tensor_reduce(small[:, 0:2], f[:, :, :], AX_X, ALU.add))
                dve.wait_ge(pre_v, made)
                first(dve.tensor_scalar(small[:, 2:4], small[:, 0:2], -1.0 / C, None, ALU.mult))
                dve.wait_ge(pre_v, made)
                for hc in range(2):
                    first(dve.tensor_scalar(f[:, hc, :], f[:, hc, :], small[:, 2 + hc:3 + hc], SCALE,
                                            ALU.add, ALU.mult))
            for b, f in enumerate((wv_fold, gwv_fold)):
                dve.wait_ge(pre, 3 + b)
                first(dve.tensor_tensor(f[:, :, :], f[:, :, :],
                                        ps[:, 2 + b, 0:C].unsqueeze(1).broadcast_to([P, 2, C]), ALU.subtract))
            dve.wait_ge(pre, 5)
            first(dve.tensor_copy(v_bias[:, :], ps[:, 4, 0:2]))
            first(dve.tensor_copy(gv_bias[:, :], ps[:, 4, 2:4]))
            dve.wait_ge(pre, 6)
            dve.wait_ge(pre_v, made)
            first(dve.tensor_copy(small[:, 0:1], ps[:, 5, 0:1]))
            dve.wait_ge(pre_v, made)
            first(dve.tensor_scalar(small[:, 2:4], cols["class_emb"][:, :], small[:, 0:1], None, ALU.subtract))
            dve.wait_ge(pre_v, made)
            first(dve.tensor_tensor(small[:, 4:6], small[:, 2:4], small[:, 2:4], ALU.mult))
            assert made == SQ_DONE
            dve.wait_ge(pre, 7)
            first(dve.tensor_scalar(small[:, 12:13], ps[:, 5, 1:2], EPS, None, ALU.add))
            dve.wait_ge(pre_v, made)
            rsqrt(first, first_settled, small[:, 12:13], small[:, 6:7], 1)
            dve.wait_ge(pre_v, made)
            first(dve.tensor_scalar(small[:, 8:10], small[:, 2:4], small[:, 6:7], None, ALU.mult))
            dve.wait_ge(pre_v, made)
            first(dve.tensor_tensor(small[:, 10:12], small[:, 8:10], cols["ga_ln_q_g"][:, :], ALU.mult))
            dve.wait_ge(pre_v, made)
            first(dve.tensor_tensor(small[:, 8:10], small[:, 10:12], cols["ga_ln_q_b"][:, :], ALU.add))
            assert made == QHAT_DONE
            dve.wait_ge(pre, 8)
            for h in range(HEADS):
                j, hc = h % 4, h // 4
                first(dve.tensor_copy(gq_block[32 * j:32 * j + 32, hc, h:h + 1],
                                      ps[32 * j:32 * j + 32, 5, 2 + hc:3 + hc]))
            assert made == GQ_DONE
            dve.wait_ge(pre, 9)
            first(dve.tensor_copy(gqk[:, :, :], ps[:, 5, 8:24].rearrange("p (m h) -> p m h", m=2)))
            dve.wait_ge(pre_v, made)
            first(dve.tensor_tensor(rows["class_emb"][:, :], rows["class_emb"][:, :], rows["ga_proj_b"][:, :], ALU.add))
            assert made == SETUP_V, made

            def chain(g, slot, begun=True):
                n = 0

                def step(ins):
                    nonlocal n
                    n += 1
                    ins.then_inc(dve_step, 1)

                def settled():
                    dve.wait_ge(dve_step, g * NDVE + n)

                def variance(eps, dst):
                    step(dve.tensor_scalar(var[:, 1:2], st6[:, 1:2], st6[:, 4:5], None, ALU.subtract))
                    step(dve.tensor_scalar(var[:, 2:3], st6[:, 2:3], st6[:, 5:6], 4.0 / C, ALU.add, ALU.mult))
                    settled()
                    step(dve.scalar_tensor_tensor(out=var[:, 3:4], in0=var[:, 1:2], scalar=var[:, 1:2],
                                                  in1=var[:, 2:3], op0=ALU.mult, op1=ALU.add))
                    settled()
                    step(dve.tensor_scalar(dst, var[:, 3:4], 0.25, eps, ALU.mult, ALU.add))

                dve.wait_ge(conv_moved, (g + 1) * 2 * NBLK)
                for m in range(2):
                    step(dve.tensor_reduce(red_sum[:, m, :], pe_t[:, slot, m, :].rearrange("p (w k) -> p w k", k=KEYS),
                                           AX_X, ALU.add))
                dve.wait_ge(pe_step, g * NPE + 1)
                step(dve.bn_stats(st6[:, :], ps[:, 6, 0:C]))
                settled()
                step(dve.tensor_scalar(mv[:, 0:1], st6[:, 1:2], st6[:, 4:5], 0.5, ALU.add, ALU.mult))
                variance(KEYS * KEYS * EPS, var[:, 0:1])
                settled()
                rsqrt(step, settled, var[:, 0:1], mv[:, 1:2], 1)
                settled()
                step(dve.tensor_scalar(red_hat[:, :], ps[:, 6, 0:C], mv[:, 0:1], mv[:, 1:2], ALU.subtract, ALU.mult))
                assert n == RED_HAT
                dve.wait_ge(pe_step, g * NPE + 4)
                for j in range(2, 4):
                    step(dve.tensor_copy(qk[:, :, j:HEADS:4, :],
                                         ps[:, 2 + j, :].rearrange("p (m h w) -> p m h w", m=2, h=2)))
                assert n == QK_MOVED
                for t in range(NH):
                    if t % 2 == 0:
                        dve.wait_ge(tok_moved, g * (NH // 2) + t // 2 + 1)
                    step(dve.bn_stats(stats[0:HALF, t, :], tok[0:HALF, t, :]))
                settled()
                s = stats[0:HALF, :, :]
                step(dve.tensor_tensor(tmp16[0:HALF, 0, :], s[:, :, 1], s[:, :, 4], ALU.subtract))
                step(dve.tensor_tensor(tmp16[0:HALF, 1, :], s[:, :, 2], s[:, :, 5], ALU.add))
                settled()
                step(dve.scalar_tensor_tensor(out=tmp16[0:HALF, 2, :], in0=tmp16[0:HALF, 0, :], scalar=C / 4,
                                              in1=tmp16[0:HALF, 0, :], op0=ALU.mult, op1=ALU.mult))
                settled()
                step(dve.tensor_tensor(tmp16[0:HALF, 0, :], tmp16[0:HALF, 1, :], tmp16[0:HALF, 2, :], ALU.add))
                settled()
                step(dve.tensor_scalar(tmp16[0:HALF, 1, :], tmp16[0:HALF, 0, :], 1.0 / C, EPS, ALU.mult, ALU.add))
                settled()
                rsqrt(step, settled, tmp16[0:HALF, 1, :], rstd[0:HALF, :], NH)
                wmask = own_window[0:HALF, :].unsqueeze(1).broadcast_to([HALF, 64, 8])
                for b in range(2):
                    dve.wait_ge(pe_step, g * NPE + 5 + b)
                    step(dve.tensor_tensor(masked[0:HALF, 64 * b:64 * b + 64, :],
                                           ps[0:HALF, 4 + b, :].rearrange("p (a w) -> p a w", w=8), wmask, ALU.mult))
                    settled()
                    step(dve.tensor_reduce(score[0:HALF, 8 * b:8 * b + 8, :], masked[0:HALF, 64 * b:64 * b + 64, :],
                                           AX_X, ALU.add))
                settled()
                by_rstd = rstd[0:HALF, :].unsqueeze(2).broadcast_to([HALF, NH, HEADS])
                step(dve.tensor_tensor(score[0:HALF, :, :], score[0:HALF, :, :], by_rstd, ALU.mult))
                assert n == SCORED, n
                dve.wait_ge(pe_step, g * NPE + 7)
                sp_ = ps[:, 6, 0:HALF].rearrange("p (w k) -> p w k", k=KEYS)
                step(dve.tensor_reduce(soft_max[:, :], sp_, AX_X, ALU.max))
                settled()
                step(dve.tensor_tensor(soft[:, :, :], sp_, soft_max[:, :].unsqueeze(2).broadcast_to([P, 8, KEYS]),
                                       ALU.subtract))
                assert n == SUBTRACTED, n
                dve.wait_ge(act_step, g * NACT + 6)
                step(dve.tensor_reduce(soft_sum[:, :], soft[:, :, :], AX_X, ALU.add))
                settled()
                step(dve.reciprocal(soft_max[:, :], soft_sum[:, :]))
                settled()
                step(dve.tensor_tensor(soft[:, :, :], soft[:, :, :],
                                       soft_max[:, :].unsqueeze(2).broadcast_to([P, 8, KEYS]), ALU.mult))
                assert n == SOFTMAXED, n
                dve.wait_ge(attn_turned, g + 1)
                step(dve.tensor_tensor(attn[0:HALF, :, :], ps[0:HALF, 7, 0:P].rearrange("p (t h) -> p t h", h=HEADS),
                                       by_rstd, ALU.mult))
                settled()
                step(dve.tensor_tensor(spread[0:HALF, :, :],
                                       attn[0:HALF, :, :].rearrange("p t h -> p (t h)").unsqueeze(2)
                                       .broadcast_to([HALF, NH * HEADS, 8]),
                                       own_window[0:HALF, :].unsqueeze(1).broadcast_to([HALF, NH * HEADS, 8]),
                                       ALU.mult))
                assert n == SPREAD, n
                dve.wait_ge(act_step, g * NACT + 10)
                step(dve.scalar_tensor_tensor(out=lo_t[:, :, :], in0=red_sum[:, :, :], scalar=1.0 / KEYS,
                                              in1=lo_part[:, :, :], op0=ALU.mult, op1=ALU.add))
                assert n == LOCAL, n
                dve.wait_ge(pe_step, g * NPE + 10)
                step(dve.bn_stats(st6[:, :], ps[:, 6, C:2 * C]))
                assert n == LO_STATS
                settled()
                variance(EPS, lo_var[:, bass.ds(g, 1)])
                dve.wait_ge(pe_step, g * NPE + 11)
                if begun:
                    dve.wait_ge(patch_out, g * 16)
                step(dve.tensor_tensor(patch[:, :], ps[:, 7, 0:C], rows["mod_b"][:, :], ALU.add))
                assert n == PATCHED
                dve.wait_ge(pe_step, g * NPE + 13)
                step(dve.tensor_copy(gs_all[:, bass.ds(g, 1), :], ps[:, 7, 0:HEADS]))
                assert n == NDVE, n

            chain(0, 0, begun=False)
            with dve.Fori(0, NG // 2 - 1) as r:
                chain(2 * r + 1, 1)
                chain(2 * r + 2, 0)
            chain(NG - 1, 1)

            dve.wait_ge(dve_step, NG * NDVE)
            rsqrt(first, first_settled, lo_var[:, :], lo_rstd[:, :], NG)
            dve.wait_ge(pre_v, made)
            by_lo = lo_rstd[:, :].unsqueeze(2).broadcast_to([P, NG, HEADS])
            first(dve.tensor_tensor(gs_all[:, :, :], gs_all[:, :, :], by_lo, ALU.mult))
            dve.wait_ge(pre, 10)
            gsp = ps[:, 0, 0:P].rearrange("p (b w) -> p b w", w=WIN)
            first(dve.tensor_reduce(soft_max[:, :], gsp, AX_X, ALU.max))
            dve.wait_ge(pre_v, made)
            gsm = s_mat[:, 0:P].rearrange("p (b w) -> p b w", w=WIN)
            first(dve.tensor_tensor(gsm, gsp, soft_max[:, :].unsqueeze(2).broadcast_to([P, GI, WIN]), ALU.subtract))
            dve.wait_ge(p2a, 1)
            first(dve.tensor_reduce(soft_sum[:, :], gsm, AX_X, ALU.add))
            dve.wait_ge(pre_v, made)
            first(dve.reciprocal(soft_max[:, :], soft_sum[:, :]))
            dve.wait_ge(pre_v, made)
            first(dve.tensor_tensor(gsm, gsm, soft_max[:, :].unsqueeze(2).broadcast_to([P, GI, WIN]), ALU.mult))
            dve.wait_ge(pre, 11)
            first(dve.tensor_tensor(gs_all[:, :, :], ps[:, 0, P:2 * P].rearrange("p (g h) -> p g h", g=NG), by_lo,
                                    ALU.mult))
            dve.wait_ge(pre_v, made)
            dve.wait_ge(group_kept, NG)
            gvh = gv_all[:, :, :].rearrange("p g (h d) -> p (g h) d", d=DH)
            first(dve.tensor_tensor(gvh, gvh, gs_all[:, :, :].rearrange("p g h -> p (g h)").unsqueeze(2)
                                    .broadcast_to([P, NG * HEADS, DH]), ALU.mult))
            assert made == CLASS_V + 8
            dve.wait_ge(pre, 13)
            dve.wait_ge(patch_out, 16 * NG)
            first(dve.tensor_tensor(patch[:, :], ps[:, 2, 0:C], rows["class_emb"][:, :], ALU.add))

            n2 = 0

            def step(ins):
                nonlocal n2
                n2 += 1
                ins.then_inc(p2v, 1)

            def settled():
                dve.wait_ge(p2v, n2)

            def normal_all():
                for t in range(NT):
                    step(dve.bn_stats(stat6[0:R, t, :], h_rows[0:R, t, :]))
                settled()
                for t in range(NT):
                    step(dve.bn_aggr(row_mv[0:R, t, :], stat6[0:R, t, :]))
                settled()
                step(dve.tensor_scalar(row_var[0:R, :], row_mv[0:R, :, 1], EPS, None, ALU.add))
                settled()
                rsqrt(step, settled, row_var[0:R, :], gcol[0:R, :], NT)
                settled()
                for t in range(NT):
                    step(dve.tensor_scalar(n_rows[0:R, t, :], h_rows[0:R, t, :], row_mv[0:R, t, 0:1],
                                           gcol[0:R, t:t + 1], ALU.subtract, ALU.mult))

            dve.wait_ge(h_in, 16 * NT)
            dve.wait_ge(pad_zero, 1)
            normal_all()
            assert n2 == LN1_DONE
            for t in range(NT):
                dve.wait_ge(p2, 3 * t + 2)
                step(dve.tensor_tensor(s_mat[0:R, 0:R], ps[0:R, 1, 0:R], neg_mask[0:R, :], ALU.add))
                settled()
                step(dve.tensor_reduce(small[0:R, 4:5], s_mat[0:R, 0:R], AX_X, ALU.max, negate=True))
                dve.wait_ge(p2a, 3 + 2 * t + 2)
                step(dve.reciprocal(small[0:R, 6:7], small[0:R, 5:6]))
                settled()
                step(dve.tensor_scalar(s_mat[0:R, 0:R], s_mat[0:R, 0:R], small[0:R, 6:7], None, ALU.mult))
                dve.wait_ge(p2, 3 * t + 3)
                step(dve.tensor_tensor(h_rows[0:R, t, :], h_rows[0:R, t, :], ps[0:R, 2, 0:C], ALU.add))
            settled()
            normal_all()
            assert n2 == LN2_DONE
            dve.wait_ge(p2a, 3 + 4 * NT)
            lg = logit[0:R, :, :]

            def wide(col):
                return col.unsqueeze(2).broadcast_to([R, NT, E])

            step(dve.tensor_reduce(gcol[0:R, :], lg, AX_X, ALU.max))
            settled()
            step(dve.tensor_tensor(gt1[0:R, :, :], lg, wide(gcol[0:R, :]), ALU.subtract))
            assert n2 == GATE_MAX
            dve.wait_ge(p2a, 3 + 4 * NT + 1)
            step(dve.tensor_reduce(gcol[0:R, :], gt1[0:R, :, :], AX_X, ALU.add))
            settled()
            step(dve.reciprocal(gcol[0:R, :], gcol[0:R, :]))
            settled()
            step(dve.tensor_tensor(lg, gt1[0:R, :, :], wide(gcol[0:R, :]), ALU.mult))
            settled()
            step(dve.tensor_copy(gt1[0:R, :, :], lg))
            settled()
            rw = rank_w[0:R, :].unsqueeze(1).broadcast_to([R, NT, E])
            for k in range(2):
                step(dve.tensor_reduce(gcol[0:R, :], gt1[0:R, :, :], AX_X, ALU.max))
                settled()
                step(dve.tensor_tensor(gt2[0:R, :, :], gt1[0:R, :, :], wide(gcol[0:R, :]), ALU.is_equal))
                settled()
                step(dve.tensor_tensor(gt2[0:R, :, :], gt2[0:R, :, :], rw, ALU.mult))
                settled()
                step(dve.tensor_reduce(gcol[0:R, :], gt2[0:R, :, :], AX_X, ALU.max))
                settled()
                step(dve.tensor_tensor(hot[0:R, k, :, :], gt2[0:R, :, :], wide(gcol[0:R, :]), ALU.is_equal))
                settled()
                if k == 0:
                    step(dve.tensor_tensor(gt3[0:R, :, :], gt1[0:R, :, :], hot[0:R, 0, :, :], ALU.subtract))
                    settled()
                    step(dve.tensor_tensor(gt1[0:R, :, :], gt3[0:R, :, :], hot[0:R, 0, :, :], ALU.subtract))
                    settled()
            assert n2 == HOT_DONE, (n2, HOT_DONE)
            dve.wait_ge(p2, DISP_AT - 1)
            r1 = ps[0:R, 4, 0:NT * E].rearrange("p (t e) -> p t e", t=NT)
            r2 = ps[0:R, 5, 0:NT * E].rearrange("p (t e) -> p t e", t=NT)
            tk = take[0:R, :, :].rearrange("p (t e) s -> p t e s", t=NT)
            gi = give[0:R, :, :].rearrange("p (t e) s -> p t e s", t=NT)
            for s in range(2):
                step(dve.scalar_tensor_tensor(out=gt1[0:R, :, :], in0=r1, scalar=float(s), in1=hot[0:R, 0, :, :],
                                              op0=ALU.is_equal, op1=ALU.mult))
                step(dve.scalar_tensor_tensor(out=gt2[0:R, :, :], in0=r2, scalar=float(s), in1=hot[0:R, 1, :, :],
                                              op0=ALU.is_equal, op1=ALU.mult))
                settled()
                step(dve.tensor_tensor(tk[:, :, :, s], gt1[0:R, :, :], gt2[0:R, :, :], ALU.add))
                settled()
            step(dve.tensor_tensor(gi[:, :, :, 0], tk[:, :, :, 0], lg, ALU.mult))
            step(dve.tensor_tensor(gt1[0:R, :, :], hot[0:R, 0, :, :], hot[0:R, 1, :, :], ALU.add))
            settled()
            step(dve.tensor_tensor(gt2[0:R, :, :], gt1[0:R, :, :], lg, ALU.mult))
            settled()
            step(dve.tensor_tensor(gi[:, :, :, 1], gt2[0:R, :, :], gi[:, :, :, 0], ALU.subtract))
            settled()
            by_seq = own_seq[0:R, :].unsqueeze(1).unsqueeze(3).broadcast_to([R, E, TI, CAP])
            assert n2 + 1 == DISP_V, (n2 + 1, DISP_V)
            for t in range(NT):
                if t:
                    dve.wait_ge(p2, DISP_AT + t - 1)
                step(dve.tensor_tensor(disp[0:R, :, :, :],
                                       take[0:R, E * t:E * t + E, :].unsqueeze(2).broadcast_to([R, E, TI, CAP]),
                                       by_seq, ALU.mult))
            assert n2 + 1 == HID_AT, (n2 + 1, HID_AT)
            A0 = 3 + 4 * NT + 1 + 2 * NT
            for e in range(E):
                b = 3 * (e % 2)
                dve.wait_ge(p2a, A0 + 3 * e + 1)
                if e:
                    dve.wait_ge(p2, EXP_AT + 2 * e - 1)
                step(dve.tensor_tensor(hid[:, 1, :], hid[:, 0, :], ps[:, b + 1, 0:SLOTS], ALU.mult))
            assert n2 + 1 == COMB_V, (n2 + 1, COMB_V)
            for t in range(NT):
                if t:
                    dve.wait_ge(p2, COMB_AT + 2 * t - 2)
                step(dve.tensor_tensor(comb[0:R, :, :, :],
                                       give[0:R, E * t:E * t + E, :].unsqueeze(2).broadcast_to([R, E, TI, CAP]),
                                       by_seq, ALU.mult))
                dve.wait_ge(p2, COMB_AT + 2 * t)
                step(dve.tensor_copy(comb_t[0:EH, :, :],
                                     ps[0:EH, 1, 0:C].rearrange("p (k r) -> p k r", k=2)[:, :, 0:R]))
                dve.wait_ge(p2, COMB_AT + 2 * t + 1)
                if t >= 2:
                    dve.wait_ge(out_sem[t % 2], 16 * (t // 2))
                step(dve.tensor_tensor(y_rows[0:R, t % 2, :], ps[0:R, 2, 0:C], h_rows[0:R, t, :], ALU.add))


def kernel(**inputs):
    import numpy as _np
    import concourse.bacc as _bacc
    from concourse.bass_utils import run_bass_kernel_spmd as _run

    v = {n: _np.asarray(x) for n, x in inputs.items()}
    pad = KFULL * P + KPAD - PIX
    x = v["x"].reshape(NG, GI, CH, SIDE, CS, PS, SIDE, CS, PS).transpose(0, 2, 5, 8, 1, 3, 6, 4, 7)
    x = _np.concatenate([x.reshape(NG, PIX, GT), _np.zeros((NG, pad, GT), _np.float32)], axis=1)
    conv_w = v["L0_tok_conv_w"].reshape(C, PIX).T
    conv_w = _np.concatenate([conv_w, _np.zeros((pad, C), _np.float32)], axis=0)
    arrays = {"x": x, "conv_w": _np.ascontiguousarray(conv_w), "cls_tok": v["cls_tok"]}
    for n in ("class_emb", "la_ln_q_g", "la_ln_q_b", "la_wq", "la_ln_kv_g", "la_ln_kv_b", "la_wkv", "la_proj_w",
              "la_proj_b", "ga_ln_q_g", "ga_ln_q_b", "ga_wq", "ga_ln_kv_g", "ga_ln_kv_b", "ga_wkv", "ga_proj_w",
              "ga_proj_b", "mod_w", "mod_b"):
        arrays[n] = v["L0_tok_" + n]
    for n in ("w_router", "w_fc", "w_gate", "w_proj"):
        arrays[n] = v["L0_ffn_" + n]
    arrays["cols"] = _np.stack([v["L0_tok_" + n].reshape(2, P) for n in COLS]).transpose(2, 0, 1)
    arrays = {n: _np.ascontiguousarray(x) for n, x in arrays.items()}
    nc = _bacc.Bacc("TRN2", target_bir_lowering=False, num_devices=1)
    aps = {n: nc.dram_tensor("in_" + n, x.shape, F32, kind="ExternalInput").ap() for n, x in arrays.items()}
    out = nc.dram_tensor("out_rows", (IMGS * TOK, C), F32, kind="ExternalOutput").ap()
    tower(nc, aps, out)
    r = _run(nc, [{"in_" + n: x for n, x in arrays.items()}], core_ids=[0])
    return r.results[0]["out_rows"].reshape(IMGS, TOK, C)
```

```python
from contextlib import ExitStack

import concourse.bass as bass
from concourse import mybir

F32 = mybir.dt.float32
I32 = mybir.dt.int32
F32R = mybir.dt.float32r
ALU = mybir.AluOpType
ACT = mybir.ActivationFunctionType
AX_X = mybir.AxisListType.X

P = 128
EPS = 1e-5
IMGS, CH, IMG, PS, CS = 128, 3, 168, 14, 3
C = 256
HEADS, DH = 8, 32
SIDE = IMG // PS // CS
WIN = SIDE * SIDE
KEYS = CS * CS
PIX = CH * PS * PS
KFULL = PIX // P
KREST = PIX - KFULL * P
KPAD = -(-KREST // 16) * 16
GI = 8
NG = IMGS // GI
GW = GI * WIN
GT = GW * KEYS
BLKS = ((0, 44 * KEYS), (44 * KEYS, 42 * KEYS), (86 * KEYS, 42 * KEYS))
NB = len(BLKS)
NPR = 3 * (KFULL + 1)
CONV_C, CONV_D = 40, 21
TW = P // KEYS
TT = TW * KEYS
NTT = -(-GW // TW)
W0 = [min(TW * t, GW - TW) for t in range(NTT)]
TH = NTT * HEADS
QUADS = [range(i, min(i + 4, NTT)) for i in range(0, NTT, 4)]
SCALE = C ** -0.5

TOK = WIN + 2
TI = 7
R = TI * TOK
NT = -(-IMGS // TI)
LASTR = (IMGS - (NT - 1) * TI) * TOK
E, CAP, H = 16, 2, 128
TS = TI * CAP
SLOTS = NT * TS
ES = E * TS
EH = ES // 2
NEG = 1e30
COLS = ("la_ln_q_g", "la_ln_q_b", "la_ln_kv_g", "la_ln_kv_b", "la_proj_b",
        "ga_ln_q_g", "ga_ln_q_b", "ga_ln_kv_g", "ga_ln_kv_b", "class_emb")


def tower(nc, a, out):
    with ExitStack() as ctx:
        stack = ctx

        def sb(name, shape, dt=F32):
            return stack.enter_context(nc.sbuf_tensor(name, shape, dt))

        def sem(name):
            return ctx.enter_context(nc.semaphore(name))

        scratch = nc.dram_tensor("tower_rows", [IMGS * TOK, C], F32, kind="Internal").ap()
        scratch_img = scratch.rearrange("(b t) c -> b t c", t=TOK)

        ident = sb("ident", [P, P])
        mean_ones = sb("mean_ones", [P, P])
        own_window = sb("own_window", [P, TW])
        own_image = sb("own_image", [P, GI])
        own_seq = sb("own_seq", [P, TI])
        same_seq = sb("same_seq", [P, R])
        earlier = sb("earlier", [P, R])
        neg_mask = sb("neg_mask", [P, R])
        rank_w = sb("rank_w", [P, E])
        proj = sb("proj", [P, 2, C])
        gproj = sb("gproj", [P, 2, C])
        router = sb("router", [P, 2, E])
        col_vectors = sb("col_vectors", [P, len(COLS), 2])
        cols = {n: col_vectors[:, i, :] for i, n in enumerate(COLS)}
        KEPT_ROWS = ("mod_b", "class_emb", "ga_proj_b")
        rows = {n: sb("row_" + n, [P, C]) for n in KEPT_ROWS}
        gv_bias = sb("gv_bias", [P, 2])
        small = sb("small", [P, 16])
        newton = sb("newton", [P, 2, 32])
        var = sb("var", [P, 32])
        lo_all = sb("lo_all", [P, NG, C])
        gwv_fold = sb("gwv_fold", [P, 2, C])
        gs_all = sb("gs_all", [P, NG, HEADS])
        lo_var = sb("lo_var", [P, NG])
        lo_rstd = sb("lo_rstd", [P, NG])
        s_mat = sb("s_mat", [P, P])
        agg_t = sb("agg_t", [P, 2, P])
        patch = sb("patch", [P, C])
        soft_max = sb("soft_max", [P, TW])
        soft_sum = sb("soft_sum", [P, TW])

        stack = ctx.enter_context(ExitStack())
        phase1 = stack
        x_raw = sb("x_raw", [P, KFULL + 1, GT])
        x_hi = sb("x_hi", [P, KFULL + 1, GT], F32R)
        x_lo = sb("x_lo", [P, KFULL + 1, GT], F32R)
        w_hi = sb("w_hi", [P, KFULL + 1, C], F32R)
        w_lo = sb("w_lo", [P, KFULL + 1, C], F32R)
        wq = sb("wq", [P, 2, C])
        mod_w = sb("mod_w", [P, 2, C])
        wk_fold = sb("wk_fold", [P, 2, C])
        wv_fold = sb("wv_fold", [P, 2, C])
        v_bias = sb("v_bias", [P, 2])
        gqk = sb("gqk", [P, 2, HEADS])
        pe_t = sb("pe_t", [P, 2, 2, GT])
        red_sum = sb("red_sum", [P, 2, 2, P])
        red_hat = sb("red_hat", [P, C])
        red_hat_t = sb("red_hat_t", [P, 2, P])
        q_t = sb("q_t", [P, 2, P])
        stats = sb("stats", [P, NTT, 6])
        tok_var = sb("tok_var", [P, 3, NTT])
        rstd = sb("rstd", [P, NTT])
        st6 = sb("st6", [P, 2, 6])
        mv = sb("mv", [P, 2])
        score = sb("score", [P, NTT, HEADS])
        soft = sb("soft", [P, TW, KEYS])
        attn = sb("attn", [P, NTT, HEADS])
        lo_t = sb("lo_t", [P, 2, P])
        lo_part = sb("lo_part", [P, 2, P])
        with ExitStack() as stack:
            w_conv = sb("w_conv", [P, KFULL + 1, C])
            wkv = sb("wkv", [P, 2, 2 * C])
            gwkv = sb("gwkv", [P, 2, 2 * C])
            gwq = sb("gwq", [P, 2, C])
            gwk_fold = sb("gwk_fold", [P, 2, C])
            gq_block = sb("gq_block", [P, 2, HEADS])
            SETUP_ROWS = ("la_ln_kv_g", "ga_ln_kv_g")
            rows.update({n: sb("row_" + n, [P, C]) for n in SETUP_ROWS})
        stack = phase1
        tok = sb("tok", [P, NTT, C])
        qk = sb("qk", [P, 2, HEADS, P])
        ctxv = sb("ctxv", [P, 2, HEADS, P])
        masked = sb("masked", [P, 2, 4 * HEADS, TW])
        spread = sb("spread", [P, TH, TW])
        phase1.close()

        stack = ctx
        w_gate = sb("w_gate", [P, E, 2, H])
        w_fc = sb("w_fc", [P, E, 2, H])
        w_proj = sb("w_proj", [P, E, C])
        xb = sb("xb", [P, 2, NT, E, TS])
        h_rows = sb("h_rows", [P, NT, C])
        n_rows = sb("n_rows", [P, NT, C])
        logit = sb("logit", [P, NT, E])
        hot = sb("hot", [P, 2, NT, E])
        gt1 = sb("gt1", [P, NT, E])
        gt2 = sb("gt2", [P, NT, E])
        gt3 = sb("gt3", [P, NT, E])
        take = sb("take", [P, NT * E, CAP])
        give = sb("give", [P, NT * E, CAP])
        gcol = sb("gcol", [P, NT])
        stat6 = sb("stat6", [P, NT, 6])
        row_mv = sb("row_mv", [P, NT, 2])
        row_var = sb("row_var", [P, NT])
        s_two = sb("s_two", [P, 2, R])
        soft2 = sb("soft2", [P, 2, 3])
        nt_t = sb("nt_t", [P, 2, 2, R])
        disp = sb("disp", [P, 2, E, TI, CAP])
        comb = sb("comb", [P, 2, E, TI, CAP])
        comb_t = sb("comb_t", [P, 2, 2, R])
        o_rows = sb("o_rows", [P, 2, 2, C])
        hid = sb("hid", [P, 2, 2, SLOTS])
        y_rows = sb("y_rows", [P, 2, C])

        ps = ctx.enter_context(nc.psum_tensor("ps", [P, 8, 512], F32))

        masks_made = sem("masks_made")
        weights_in = sem("weights_in")
        w_split = sem("w_split")
        raw_in = [sem(f"raw_in_{j}") for j in range(NB)]
        hi_made = sem("hi_made")
        lo_made = sem("lo_made")
        conv_done = sem("conv_done")
        conv_moved = sem("conv_moved")
        pe_front, pe_main, pe_tail = sem("pe_front"), sem("pe_main"), sem("pe_tail")
        act_front, act_main, act_tail = sem("act_front"), sem("act_main"), sem("act_tail")
        dve_front, dve_main, dve_tail = sem("dve_front"), sem("dve_main"), sem("dve_tail")
        red_made = sem("red_made")
        tok_turned, tok_moved = sem("tok_turned"), sem("tok_moved")
        ctx_done, ctx_moved = sem("ctx_done"), sem("ctx_moved")
        group_kept = sem("group_kept")
        patch_out = sem("patch_out")
        cls_out = sem("cls_out")
        pre, pre_v = sem("pre"), sem("pre_v")
        cls_exp, cls_moved, cls_gathered = sem("cls_exp"), sem("cls_moved"), sem("cls_gathered")
        ffn_in, pad_zero = sem("ffn_in"), sem("pad_zero")
        h_in = [sem(f"h_in_{i}") for i in range(4)]
        rows_normal = sem("rows_normal")
        rows_turned, rows_moved = sem("rows_turned"), sem("rows_moved")
        sums_done, sums_masked, max_found = sem("sums_done"), sem("sums_masked"), sem("max_found")
        exped, inverted, weighted = sem("exped"), sem("inverted"), sem("weighted")
        mixed, added = sem("mixed"), sem("added")
        logits_done, logits_moved = sem("logits_done"), sem("logits_moved")
        p2v = sem("p2v")
        gate_exp, ranked = sem("gate_exp"), sem("ranked")
        disp_made, disp_done, disp_moved = sem("disp_made"), sem("disp_done"), sem("disp_moved")
        up_done, silu_done, hid_done = sem("up_done"), sem("silu_done"), sem("hid_done")
        down_done, down_moved = sem("down_done"), sem("down_moved")
        comb_made, outs_turned, comb_moved = sem("comb_made"), sem("outs_turned"), sem("comb_moved")
        outs_moved, y_done, y_made = sem("outs_moved"), sem("y_done"), sem("y_made")
        out_sem = [sem("out_even"), sem("out_odd")]

        block = ctx.enter_context(nc.Block())

        def mpn(ap):
            return ap.rearrange("(m p) n -> p m n", p=P)

        LASTW = GW - W0[-2]
        CTX_FILLS = ((0, 0), (0, 1), (0, 2), (1, 0), (1, 1))
        NR = 11
        PF, PM, PT = 5, 5, 4
        AF, AM, AT = 5, 1, 4
        RED_HAT = 1 + 5 + NR + 1
        DF = RED_HAT + 2
        QUAD0 = 4 * 2 + 1
        SCORED = NTT + 2 * len(QUADS) + 5 + NR + 1
        SUBTRACTED = SCORED + 2
        SOFTMAXED = SUBTRACTED + 3
        SPREAD = SOFTMAXED + 2
        DM = SPREAD
        LOCAL, PATCHED = 1, 7
        DT = 8
        W_SPLIT = 4
        SQ_DONE = 4 + 2 * 5 + 2 + 2 + 3
        QHAT_DONE = SQ_DONE + 1 + NR + 3
        GQ_DONE = QHAT_DONE + HEADS
        SETUP_V = GQ_DONE + 2
        CLASS_V = SETUP_V + NR
        MASKS = 8 + 8 + 2 + E
        W_DMAS = 2 + 8 + len(KEPT_ROWS) + len(SETUP_ROWS) + 1
        LN2_DONE = 2 * NT + 4 * (1 + NR) + 2 * NT + 1 + NR
        GATE_MAX = LN2_DONE + 2
        HOT_DONE = GATE_MAX + 4 + 5 + 1 + 5
        H_LOTS = (0, 5, 10, 15, NT)

        def cls_ctx_move(move, k, *args):
            move(ctxv[:, k // 2, :, 64 * (k % 2):64 * (k % 2) + 64].rearrange("p h (g b) -> p g h b", b=GI),
                 ps[:, 1 + k, :].rearrange("p (g h b) -> p g h b", g=NG // 2, h=HEADS), *args).then_inc(cls_moved, 1)

        cls_spread = spread[:, :, :].rearrange("p a w -> p (a w)")[:, 0:NG * HEADS * GI]\
            .rearrange("p (a b) -> p a b", b=GI)

        @block.sync
        def _(sp):
            def load(g, j):
                c, n = BLKS[j]
                if not isinstance(g, int) or g >= 1:
                    sp.wait_ge(lo_made, g * NB - NB + j + 1)
                src = a["x"][g] if isinstance(g, int) else a["x"][bass.ds(g, 1)].rearrange("o k t -> (o k) t")
                sp.dma_start(x_raw[:, 0:KFULL, c:c + n],
                             src[0:KFULL * P, c:c + n].rearrange("(k p) t -> p k t", p=P)).then_inc(raw_in[j], 16)
                sp.dma_start(x_raw[0:KPAD, KFULL, c:c + n], src[KFULL * P:KFULL * P + KPAD, c:c + n])\
                    .then_inc(raw_in[j], 16)

            def store(g):
                sp.wait_ge(dve_tail, g * DT + PATCHED)
                sp.dma_start(scratch_img[bass.ds(g * GI, GI), 1:1 + WIN, :], patch[:, :]).then_inc(patch_out, 16)

            for j in range(NB):
                load(0, j)
            sp.dma_start(scratch_img[:, 0:1, :], a["cls_tok"].broadcast_to([IMGS, 1, C])).then_inc(patch_out, 16)
            for g in (1, 2, 3):
                for j in range(NB):
                    load(g, j)
            with sp.Fori(1, NG - 3) as g:
                store(g - 1)
                for j in range(NB):
                    load(g + 3, j)
            for g in range(NG - 3, NG + 1):
                store(g - 1)
                if g == NG - 1:
                    sp.wait_ge(conv_done, NG * 2 * NB)
                    sp.dma_start(w_gate[:, :, :, :], a["w_gate"].rearrange("e (m p) h -> p e m h", p=P))\
                        .then_inc(ffn_in, 16)
                    sp.dma_start(w_fc[:, :, :, :], a["w_fc"].rearrange("e (m p) h -> p e m h", p=P))\
                        .then_inc(ffn_in, 16)
                    sp.dma_start(w_proj[:, :, :], a["w_proj"].rearrange("e h c -> h e c")).then_inc(ffn_in, 16)
            sp.wait_ge(pre_v, CLASS_V + 9)
            sp.wait_ge(patch_out, 16 + 16 * NG)
            sp.dma_start(scratch_img[:, 1 + WIN, :], patch[:, :]).then_inc(cls_out, 16)
            sp.wait_ge(cls_out, 16)
            sp.wait_ge(pad_zero, 1)
            for i in range(4):
                for t in range(H_LOTS[i], H_LOTS[i + 1]):
                    n = R if t < NT - 1 else LASTR
                    sp.dma_start(h_rows[0:n, t, :], scratch[t * R:t * R + n, :]).then_inc(h_in[i], 16)
            for t in range(NT):
                sp.wait_ge(y_made, t + 1)
                n = R if t < NT - 1 else LASTR
                sp.dma_start(out[t * R:t * R + n, :], y_rows[0:n, t % 2, :]).then_inc(out_sem[t % 2], 16)
            sp.wait_ge(out_sem[0], 16 * ((NT + 1) // 2))
            sp.wait_ge(out_sem[1], 16 * (NT // 2))

        @block.gpsimd
        def _(pool):
            pool.memset(ident[:, :], 0.0).then_inc(masks_made, 1)
            pool.memset(mean_ones[:, :], 1.0 / C).then_inc(masks_made, 1)
            for m in (own_window, own_image, own_seq, same_seq):
                pool.memset(m[:, :], 1.0).then_inc(masks_made, 1)
            pool.memset(gq_block[:, :, :], 0.0).then_inc(masks_made, 1)
            n = 7
            pool.wait_ge(masks_made, n)
            pool.affine_select(out=ident[:, :], in_=ident[:, :], compare_op=ALU.not_equal, fill=1.0, base=0,
                               pattern=[[-1, P]], channel_multiplier=1).then_inc(masks_made, 1)
            n += 1
            for m, size, pat in ((own_window, KEYS, [[-KEYS, TW]]), (own_image, WIN, [[-WIN, GI]]),
                                 (own_seq, TOK, [[-TOK, TI]]), (same_seq, TOK, [[-TOK, TI], [0, TOK]])):
                up = [[-s, k] for s, k in pat]
                pool.affine_select(out=m[:, :], in_=m[:, :], compare_op=ALU.is_ge, fill=0.0, base=0,
                                   pattern=pat, channel_multiplier=1).then_inc(masks_made, 1)
                n += 1
                pool.wait_ge(masks_made, n)
                pool.affine_select(out=m[:, :], in_=m[:, :], compare_op=ALU.is_ge, fill=0.0, base=size - 1,
                                   pattern=up, channel_multiplier=-1).then_inc(masks_made, 1)
                n += 1
                pool.wait_ge(masks_made, n)
            pool.affine_select(out=earlier[:, :], in_=same_seq[:, :], compare_op=ALU.is_ge, fill=0.0, base=-1,
                               pattern=[[1, R]], channel_multiplier=-1).then_inc(masks_made, 1)
            pool.tensor_scalar(neg_mask[:, :], same_seq[:, :], -1.0, NEG, ALU.add, ALU.mult).then_inc(masks_made, 1)
            for e in range(E):
                pool.memset(rank_w[:, e:e + 1], float(E - e)).then_inc(masks_made, 1)
            n += 2 + E
            assert n == MASKS

            def split_lo(g, j):
                c, n = BLKS[j]
                pool.wait_ge(hi_made, g * NB + j + 1)
                pool.tensor_tensor(x_lo[:, 0:KFULL, c:c + n], x_raw[:, 0:KFULL, c:c + n],
                                   x_hi[:, 0:KFULL, c:c + n].bitcast(F32), ALU.subtract)
                pool.tensor_tensor(x_lo[0:KREST, KFULL, c:c + n], x_raw[0:KREST, KFULL, c:c + n],
                                   x_hi[0:KREST, KFULL, c:c + n].bitcast(F32), ALU.subtract).then_inc(lo_made, 1)

            for j in range(NB):
                split_lo(0, j)
            with pool.Fori(1, NG) as g:
                for j in range(NB):
                    split_lo(g, j)
            pool.wait_ge(pre_v, CLASS_V + 9)
            pool.memset(h_rows[:, NT - 1, :], 0.0).then_inc(pad_zero, 1)

        @block.scalar
        def _(act):
            act.dma_start(w_conv[:, 0:KFULL, :], a["conv_w"][0:KFULL * P, :].rearrange("(k p) c -> p k c", p=P))\
                .then_inc(weights_in, 16)
            act.dma_start(w_conv[0:KPAD, KFULL, :], a["conv_w"][KFULL * P:KFULL * P + KPAD, :])\
                .then_inc(weights_in, 16)
            for t, n in ((wkv, "la_wkv"), (wq, "la_wq"), (gwkv, "ga_wkv"), (gwq, "ga_wq"), (proj, "la_proj_w"),
                         (gproj, "ga_proj_w"), (mod_w, "mod_w"), (router, "w_router")):
                act.dma_start(t[:, :, :], mpn(a[n])).then_inc(weights_in, 16)
            for n in KEPT_ROWS + SETUP_ROWS:
                act.dma_start(rows[n][:, :], a[n].rearrange("(o c) -> o c", o=1).broadcast_to([P, C]))\
                    .then_inc(weights_in, 16)
            act.dma_start(col_vectors[:, :, :], a["cols"]).then_inc(weights_in, 16)

            def split_hi(g, j):
                c, n = BLKS[j]
                act.wait_ge(raw_in[j], g * 32 + 32)
                if not isinstance(g, int) or g >= 1:
                    act.wait_ge(conv_done, g * 2 * NB - 2 * NB + 2 * j + 2)
                act.activation(x_hi[:, 0:KFULL, c:c + n], x_raw[:, 0:KFULL, c:c + n], ACT.Copy)
                act.activation(x_hi[0:KREST, KFULL, c:c + n], x_raw[0:KREST, KFULL, c:c + n], ACT.Copy)\
                    .then_inc(hi_made, 1)

            def conv_move(g, slot, n):
                c, w = BLKS[n // 2]
                act.wait_ge(conv_done, g * 2 * NB + n + 1)
                act.activation(pe_t[:, slot, n % 2, c:c + w], ps[:, n % 2, 0:w], ACT.Copy).then_inc(conv_moved, 1)

            def front(g):
                act.wait_ge(pe_front, g * PF + 2)
                for m in range(2):
                    act.activation(red_hat_t[:, m, :], ps[:, 3, P * m:P * m + P], ACT.Identity,
                                   bias=cols["la_ln_q_b"][:, m:m + 1], scale=cols["la_ln_q_g"][:, m:m + 1])\
                        .then_inc(act_front, 1)
                act.wait_ge(pe_front, g * PF + 3)
                act.activation(q_t[:, :, :], ps[:, 2, 0:C], ACT.Copy).then_inc(act_front, 1)

            def front_keys(g):
                for i, j in enumerate((0, 2)):
                    act.wait_ge(pe_front, g * PF + 4 + i)
                    act.activation(qk[:, :, j:HEADS:4, :],
                                   ps[:, j, :].rearrange("p (m h w) -> p m h w", m=2, h=2), ACT.Copy)\
                        .then_inc(act_front, 1)

            def tail_a(g):
                act.wait_ge(pe_tail, g * PT + 2)
                for m in range(2):
                    act.activation(lo_part[:, m, :], ps[:, 7, P * m:P * m + P], ACT.Identity,
                                   bias=cols["la_proj_b"][:, m:m + 1]).then_inc(act_tail, 1)

            def tail_b(g):
                act.wait_ge(pe_tail, g * PT + 3)
                act.activation(lo_all[:, bass.ds(g, 1), :], ps[:, 6, C:2 * C], ACT.Copy).then_inc(group_kept, 1)

            def body(g, slot, tail=True, nxt=True, split=True):
                if tail:
                    tail_a(g - 1)
                for k in range(NTT // 2):
                    act.wait_ge(tok_turned, g * (NTT // 2) + k + 1)
                    act.activation(tok[0:TT, 2 * k:2 * k + 2, :], ps[0:TT, 2 + k % 2, :], ACT.Copy)\
                        .then_inc(tok_moved, 1)
                if nxt:
                    conv_move(g + 1, 1 - slot, 0)
                    if tail:
                        split_hi(g + 1, 2)
                    conv_move(g + 1, 1 - slot, 1)
                    if split:
                        split_hi(g + 2, 0)
                    conv_move(g + 1, 1 - slot, 2)
                act.wait_ge(dve_main, g * DM + SUBTRACTED)
                act.activation(soft[0:TH, :, :], soft[0:TH, :, :], ACT.Exp).then_inc(act_main, 1)
                if nxt:
                    conv_move(g + 1, 1 - slot, 3)
                    if split:
                        split_hi(g + 2, 1)
                    conv_move(g + 1, 1 - slot, 4)
                    conv_move(g + 1, 1 - slot, 5)
                for k, (m, q) in enumerate(CTX_FILLS):
                    if tail and k == 3:
                        tail_b(g - 1)
                    act.wait_ge(ctx_done, g * len(CTX_FILLS) + k + 1)
                    n = len(QUADS[q]) * HEADS * TW
                    if q < 2:
                        act.activation(ctxv[:, m, :, W0[4 * q]:W0[4 * q] + 4 * TW].rearrange("p h (t w) -> p t h w", w=TW),
                                       ps[:, 4 + k % 2, 0:n].rearrange("p (t h w) -> p t h w", t=4, h=HEADS), ACT.Copy)\
                            .then_inc(ctx_moved, 1)
                    else:
                        act.activation(ctxv[:, :, :, W0[-2]:GW],
                                       ps[:, 4 + k % 2, 0:2 * HEADS * LASTW].rearrange("p (m h w) -> p m h w", m=2, h=HEADS),
                                       ACT.Copy).then_inc(ctx_moved, 1)
                if nxt:
                    front(g + 1)
                act.wait_ge(pe_tail, g * PT + 1)
                for m in range(2):
                    act.activation(agg_t[:, m, :], ps[:, 6, P * m:P * m + P], ACT.Identity,
                                   bias=v_bias[:, m:m + 1]).then_inc(act_tail, 1)
                if nxt:
                    front_keys(g + 1)

            for j in range(NB):
                split_hi(0, j)
            act.wait_ge(pre_v, SETUP_V)
            for j in range(NB):
                conv_move(0, 0, 2 * j)
                conv_move(0, 0, 2 * j + 1)
                split_hi(1, j)
            front(0)
            front_keys(0)
            body(0, 0, tail=False)
            with act.Fori(0, NG // 2 - 2) as r:
                body(2 * r + 1, 1)
                body(2 * r + 2, 0)
            body(NG - 3, 1)
            body(NG - 2, 0, split=False)
            body(NG - 1, 1, nxt=False)
            tail_a(NG - 1)
            tail_b(NG - 1)

            act.wait_ge(pre_v, CLASS_V + 3)
            act.activation(s_mat[:, 0:P], s_mat[:, 0:P], ACT.Exp).then_inc(cls_exp, 1)
            for k in (0, 2):
                act.wait_ge(pre, 12 + k)
                cls_ctx_move(act.activation, k, ACT.Copy)
            act.wait_ge(pre, 16)
            for m in range(2):
                act.activation(agg_t[:, m, :], ps[:, 5, P * m:P * m + P], ACT.Identity,
                               bias=gv_bias[:, m:m + 1]).then_inc(cls_gathered, 1)

            def rows_move(i, t):
                act.wait_ge(rows_turned, i * NT + t + 1)
                act.activation(nt_t[:, t % 2, :, :], ps[:, t % 2, 0:2 * R], ACT.Copy).then_inc(rows_moved, 1)

            rows_move(0, 0)
            for t in range(NT):
                if t + 1 < NT:
                    rows_move(0, t + 1)
                act.wait_ge(max_found, t + 1)
                act.activation(s_two[0:R, t % 2, :], s_two[0:R, t % 2, :], ACT.Exp, bias=soft2[0:R, t % 2, 0:1],
                               accum_out=soft2[0:R, t % 2, 1:2]).then_inc(exped, 1)
            for t in range(NT):
                rows_move(1, t)
            act.wait_ge(logits_done, NT)
            act.activation(logit[0:R, :, :], ps[0:R, 2, 0:NT * E], ACT.Copy).then_inc(logits_moved, 1)
            act.wait_ge(p2v, GATE_MAX)
            act.activation(gt1[0:R, :, :], gt1[0:R, :, :], ACT.Exp).then_inc(gate_exp, 1)
            for t in range(NT):
                act.wait_ge(disp_done, t + 1)
                for m in range(2):
                    act.activation(xb[:, m, t, :, :], ps[:, t % 2, ES * m:ES * m + ES], ACT.Copy)\
                        .then_inc(disp_moved, 1)

            def silu(e):
                act.wait_ge(up_done, e + 1)
                if e >= 2:
                    act.wait_ge(hid_done, e - 1)
                act.activation(hid[:, e % 2, 0, :], ps[:, 2 * (e % 2), 0:SLOTS], ACT.Silu).then_inc(silu_done, 1)

            silu(0)
            for e in range(E):
                if e + 1 < E:
                    silu(e + 1)
                act.wait_ge(down_done, e + 1)
                for m in range(2):
                    act.activation(xb[:, m, :, e, :],
                                   ps[:, 4 + 2 * (e % 2) + m, 0:SLOTS].rearrange("p (t s) -> p t s", t=NT), ACT.Copy)\
                        .then_inc(down_moved, 1)
            for t in range(NT):
                act.wait_ge(outs_turned, t + 1)
                if t >= 2:
                    act.wait_ge(y_done, t - 1)
                act.activation(o_rows[0:EH, t % 2, :, :], ps[0:EH, t % 2, :], ACT.Copy).then_inc(outs_moved, 1)

        @block.tensor
        def _(pe):
            pe.wait_ge(weights_in, 16 * W_DMAS)
            pe.wait_ge(masks_made, MASKS)
            for b, w in enumerate((wkv, gwkv)):
                for hc in range(2):
                    for m in range(2):
                        last = pe.transpose(ps[:, b, C * hc + P * m:C * hc + P * m + P], w[:, m, P * hc:P * hc + P],
                                            ident[:, :])
                last.then_inc(pre, 1)
            pe.wait_ge(pre_v, 4)
            for b, w in enumerate((wv_fold, gwv_fold)):
                for m in range(2):
                    last = pe.matmul(ps[:, 2 + b, 0:C], mean_ones[:, :], w[:, m, :], start=(m == 0), stop=(m == 1))
                last.then_inc(pre, 1)
            for i, (w, bc) in enumerate(((wkv, "la_ln_kv_b"), (gwkv, "ga_ln_kv_b"))):
                for hc in range(2):
                    for m in range(2):
                        last = pe.matmul(ps[:, 4, 2 * i + hc:2 * i + hc + 1], w[:, m, C + P * hc:C + P * hc + P],
                                         cols[bc][:, m:m + 1], start=(m == 0), stop=(m == 1))
            last.then_inc(pre, 1)
            for m in range(2):
                last = pe.matmul(ps[:, 5, 0:1], mean_ones[:, :], cols["class_emb"][:, m:m + 1],
                                 start=(m == 0), stop=(m == 1))
            last.then_inc(pre, 1)
            pe.wait_ge(pre_v, SQ_DONE)
            for m in range(2):
                last = pe.matmul(ps[:, 5, 1:2], mean_ones[:, :], small[:, 4 + m:5 + m], start=(m == 0), stop=(m == 1))
            last.then_inc(pre, 1)
            pe.wait_ge(pre_v, QHAT_DONE)
            for hc in range(2):
                for m in range(2):
                    last = pe.matmul(ps[:, 5, 2 + hc:3 + hc], gwq[:, m, P * hc:P * hc + P], small[:, 8 + m:9 + m],
                                     start=(m == 0), stop=(m == 1))
            last.then_inc(pre, 1)
            pe.wait_ge(pre_v, GQ_DONE)
            for m in range(2):
                for hc in range(2):
                    last = pe.matmul(ps[:, 5, 8 + 8 * m:16 + 8 * m], gwk_fold[:, hc, P * m:P * m + P],
                                     gq_block[:, hc, :], start=(hc == 0), stop=(hc == 1))
            last.then_inc(pre, 1)
            pe.wait_ge(pre_v, SETUP_V)
            pe.wait_ge(w_split, W_SPLIT)

            def conv_part(g, first, count):
                for u in range(first, first + count):
                    n, i = u // NPR, u % NPR
                    m, j, k, part = n % 2, n // 2, i // 3, i % 3
                    c, w = BLKS[j]
                    if u % (2 * NPR) == 0:
                        pe.wait_ge(lo_made, g * NB + j + 1)
                    if i == 0 and (n >= 2 or not isinstance(g, int) or g >= 1):
                        pe.wait_ge(conv_moved, g * 2 * NB + n - 1)
                    if u == 0 and (not isinstance(g, int) or g >= 1):
                        pe.wait_ge(act_front, g * AF)
                    kk = P if k < KFULL else KREST
                    wt, xt = ((w_hi, x_hi), (w_hi, x_lo), (w_lo, x_hi))[part]
                    mm = pe.matmul(ps[:, m, 0:w], wt[0:kk, k, P * m:P * m + P], xt[0:kk, k, c:c + w],
                                   start=(i == 0), stop=(i == NPR - 1))
                    if i == NPR - 1:
                        mm.then_inc(conv_done, 1)

            def turn_window_sums(g, slot):
                pe.wait_ge(red_made, g * 2 * NB + 2 * NB)
                if not isinstance(g, int) or g >= 1:
                    pe.wait_ge(tok_moved, g * (NTT // 2))
                for m in range(2):
                    last = pe.transpose(ps[:, 2, P * m:P * m + P], red_sum[:, slot, m, :], ident[:, :])
                last.then_inc(pe_front, 1)

            def turn_red_hat(g):
                pe.wait_ge(dve_front, g * DF + RED_HAT)
                for m in range(2):
                    last = pe.transpose(ps[:, 3, P * m:P * m + P], red_hat[:, P * m:P * m + P], ident[:, :])
                last.then_inc(pe_front, 1)

            def queries(g):
                pe.wait_ge(act_front, g * AF + 2)
                for hc in range(2):
                    for m in range(2):
                        last = pe.matmul(ps[:, 2, P * hc:P * hc + P], wq[:, m, P * hc:P * hc + P], red_hat_t[:, m, :],
                                         start=(m == 0), stop=(m == 1))
                last.then_inc(pe_front, 1)

            def query_keys(g):
                pe.wait_ge(act_front, g * AF + 3)
                pe.wait_ge(conv_moved, g * 2 * NB + 2 * NB)
                for pair in ((0, 1), (2, 3)):
                    for m in range(2):
                        for hc in range(2):
                            for j in pair:
                                o = P * (2 * m + hc)
                                last = pe.matmul(ps[:, j, o:o + P], wk_fold[32 * j:32 * j + 32, hc, P * m:P * m + P],
                                                 q_t[32 * j:32 * j + 32, hc, :], start=True, stop=True)
                    last.then_inc(pe_front, 1)

            def gather_values(g, hc):
                if hc == 0:
                    pe.wait_ge(ctx_moved, g * len(CTX_FILLS) + len(CTX_FILLS))
                    if not isinstance(g, int) or g >= 1:
                        pe.wait_ge(group_kept, g)
                for j in range(4):
                    h = 4 * hc + j
                    for m in range(2):
                        last = pe.matmul(ps[32 * j:32 * j + 32, 6, P * hc:P * hc + P],
                                         wv_fold[:, m, DH * h:DH * h + DH], ctxv[:, m, h, :],
                                         start=(m == 0), stop=(m == 1))
                if hc == 1:
                    last.then_inc(pe_tail, 1)

            def project(g):
                pe.wait_ge(act_tail, g * AT + 2)
                for m in range(2):
                    for hc in range(2):
                        last = pe.matmul(ps[:, 7, P * m:P * m + P], proj[:, hc, P * m:P * m + P], agg_t[:, hc, :],
                                         start=(hc == 0), stop=(hc == 1))
                last.then_inc(pe_tail, 1)

            def local_out(g):
                pe.wait_ge(dve_tail, g * DT + LOCAL)
                for m in range(2):
                    last = pe.transpose(ps[:, 6, C + P * m:C + P * m + P], lo_t[:, m, :], ident[:, :])
                last.then_inc(pe_tail, 1)
                for m in range(2):
                    pe.matmul(ps[:, 7, 0:C], lo_t[:, m, :], mod_w[:, m, :], start=(m == 0), stop=(m == 1))
                for m in range(2):
                    last = pe.matmul(ps[:, 7, C:C + HEADS], lo_t[:, m, :], gqk[:, m, :], start=(m == 0), stop=(m == 1))
                last.then_inc(pe_tail, 1)

            def body(g, slot, tail=True, nxt=True):
                at = 0

                def conv(n):
                    nonlocal at
                    if nxt:
                        conv_part(g + 1, at, n)
                        at += n

                if tail:
                    project(g - 1)
                pe.wait_ge(act_front, g * AF + AF)
                pe.wait_ge(dve_front, g * DF + DF)
                for k in range(NTT // 2):
                    if k >= 2:
                        pe.wait_ge(tok_moved, g * (NTT // 2) + k - 1)
                    for t in (2 * k, 2 * k + 1):
                        for m in range(2):
                            o = C * (t % 2) + P * m
                            last = pe.transpose(ps[0:TT, 2 + k % 2, o:o + P],
                                                pe_t[:, slot, m, KEYS * W0[t]:KEYS * W0[t] + TT], ident[:, :])
                    last.then_inc(tok_turned, 1)
                    if k == 4:
                        pe.wait_ge(dve_main, g * DM + QUAD0)
                    for t in (2 * k, 2 * k + 1):
                        for m in range(2):
                            o = HEADS * TW * (t % 4)
                            last = pe.matmul(ps[0:TT, 4 + (t // 4) % 2, o:o + HEADS * TW],
                                             pe_t[:, slot, m, KEYS * W0[t]:KEYS * W0[t] + TT],
                                             qk[:, m, :, W0[t]:W0[t] + TW], start=(m == 0), stop=(m == 1))
                    if k in (1, 3, 4):
                        last.then_inc(pe_main, 1)
                    conv(2)
                conv(CONV_C)
                pe.wait_ge(dve_main, g * DM + SCORED)
                pe.transpose(ps[0:TH, 6, 0:TT], score[0:TT, :, :], ident[0:TT, 0:TT]).then_inc(pe_main, 1)
                conv(CONV_D)
                pe.wait_ge(dve_main, g * DM + SOFTMAXED)
                if tail:
                    pe.wait_ge(dve_tail, g * DT - DT + LOCAL)
                pe.transpose(ps[0:TT, 7, 0:TH], soft[0:TH, :, :], ident[0:TH, 0:TH]).then_inc(pe_main, 1)
                conv(2 * NB * NPR - CONV_D - CONV_C - NTT)
                assert not nxt or at == 2 * NB * NPR, at
                pe.wait_ge(dve_main, g * DM + SPREAD)
                pe.wait_ge(tok_moved, g * (NTT // 2) + NTT // 2)

                def weigh(dst, m, t, windows):
                    return pe.matmul(dst, tok[0:TT, t, P * m:P * m + P],
                                     spread[0:TT, HEADS * t:HEADS * t + HEADS, 0:windows], start=True, stop=True)

                for k, (m, q) in enumerate(CTX_FILLS):
                    if k >= 2:
                        pe.wait_ge(ctx_moved, g * len(CTX_FILLS) + k - 1)
                    bank = ps[:, 4 + k % 2, :]
                    if q < 2:
                        for t in QUADS[q]:
                            o = HEADS * TW * (t % 4)
                            last = weigh(bank[:, o:o + HEADS * TW], m, t, TW)
                    else:
                        w = W0[-1] - W0[-2]
                        for m in range(2):
                            o = HEADS * LASTW * m
                            both = bank[:, o:o + HEADS * LASTW].rearrange("p (h w) -> p h w", h=HEADS)
                            weigh(both[:, :, 0:w], m, NTT - 2, w)
                            last = weigh(both[:, :, w:LASTW], m, NTT - 1, TW)
                    last.then_inc(ctx_done, 1)
                    if nxt and k == 0:
                        turn_window_sums(g + 1, 1 - slot)
                    if tail and k == 2:
                        local_out(g - 1)
                if nxt:
                    turn_red_hat(g + 1)
                gather_values(g, 0)
                if nxt:
                    queries(g + 1)
                gather_values(g, 1)
                if nxt:
                    query_keys(g + 1)
                if tail:
                    pe.wait_ge(dve_tail, g * DT)

            conv_part(0, 0, 2 * NB * NPR)
            turn_window_sums(0, 0)
            turn_red_hat(0)
            queries(0)
            query_keys(0)
            body(0, 0, tail=False)
            with pe.Fori(0, NG // 2 - 1) as r:
                body(2 * r + 1, 1)
                body(2 * r + 2, 0)
            body(NG - 1, 1, nxt=False)
            project(NG - 1)
            local_out(NG - 1)

            pe.wait_ge(pre_v, CLASS_V + 1)
            pe.transpose(ps[:, 0, 0:P], gs_all[:, :, :], ident[:, :]).then_inc(pre, 1)
            pe.wait_ge(pre_v, CLASS_V + 6)
            pe.transpose(ps[:, 0, P:2 * P], s_mat[:, 0:P], ident[:, :]).then_inc(pre, 1)
            pe.wait_ge(pre_v, CLASS_V + 8)
            pe.wait_ge(group_kept, NG)
            for k in range(4):
                m = k // 2
                for i in range(NG // 2):
                    g = NG // 2 * (k % 2) + i
                    last = pe.matmul(ps[:, 1 + k, HEADS * GI * i:HEADS * GI * i + HEADS * GI],
                                     lo_all[:, g, P * m:P * m + P], cls_spread[:, HEADS * g:HEADS * g + HEADS, :],
                                     start=True, stop=True)
                last.then_inc(pre, 1)
            pe.wait_ge(cls_moved, 4)
            for hc in range(2):
                for j in range(4):
                    h = 4 * hc + j
                    for m in range(2):
                        last = pe.matmul(ps[32 * j:32 * j + 32, 5, P * hc:P * hc + P],
                                         gwv_fold[:, m, DH * h:DH * h + DH], ctxv[:, m, h, :],
                                         start=(m == 0), stop=(m == 1))
            last.then_inc(pre, 1)
            pe.wait_ge(cls_gathered, 2)
            for hc in range(2):
                last = pe.matmul(ps[:, 6, 0:C], agg_t[:, hc, :], gproj[:, hc, :], start=(hc == 0), stop=(hc == 1))
            last.then_inc(pre, 1)

            def turn_rows(i, t):
                pe.wait_ge(rows_normal, i * NT + t + 1)
                if i or t >= 2:
                    pe.wait_ge(rows_moved, i * NT + t - 1)
                for m in range(2):
                    last = pe.transpose(ps[:, t % 2, R * m:R * m + R], n_rows[0:R, t, P * m:P * m + P],
                                        ident[0:R, 0:R])
                last.then_inc(rows_turned, 1)

            def products(t):
                pe.wait_ge(rows_moved, t + 1)
                if t >= 2:
                    pe.wait_ge(sums_masked, t - 1)
                for m in range(2):
                    last = pe.matmul(ps[0:R, 2 + t % 2, 0:R], nt_t[:, t % 2, m, :], nt_t[:, t % 2, m, :],
                                     start=(m == 0), stop=(m == 1))
                last.then_inc(sums_done, 1)

            turn_rows(0, 0)
            products(0)
            for t in range(NT):
                if t + 1 < NT:
                    turn_rows(0, t + 1)
                    products(t + 1)
                pe.wait_ge(weighted, t + 1)
                if t >= 2:
                    pe.wait_ge(added, t - 1)
                pe.matmul(ps[0:R, 4 + t % 2, 0:C], s_two[0:R, t % 2, :], n_rows[0:R, t, :], start=True, stop=True)\
                    .then_inc(mixed, 1)
            turn_rows(1, 0)
            for t in range(NT):
                if t + 1 < NT:
                    turn_rows(1, t + 1)
                pe.wait_ge(rows_moved, NT + t + 1)
                for m in range(2):
                    last = pe.matmul(ps[0:R, 2, E * t:E * t + E], nt_t[:, t % 2, m, :], router[:, m, :],
                                     start=(m == 0), stop=(m == 1))
                last.then_inc(logits_done, 1)
            pe.wait_ge(p2v, HOT_DONE)
            pe.matmul(ps[0:R, 4, 0:NT * E], earlier[0:R, :], hot[0:R, 0, :, :], start=True, stop=True)
            pe.matmul(ps[0:R, 5, 0:NT * E], same_seq[0:R, :], hot[0:R, 0, :, :], start=True, stop=False)
            pe.matmul(ps[0:R, 5, 0:NT * E], earlier[0:R, :], hot[0:R, 1, :, :], start=False, stop=True)\
                .then_inc(ranked, 1)
            for t in range(NT):
                pe.wait_ge(disp_made, t + 1)
                if t >= 2:
                    pe.wait_ge(disp_moved, 2 * t - 2)
                for m in range(2):
                    last = pe.matmul(ps[:, t % 2, ES * m:ES * m + ES], n_rows[0:R, t, P * m:P * m + P],
                                     disp[0:R, t % 2, :, :, :], start=True, stop=True)
                last.then_inc(disp_done, 1)

            def up(e):
                if e == 0:
                    pe.wait_ge(ffn_in, 48)
                    pe.wait_ge(disp_moved, 2 * NT)
                if e >= 2:
                    pe.wait_ge(hid_done, e - 1)
                for i, w in enumerate((w_gate, w_fc)):
                    for m in range(2):
                        last = pe.matmul(ps[:, 2 * (e % 2) + i, 0:SLOTS], w[:, e, m, :], xb[:, m, :, e, :],
                                         start=(m == 0), stop=(m == 1))
                last.then_inc(up_done, 1)

            up(0)
            for e in range(E):
                if e + 1 < E:
                    up(e + 1)
                pe.wait_ge(hid_done, e + 1)
                if e >= 2:
                    pe.wait_ge(down_moved, 2 * e - 2)
                for m in range(2):
                    last = pe.matmul(ps[:, 4 + 2 * (e % 2) + m, 0:SLOTS], w_proj[:, e, P * m:P * m + P],
                                     hid[:, e % 2, 1, :], start=True, stop=True)
                last.then_inc(down_done, 1)

            def turn_outs(t):
                if t == 0:
                    pe.wait_ge(down_moved, 2 * E)
                if t >= 2:
                    pe.wait_ge(outs_moved, t - 1)
                for half in range(2):
                    for m in range(2):
                        pe.transpose(ps[0:EH, t % 2, C * half + P * m:C * half + P * m + P],
                                     xb[:, m, t, 8 * half:8 * half + 8, :], ident[:, :])
                pe.wait_ge(comb_made, t + 1)
                if t >= 2:
                    pe.wait_ge(comb_moved, t - 1)
                for half in range(2):
                    last = pe.transpose(ps[0:EH, 2 + t % 2, P * half:P * half + R],
                                        comb[0:R, t % 2, 8 * half:8 * half + 8, :, :], ident[0:R, 0:R])
                last.then_inc(outs_turned, 1)

            turn_outs(0)
            for t in range(NT):
                if t + 1 < NT:
                    turn_outs(t + 1)
                pe.wait_ge(comb_moved, t + 1)
                pe.wait_ge(outs_moved, t + 1)
                if t >= 2:
                    pe.wait_ge(y_made, t - 1)
                for half in range(2):
                    last = pe.matmul(ps[0:R, 4 + t % 2, 0:C], comb_t[0:EH, t % 2, half, :],
                                     o_rows[0:EH, t % 2, half, :], start=(half == 0), stop=(half == 1))
                last.then_inc(y_done, 1)

        @block.vector
        def _(dve):
            def rsqrt(step, settled, v, y, n):
                p = v.shape[0]
                a, b = newton[0:p, 0, 0:n], newton[0:p, 1, 0:n]
                step(dve.tensor_scalar(a.bitcast(I32), v.bitcast(I32), 1, None, ALU.logical_shift_right))
                settled()
                step(dve.tensor_scalar(y.bitcast(I32), a.bitcast(I32), -1.0, float(0x5f3759df), ALU.mult, ALU.add))
                for _ in range(3):
                    settled()
                    step(dve.tensor_tensor(a, y, y, ALU.mult))
                    settled()
                    step(dve.scalar_tensor_tensor(out=b, in0=a, scalar=-0.5, in1=v, op0=ALU.mult, op1=ALU.mult))
                    settled()
                    step(dve.scalar_tensor_tensor(out=y, in0=b, scalar=1.5, in1=y, op0=ALU.add, op1=ALU.mult))

            made = 0

            def first(ins):
                nonlocal made
                made += 1
                ins.then_inc(pre_v, 1)

            def first_settled():
                dve.wait_ge(pre_v, made)

            dve.wait_ge(masks_made, MASKS)
            dve.wait_ge(weights_in, 16 * W_DMAS)
            for kk, k0, k1 in ((P, 0, KFULL), (KREST, KFULL, KFULL + 1)):
                dve.tensor_copy(w_hi[0:kk, k0:k1, :], w_conv[0:kk, k0:k1, :]).then_inc(w_split, 1)
            dve.wait_ge(w_split, 2)
            for kk, k0, k1 in ((P, 0, KFULL), (KREST, KFULL, KFULL + 1)):
                dve.tensor_tensor(w_lo[0:kk, k0:k1, :], w_conv[0:kk, k0:k1, :], w_hi[0:kk, k0:k1, :].bitcast(F32),
                                  ALU.subtract).then_inc(w_split, 1)
            for w, f, gn in ((wkv, wv_fold, "la_ln_kv_g"), (gwkv, gwv_fold, "ga_ln_kv_g")):
                for m in range(2):
                    first(dve.tensor_scalar(f[:, m, :], w[:, m, C:2 * C], cols[gn][:, m:m + 1], None, ALU.mult))
            for b, (f, gn) in enumerate(((wk_fold, "la_ln_kv_g"), (gwk_fold, "ga_ln_kv_g"))):
                dve.wait_ge(pre, b + 1)
                first(dve.tensor_tensor(f[:, :, :], ps[:, b, :].rearrange("p (h c) -> p h c", h=2),
                                        rows[gn][:, :].unsqueeze(1).broadcast_to([P, 2, C]), ALU.mult))
                dve.wait_ge(pre_v, made)
                first(dve.tensor_reduce(small[:, 0:2], f[:, :, :], AX_X, ALU.add))
                dve.wait_ge(pre_v, made)
                first(dve.tensor_scalar(small[:, 2:4], small[:, 0:2], -1.0 / C, None, ALU.mult))
                dve.wait_ge(pre_v, made)
                for hc in range(2):
                    first(dve.tensor_scalar(f[:, hc, :], f[:, hc, :], small[:, 2 + hc:3 + hc], SCALE,
                                            ALU.add, ALU.mult))
            for b, f in enumerate((wv_fold, gwv_fold)):
                dve.wait_ge(pre, 3 + b)
                first(dve.tensor_tensor(f[:, :, :], f[:, :, :],
                                        ps[:, 2 + b, 0:C].unsqueeze(1).broadcast_to([P, 2, C]), ALU.subtract))
            dve.wait_ge(pre, 5)
            first(dve.tensor_copy(v_bias[:, :], ps[:, 4, 0:2]))
            first(dve.tensor_copy(gv_bias[:, :], ps[:, 4, 2:4]))
            dve.wait_ge(pre, 6)
            dve.wait_ge(pre_v, made)
            first(dve.tensor_copy(small[:, 0:1], ps[:, 5, 0:1]))
            dve.wait_ge(pre_v, made)
            first(dve.tensor_scalar(small[:, 2:4], cols["class_emb"][:, :], small[:, 0:1], None, ALU.subtract))
            dve.wait_ge(pre_v, made)
            first(dve.tensor_tensor(small[:, 4:6], small[:, 2:4], small[:, 2:4], ALU.mult))
            assert made == SQ_DONE
            dve.wait_ge(pre, 7)
            first(dve.tensor_scalar(small[:, 12:13], ps[:, 5, 1:2], EPS, None, ALU.add))
            dve.wait_ge(pre_v, made)
            rsqrt(first, first_settled, small[:, 12:13], small[:, 6:7], 1)
            dve.wait_ge(pre_v, made)
            first(dve.tensor_scalar(small[:, 8:10], small[:, 2:4], small[:, 6:7], None, ALU.mult))
            dve.wait_ge(pre_v, made)
            first(dve.tensor_tensor(small[:, 10:12], small[:, 8:10], cols["ga_ln_q_g"][:, :], ALU.mult))
            dve.wait_ge(pre_v, made)
            first(dve.tensor_tensor(small[:, 8:10], small[:, 10:12], cols["ga_ln_q_b"][:, :], ALU.add))
            assert made == QHAT_DONE
            dve.wait_ge(pre, 8)
            for h in range(HEADS):
                j, hc = h % 4, h // 4
                first(dve.tensor_copy(gq_block[32 * j:32 * j + 32, hc, h:h + 1],
                                      ps[32 * j:32 * j + 32, 5, 2 + hc:3 + hc]))
            assert made == GQ_DONE
            dve.wait_ge(pre, 9)
            first(dve.tensor_copy(gqk[:, :, :], ps[:, 5, 8:24].rearrange("p (m h) -> p m h", m=2)))
            dve.wait_ge(pre_v, made)
            first(dve.tensor_tensor(rows["class_emb"][:, :], rows["class_emb"][:, :], rows["ga_proj_b"][:, :], ALU.add))
            assert made == SETUP_V, made

            def variance(step, settled, st, eps, dst, v):
                step(dve.tensor_scalar(v[:, 1:2], st[:, 1:2], st[:, 4:5], None, ALU.subtract))
                step(dve.tensor_scalar(v[:, 2:3], st[:, 2:3], st[:, 5:6], 4.0 / C, ALU.add, ALU.mult))
                settled()
                step(dve.scalar_tensor_tensor(out=v[:, 3:4], in0=v[:, 1:2], scalar=v[:, 1:2], in1=v[:, 2:3],
                                              op0=ALU.mult, op1=ALU.add))
                settled()
                step(dve.tensor_scalar(dst, v[:, 3:4], 0.25, eps, ALU.mult, ALU.add))

            def window_sums(g, slot, n):
                c, w = BLKS[n // 2]
                dve.wait_ge(conv_moved, g * 2 * NB + n + 1)
                dve.tensor_reduce(red_sum[:, slot, n % 2, c // KEYS:(c + w) // KEYS],
                                  pe_t[:, slot, n % 2, c:c + w].rearrange("p (w k) -> p w k", k=KEYS), AX_X, ALU.add)\
                    .then_inc(red_made, 1)

            def front(g, between=None):
                n = 0

                def step(ins):
                    nonlocal n
                    n += 1
                    ins.then_inc(dve_front, 1)

                def settled():
                    dve.wait_ge(dve_front, g * DF + n)

                dve.wait_ge(pe_front, g * PF + 1)
                step(dve.bn_stats(st6[:, 0, :], ps[:, 2, 0:C]))
                settled()
                step(dve.tensor_scalar(mv[:, 0:1], st6[:, 0, 1:2], st6[:, 0, 4:5], 0.5, ALU.add, ALU.mult))
                variance(step, settled, st6[:, 0, :], KEYS * KEYS * EPS, var[:, 0:1], var)
                settled()
                rsqrt(step, settled, var[:, 0:1], mv[:, 1:2], 1)
                settled()
                step(dve.tensor_scalar(red_hat[:, :], ps[:, 2, 0:C], mv[:, 0:1], mv[:, 1:2], ALU.subtract, ALU.mult))
                assert n == RED_HAT
                if between:
                    between()
                for i, j in enumerate((1, 3)):
                    dve.wait_ge(pe_front, g * PF + 4 + i)
                    step(dve.tensor_copy(qk[:, :, j:HEADS:4, :],
                                         ps[:, j, :].rearrange("p (m h w) -> p m h w", m=2, h=2)))
                assert n == DF

            tail_n = 0

            def tail_step(ins):
                nonlocal tail_n
                tail_n += 1
                ins.then_inc(dve_tail, 1)

            def tail_local(g, slot):
                nonlocal tail_n
                tail_n = 0
                dve.wait_ge(act_tail, g * AT + 4)
                tail_step(dve.scalar_tensor_tensor(out=lo_t[:, :, :], in0=red_sum[:, slot, :, :], scalar=1.0 / KEYS,
                                                   in1=lo_part[:, :, :], op0=ALU.mult, op1=ALU.add))

            def tail_stats(g):
                dve.wait_ge(group_kept, g + 1)
                tail_step(dve.bn_stats(st6[:, 1, :], lo_all[:, bass.ds(g, 1), :]))
                settled = lambda: dve.wait_ge(dve_tail, g * DT + tail_n)
                settled()
                variance(tail_step, settled, st6[:, 1, :], EPS, lo_var[:, bass.ds(g, 1)], var[:, 8:16])
                dve.wait_ge(pe_tail, g * PT + 4)
                dve.wait_ge(patch_out, g * 16 + 16)
                tail_step(dve.tensor_tensor(patch[:, :], ps[:, 7, 0:C], rows["mod_b"][:, :], ALU.add))
                assert tail_n == PATCHED

                tail_step(dve.tensor_copy(gs_all[:, bass.ds(g, 1), :], ps[:, 7, C:C + HEADS]))
                assert tail_n == DT

            def body(g, slot, tail=True, nxt=True):
                n = 0

                def step(ins):
                    nonlocal n
                    n += 1
                    ins.then_inc(dve_main, 1)

                def settled():
                    dve.wait_ge(dve_main, g * DM + n)

                def sums(i):
                    if nxt:
                        window_sums(g + 1, 1 - slot, i)

                made_at = {}

                def mask(q):
                    dve.wait_ge(pe_main, g * PM + 1 + q)
                    a = HEADS * len(QUADS[q])
                    step(dve.tensor_tensor(masked[0:TT, q % 2, 0:a, :],
                                           ps[0:TT, 4 + q % 2, 0:a * TW].rearrange("p (a w) -> p a w", w=TW),
                                           own_window[0:TT, :].unsqueeze(1).broadcast_to([TT, a, TW]), ALU.mult))
                    made_at[q] = n

                def reduce(q):
                    dve.wait_ge(dve_main, g * DM + made_at[q])
                    a = HEADS * len(QUADS[q])
                    step(dve.tensor_reduce(score[0:TT, 4 * q:4 * q + len(QUADS[q]), :], masked[0:TT, q % 2, 0:a, :],
                                           AX_X, ALU.add))

                for t in range(NTT):
                    if t % 2 == 0:
                        dve.wait_ge(tok_moved, g * (NTT // 2) + t // 2 + 1)
                    step(dve.bn_stats(stats[0:TT, t, :], tok[0:TT, t, :]))
                    if tail and t == 1:
                        tail_local(g - 1, 1 - slot)
                    if t == 3:
                        mask(0)
                    if t == 4:
                        reduce(0)
                    if t == 7:
                        mask(1)
                    if t == 8:
                        reduce(1)
                settled()
                s = stats[0:TT, :, :]
                v0, v1, v2 = (tok_var[0:TT, i, :] for i in range(3))
                step(dve.tensor_tensor(v0, s[:, :, 1], s[:, :, 4], ALU.subtract))
                step(dve.tensor_tensor(v1, s[:, :, 2], s[:, :, 5], ALU.add))
                mask(2)
                dve.wait_ge(dve_main, g * DM + made_at[2] - 1)
                step(dve.scalar_tensor_tensor(out=v2, in0=v0, scalar=C / 4, in1=v0, op0=ALU.mult, op1=ALU.mult))
                settled()
                reduce(2)
                step(dve.tensor_tensor(v0, v1, v2, ALU.add))
                settled()
                step(dve.tensor_scalar(v1, v0, 1.0 / C, EPS, ALU.mult, ALU.add))
                settled()
                rsqrt(step, settled, v1, rstd[0:TT, :], NTT)
                settled()
                by_rstd = rstd[0:TT, :].unsqueeze(2).broadcast_to([TT, NTT, HEADS])
                step(dve.tensor_tensor(score[0:TT, :, :], score[0:TT, :, :], by_rstd, ALU.mult))
                assert n == SCORED, (n, SCORED)
                sums(0)
                sums(1)
                dve.wait_ge(pe_main, g * PM + 4)
                sp_ = ps[0:TH, 6, 0:TT].rearrange("p (w k) -> p w k", k=KEYS)
                top, total = soft_max[0:TH, :], soft_sum[0:TH, :]
                per_window = top.unsqueeze(2).broadcast_to([TH, TW, KEYS])
                step(dve.tensor_reduce(top, sp_, AX_X, ALU.max))
                settled()
                step(dve.tensor_tensor(soft[0:TH, :, :], sp_, per_window, ALU.subtract))
                assert n == SUBTRACTED, n
                sums(2)
                dve.wait_ge(act_main, g * AM + 1)
                step(dve.tensor_reduce(total, soft[0:TH, :, :], AX_X, ALU.add))
                settled()
                step(dve.reciprocal(top, total))
                settled()
                step(dve.tensor_tensor(soft[0:TH, :, :], soft[0:TH, :, :], per_window, ALU.mult))
                assert n == SOFTMAXED, n
                sums(3)
                dve.wait_ge(pe_main, g * PM + 5)
                step(dve.tensor_tensor(attn[0:TT, :, :], ps[0:TT, 7, 0:TH].rearrange("p (t h) -> p t h", h=HEADS),
                                       by_rstd, ALU.mult))
                settled()
                step(dve.tensor_tensor(spread[0:TT, :, :],
                                       attn[0:TT, :, :].rearrange("p t h -> p (t h)").unsqueeze(2)
                                       .broadcast_to([TT, TH, TW]),
                                       own_window[0:TT, :].unsqueeze(1).broadcast_to([TT, TH, TW]), ALU.mult))
                assert n == DM, n
                sums(4)
                sums(5)
                last_stats = (lambda: tail_stats(g - 1)) if tail else None
                if nxt:
                    front(g + 1, last_stats)
                elif tail:
                    last_stats()

            for i in range(2 * NB):
                window_sums(0, 0, i)
            front(0)
            body(0, 0, tail=False)
            with dve.Fori(0, NG // 2 - 1) as r:
                body(2 * r + 1, 1)
                body(2 * r + 2, 0)
            body(NG - 1, 1, nxt=False)
            tail_local(NG - 1, 1)
            tail_stats(NG - 1)

            dve.wait_ge(dve_tail, NG * DT)
            top = soft_max[:, 0:GI]
            rsqrt(first, first_settled, lo_var[:, :], lo_rstd[:, :], NG)
            dve.wait_ge(pre_v, made)
            by_lo = lo_rstd[:, :].unsqueeze(2).broadcast_to([P, NG, HEADS])
            first(dve.tensor_tensor(gs_all[:, :, :], gs_all[:, :, :], by_lo, ALU.mult))
            dve.wait_ge(pre, 10)
            gsp = ps[:, 0, 0:P].rearrange("p (b w) -> p b w", w=WIN)
            first(dve.tensor_reduce(top, gsp, AX_X, ALU.max))
            dve.wait_ge(pre_v, made)
            gsm = s_mat[:, 0:P].rearrange("p (b w) -> p b w", w=WIN)
            first(dve.tensor_tensor(gsm, gsp, top.unsqueeze(2).broadcast_to([P, GI, WIN]), ALU.subtract))
            dve.wait_ge(cls_exp, 1)
            first(dve.tensor_reduce(soft_sum[:, 0:GI], gsm, AX_X, ALU.add))
            dve.wait_ge(pre_v, made)
            first(dve.reciprocal(top, soft_sum[:, 0:GI]))
            dve.wait_ge(pre_v, made)
            first(dve.tensor_tensor(gsm, gsm, top.unsqueeze(2).broadcast_to([P, GI, WIN]), ALU.mult))
            dve.wait_ge(pre, 11)
            first(dve.tensor_tensor(gs_all[:, :, :], ps[:, 0, P:2 * P].rearrange("p (g h) -> p g h", g=NG), by_lo,
                                    ALU.mult))
            dve.wait_ge(pre_v, made)
            first(dve.tensor_tensor(cls_spread, gs_all[:, :, :].rearrange("p g h -> p (g h)").unsqueeze(2)
                                    .broadcast_to([P, NG * HEADS, GI]),
                                    own_image[:, :].unsqueeze(1).broadcast_to([P, NG * HEADS, GI]), ALU.mult))
            assert made == CLASS_V + 8
            for k in (1, 3):
                dve.wait_ge(pre, 12 + k)
                cls_ctx_move(dve.tensor_copy, k)
            dve.wait_ge(pre, 17)
            dve.wait_ge(patch_out, 16 + 16 * NG)
            first(dve.tensor_tensor(patch[:, :], ps[:, 6, 0:C], rows["class_emb"][:, :], ALU.add))

            n2 = 0

            def step(ins):
                nonlocal n2
                n2 += 1
                ins.then_inc(p2v, 1)

            def settled():
                dve.wait_ge(p2v, n2)

            def normal_all(i):
                for lot in range(4) if i == 0 else (4,):
                    tiles = range(H_LOTS[lot], H_LOTS[lot + 1]) if i == 0 else range(NT)
                    if i == 0:
                        dve.wait_ge(h_in[lot], 16 * len(tiles))
                    for t in tiles:
                        if i == 1:
                            dve.wait_ge(added, t + 1)
                        step(dve.bn_stats(stat6[0:R, t, :], h_rows[0:R, t, :]))
                    settled()
                    for t in tiles:
                        step(dve.bn_aggr(row_mv[0:R, t, :], stat6[0:R, t, :]))
                    settled()
                    lo, hi = tiles[0], tiles[-1] + 1
                    step(dve.tensor_scalar(row_var[0:R, lo:hi], row_mv[0:R, lo:hi, 1], EPS, None, ALU.add))
                    settled()
                    rsqrt(step, settled, row_var[0:R, lo:hi], gcol[0:R, lo:hi], hi - lo)
                    settled()
                    for t in tiles:
                        dve.tensor_scalar(n_rows[0:R, t, :], h_rows[0:R, t, :], row_mv[0:R, t, 0:1],
                                          gcol[0:R, t:t + 1], ALU.subtract, ALU.mult).then_inc(rows_normal, 1)

            dve.wait_ge(pad_zero, 1)
            normal_all(0)

            def mask_max(t):
                b = t % 2
                dve.wait_ge(sums_done, t + 1)
                if t >= 2:
                    dve.wait_ge(mixed, t - 1)
                dve.tensor_tensor(s_two[0:R, b, :], ps[0:R, 2 + b, 0:R], neg_mask[0:R, :], ALU.add)\
                    .then_inc(sums_masked, 1)
                dve.wait_ge(sums_masked, t + 1)
                dve.tensor_reduce(soft2[0:R, b, 0:1], s_two[0:R, b, :], AX_X, ALU.max, negate=True)\
                    .then_inc(max_found, 1)

            def add_mixed(t):
                dve.wait_ge(mixed, t + 1)
                dve.tensor_tensor(h_rows[0:R, t, :], h_rows[0:R, t, :], ps[0:R, 4 + t % 2, 0:C], ALU.add)\
                    .then_inc(added, 1)

            mask_max(0)
            for t in range(NT):
                b = t % 2
                if t >= 1:
                    add_mixed(t - 1)
                if t + 1 < NT:
                    mask_max(t + 1)
                dve.wait_ge(exped, t + 1)
                dve.reciprocal(soft2[0:R, b, 2:3], soft2[0:R, b, 1:2]).then_inc(inverted, 1)
                dve.wait_ge(inverted, t + 1)
                dve.tensor_scalar(s_two[0:R, b, :], s_two[0:R, b, :], soft2[0:R, b, 2:3], None, ALU.mult)\
                    .then_inc(weighted, 1)
            add_mixed(NT - 1)
            normal_all(1)
            assert n2 == LN2_DONE, n2
            dve.wait_ge(logits_moved, 1)
            lg = logit[0:R, :, :]

            def wide(col):
                return col.unsqueeze(2).broadcast_to([R, NT, E])

            step(dve.tensor_reduce(gcol[0:R, :], lg, AX_X, ALU.max))
            settled()
            step(dve.tensor_tensor(gt1[0:R, :, :], lg, wide(gcol[0:R, :]), ALU.subtract))
            assert n2 == GATE_MAX
            dve.wait_ge(gate_exp, 1)
            step(dve.tensor_reduce(gcol[0:R, :], gt1[0:R, :, :], AX_X, ALU.add))
            settled()
            step(dve.reciprocal(gcol[0:R, :], gcol[0:R, :]))
            settled()
            step(dve.tensor_tensor(lg, gt1[0:R, :, :], wide(gcol[0:R, :]), ALU.mult))
            settled()
            step(dve.tensor_copy(gt1[0:R, :, :], lg))
            settled()
            rw = rank_w[0:R, :].unsqueeze(1).broadcast_to([R, NT, E])
            for k in range(2):
                step(dve.tensor_reduce(gcol[0:R, :], gt1[0:R, :, :], AX_X, ALU.max))
                settled()
                step(dve.tensor_tensor(gt2[0:R, :, :], gt1[0:R, :, :], wide(gcol[0:R, :]), ALU.is_equal))
                settled()
                step(dve.tensor_tensor(gt2[0:R, :, :], gt2[0:R, :, :], rw, ALU.mult))
                settled()
                step(dve.tensor_reduce(gcol[0:R, :], gt2[0:R, :, :], AX_X, ALU.max))
                settled()
                step(dve.tensor_tensor(hot[0:R, k, :, :], gt2[0:R, :, :], wide(gcol[0:R, :]), ALU.is_equal))
                settled()
                if k == 0:
                    step(dve.scalar_tensor_tensor(out=gt1[0:R, :, :], in0=hot[0:R, 0, :, :], scalar=-2.0,
                                                  in1=gt1[0:R, :, :], op0=ALU.mult, op1=ALU.add))
                    settled()
            assert n2 == HOT_DONE, (n2, HOT_DONE)
            dve.wait_ge(ranked, 1)
            r1 = ps[0:R, 4, 0:NT * E].rearrange("p (t e) -> p t e", t=NT)
            r2 = ps[0:R, 5, 0:NT * E].rearrange("p (t e) -> p t e", t=NT)
            tk = take[0:R, :, :].rearrange("p (t e) s -> p t e s", t=NT)
            gi = give[0:R, :, :].rearrange("p (t e) s -> p t e s", t=NT)
            for s in range(2):
                step(dve.scalar_tensor_tensor(out=gt1[0:R, :, :], in0=r1, scalar=float(s), in1=hot[0:R, 0, :, :],
                                              op0=ALU.is_equal, op1=ALU.mult))
                step(dve.scalar_tensor_tensor(out=gt2[0:R, :, :], in0=r2, scalar=float(s), in1=hot[0:R, 1, :, :],
                                              op0=ALU.is_equal, op1=ALU.mult))
                settled()
                step(dve.tensor_tensor(tk[:, :, :, s], gt1[0:R, :, :], gt2[0:R, :, :], ALU.add))
                settled()
            by_seq = own_seq[0:R, :].unsqueeze(1).unsqueeze(3).broadcast_to([R, E, TI, CAP])

            def per_slot(dst, src, t, made_sem):
                dve.tensor_tensor(dst[0:R, t % 2, :, :, :],
                                  src[0:R, E * t:E * t + E, :].unsqueeze(2).broadcast_to([R, E, TI, CAP]),
                                  by_seq, ALU.mult).then_inc(made_sem, 1)

            for t in range(NT):
                if t >= 2:
                    dve.wait_ge(disp_done, t - 1)
                per_slot(disp, take, t, disp_made)
            step(dve.tensor_tensor(gi[:, :, :, 0], tk[:, :, :, 0], lg, ALU.mult))
            step(dve.tensor_tensor(gt3[0:R, :, :], hot[0:R, 0, :, :], hot[0:R, 1, :, :], ALU.add))
            settled()
            step(dve.tensor_tensor(gt2[0:R, :, :], gt3[0:R, :, :], lg, ALU.mult))
            settled()
            step(dve.tensor_tensor(gi[:, :, :, 1], gt2[0:R, :, :], gi[:, :, :, 0], ALU.subtract))
            settled()
            for e in range(E):
                b = e % 2
                dve.wait_ge(silu_done, e + 1)
                if e >= 2:
                    dve.wait_ge(down_done, e - 1)
                dve.tensor_tensor(hid[:, b, 1, :], hid[:, b, 0, :], ps[:, 2 * b + 1, 0:SLOTS], ALU.mult)\
                    .then_inc(hid_done, 1)

            def comb_move(t):
                b = t % 2
                dve.wait_ge(outs_turned, t + 1)
                if t >= 2:
                    dve.wait_ge(y_done, t - 1)
                dve.tensor_copy(comb_t[0:EH, b, :, :],
                                ps[0:EH, 2 + b, 0:C].rearrange("p (k r) -> p k r", k=2)[:, :, 0:R])\
                    .then_inc(comb_moved, 1)

            per_slot(comb, give, 0, comb_made)
            per_slot(comb, give, 1, comb_made)
            comb_move(0)
            for t in range(NT):
                b = t % 2
                if t + 2 < NT:
                    dve.wait_ge(outs_turned, t + 1)
                    per_slot(comb, give, t + 2, comb_made)
                if t + 1 < NT:
                    comb_move(t + 1)
                dve.wait_ge(y_done, t + 1)
                if t >= 2:
                    dve.wait_ge(out_sem[b], 16 * (t // 2))
                dve.tensor_tensor(y_rows[0:R, b, :], ps[0:R, 4 + b, 0:C], h_rows[0:R, t, :], ALU.add)\
                    .then_inc(y_made, 1)


def kernel(**inputs):
    import numpy as _np
    import concourse.bacc as _bacc
    from concourse.bass_utils import run_bass_kernel_spmd as _run

    v = {n: _np.asarray(x) for n, x in inputs.items()}
    pad = KFULL * P + KPAD - PIX
    x = v["x"].reshape(NG, GI, CH, SIDE, CS, PS, SIDE, CS, PS).transpose(0, 2, 5, 8, 1, 3, 6, 4, 7)
    x = _np.concatenate([x.reshape(NG, PIX, GT), _np.zeros((NG, pad, GT), _np.float32)], axis=1)
    conv_w = v["L0_tok_conv_w"].reshape(C, PIX).T
    conv_w = _np.concatenate([conv_w, _np.zeros((pad, C), _np.float32)], axis=0)
    arrays = {"x": x, "conv_w": _np.ascontiguousarray(conv_w), "cls_tok": v["cls_tok"]}
    for n in ("class_emb", "la_ln_q_g", "la_ln_q_b", "la_wq", "la_ln_kv_g", "la_ln_kv_b", "la_wkv", "la_proj_w",
              "la_proj_b", "ga_ln_q_g", "ga_ln_q_b", "ga_wq", "ga_ln_kv_g", "ga_ln_kv_b", "ga_wkv", "ga_proj_w",
              "ga_proj_b", "mod_w", "mod_b"):
        arrays[n] = v["L0_tok_" + n]
    for n in ("w_router", "w_fc", "w_gate", "w_proj"):
        arrays[n] = v["L0_ffn_" + n]
    arrays["cols"] = _np.stack([v["L0_tok_" + n].reshape(2, P) for n in COLS]).transpose(2, 0, 1)
    arrays = {n: _np.ascontiguousarray(x) for n, x in arrays.items()}
    nc = _bacc.Bacc("TRN2", target_bir_lowering=False, num_devices=1)
    aps = {n: nc.dram_tensor("in_" + n, x.shape, F32, kind="ExternalInput").ap() for n, x in arrays.items()}
    out = nc.dram_tensor("out_rows", (IMGS * TOK, C), F32, kind="ExternalOutput").ap()
    tower(nc, aps, out)
    r = _run(nc, [{"in_" + n: x for n, x in arrays.items()}], core_ids=[0])
    return r.results[0]["out_rows"].reshape(IMGS, TOK, C)
```

```python
from contextlib import ExitStack

import concourse.bass as bass
from concourse import mybir

F32 = mybir.dt.float32
I32 = mybir.dt.int32
F32R = mybir.dt.float32r
ALU = mybir.AluOpType
ACT = mybir.ActivationFunctionType
AX_X = mybir.AxisListType.X

P = 128
EPS = 1e-5
IMGS, CH, IMG, PS, CS = 128, 3, 168, 14, 3
C = 256
HEADS, DH = 8, 32
SIDE = IMG // PS // CS
WIN = SIDE * SIDE
KEYS = CS * CS
PIX = CH * PS * PS
KFULL = PIX // P
KREST = PIX - KFULL * P
KPAD = -(-KREST // 16) * 16
GI = 8
NG = IMGS // GI
GW = GI * WIN
GT = GW * KEYS
BLKS = ((0, 44 * KEYS), (44 * KEYS, 42 * KEYS), (86 * KEYS, 42 * KEYS))
NB = len(BLKS)
NPR = 3 * (KFULL + 1)
AHEAD, CONV_C, CONV_D = 12, 34, 20
TW = P // KEYS
TT = TW * KEYS
NTT = -(-GW // TW)
W0 = [min(TW * t, GW - TW) for t in range(NTT)]
TH = NTT * HEADS
QUADS = [range(i, min(i + 4, NTT)) for i in range(0, NTT, 4)]
SCALE = C ** -0.5

TOK = WIN + 2
TI = 7
R = TI * TOK
NT = -(-IMGS // TI)
LASTR = (IMGS - (NT - 1) * TI) * TOK
E, CAP, H = 16, 2, 128
TS = TI * CAP
SLOTS = NT * TS
ES = E * TS
EARLY_NORMALS = 14
LO_SLOTS = 8
EH = ES // 2
NEG = 1e30
COLS = ("la_ln_q_g", "la_ln_q_b", "la_ln_kv_g", "la_ln_kv_b", "la_proj_b",
        "ga_ln_q_g", "ga_ln_q_b", "ga_ln_kv_g", "ga_ln_kv_b", "class_emb")


def tower(nc, a, out):
    with ExitStack() as ctx:
        stack = ctx

        def sb(name, shape, dt=F32):
            return stack.enter_context(nc.sbuf_tensor(name, shape, dt))

        def sem(name):
            return ctx.enter_context(nc.semaphore(name))

        scratch = nc.dram_tensor("tower_rows", [IMGS * TOK, C], F32, kind="Internal").ap()
        scratch_img = scratch.rearrange("(b t) c -> b t c", t=TOK)

        ident = sb("ident", [P, P])
        mean_ones = sb("mean_ones", [P, P])
        own_window = sb("own_window", [P, TW])
        own_image = sb("own_image", [P, GI])
        earlier_r = sb("earlier_r", [P, R], F32R)
        same_seq_r = sb("same_seq_r", [P, R], F32R)
        own_seq = sb("own_seq", [P, TI])
        same_seq = sb("same_seq", [P, R])
        earlier = sb("earlier", [P, R])
        neg_mask = sb("neg_mask", [P, R])
        rank_w = sb("rank_w", [P, E])
        proj = sb("proj", [P, 2, C])
        gproj = sb("gproj", [P, 2, C])
        router = sb("router", [P, 2, E])
        col_vectors = sb("col_vectors", [P, len(COLS), 2])
        cols = {n: col_vectors[:, i, :] for i, n in enumerate(COLS)}
        KEPT_ROWS = ("mod_b", "class_emb", "ga_proj_b")
        rows = {n: sb("row_" + n, [P, C]) for n in KEPT_ROWS}
        gv_bias = sb("gv_bias", [P, 2])
        small = sb("small", [P, 16])
        newton = sb("newton", [P, 2, 32])
        var = sb("var", [P, 32])
        lo_all = sb("lo_all", [P, NG, C])
        gwv_fold = sb("gwv_fold", [P, 2, C])
        gs_all = sb("gs_all", [P, NG, HEADS])
        lo_var = sb("lo_var", [P, NG])
        lo_rstd = sb("lo_rstd", [P, NG])
        s_mat = sb("s_mat", [P, P])
        agg_t = sb("agg_t", [P, 2, P])
        patch = sb("patch", [P, C])
        soft_max = sb("soft_max", [P, TW])
        soft_sum = sb("soft_sum", [P, TW])

        stack = ctx.enter_context(ExitStack())
        phase1 = stack
        x_raw = sb("x_raw", [P, KFULL + 1, GT])
        x_hi = sb("x_hi", [P, KFULL + 1, GT], F32R)
        x_lo = sb("x_lo", [P, KFULL + 1, GT], F32R)
        w_hi = sb("w_hi", [P, KFULL + 1, C], F32R)
        w_lo = sb("w_lo", [P, KFULL + 1, C], F32R)
        wq = sb("wq", [P, 2, C])
        mod_w = sb("mod_w", [P, 2, C + HEADS])
        wk_fold = sb("wk_fold", [P, 2, C])
        wv_fold = sb("wv_fold", [P, 2, C])
        v_bias = sb("v_bias", [P, 2])
        pe_t = sb("pe_t", [P, 2, 2, GT])
        red_sum = sb("red_sum", [P, 2, 2, P])
        red_hat = sb("red_hat", [P, C])
        red_hat_t = sb("red_hat_t", [P, 2, P])
        q_t = sb("q_t", [P, 2, P])
        stats = sb("stats", [P, NTT, 6])
        tok_var = sb("tok_var", [P, 3, NTT])
        rstd = sb("rstd", [P, NTT])
        st6 = sb("st6", [P, 2, 6])
        mv = sb("mv", [P, 2])
        score = sb("score", [P, NTT, HEADS])
        soft = sb("soft", [P, TW, KEYS])
        attn = sb("attn", [P, NTT, HEADS])
        lo_t = sb("lo_t", [P, 2, P])
        lo_part = sb("lo_part", [P, 2, P])
        with ExitStack() as stack:
            w_conv = sb("w_conv", [P, KFULL + 1, C])
            wkv = sb("wkv", [P, 2, 2 * C])
            gwkv = sb("gwkv", [P, 2, 2 * C])
            gwq = sb("gwq", [P, 2, C])
            gwk_fold = sb("gwk_fold", [P, 2, C])
            gq_block = sb("gq_block", [P, 2, HEADS])
            SETUP_ROWS = ("la_ln_kv_g", "ga_ln_kv_g")
            rows.update({n: sb("row_" + n, [P, C]) for n in SETUP_ROWS})
        stack = phase1
        tok = sb("tok", [P, NTT, C])
        qk = sb("qk", [P, 2, HEADS, P])
        ctxv = sb("ctxv", [P, 2, HEADS, P])
        masked = sb("masked", [P, 2, 4 * HEADS, TW])
        spread = sb("spread", [P, TH, TW])
        phase1.close()

        stack = ctx
        w_gate = sb("w_gate", [P, E, 2, H])
        w_fc = sb("w_fc", [P, E, 2, H])
        w_proj = sb("w_proj", [P, E, C])
        h_rows = sb("h_rows", [P, NT, C])
        xb = sb("xb", [P, 2, NT, E, TS])
        n_rows = sb("n_rows", [P, NT, C])
        n_hi = sb("n_hi", [P, NT, C], F32R)
        logit = sb("logit", [P, NT, E])
        hot = sb("hot", [P, 2, NT, E], F32R)
        gt1 = sb("gt1", [P, NT, E])
        gt2 = sb("gt2", [P, NT, E])
        gt3 = sb("gt3", [P, NT, E])
        take = sb("take", [P, NT * E, CAP])
        give = sb("give", [P, NT * E, CAP])
        gate_col = sb("gate_col", [P, NT])
        stat6 = sb("stat6", [P, NT, 6])
        row_mv = sb("row_mv", [P, NT, 2])
        row_var = sb("row_var", [P, NT])
        row_rstd = sb("row_rstd", [P, NT])
        row_shift = sb("row_shift", [P, NT])
        s_slots = sb("s_slots", [P, 4, R])
        soft2 = sb("soft2", [P, 4, 3])
        nt_t = sb("nt_t", [P, 3, 2, R])
        h_t = sb("h_t", [P, 3, 2, R])
        disp = sb("disp", [P, 2, E, TI, CAP], F32R)
        comb = sb("comb", [P, 2, E, TI, CAP])
        comb_t = sb("comb_t", [P, 2, 2, R])
        with ExitStack() as stack:
            n_lo = sb("n_lo", [P, LO_SLOTS, C], F32R)
        stack = ctx
        o_rows = sb("o_rows", [P, 2, 2, C])
        hid = sb("hid", [P, 2, 2, SLOTS])
        y_rows = sb("y_rows", [P, 2, C])

        ps = ctx.enter_context(nc.psum_tensor("ps", [P, 8, 512], F32))

        masks_made = sem("masks_made")
        conv_w_in = sem("conv_w_in")
        weights_in = sem("weights_in")
        w_split = sem("w_split")
        raw_in = [sem(f"raw_in_{j}") for j in range(NB)]
        hi_made = sem("hi_made")
        lo_made = sem("lo_made")
        conv_done = sem("conv_done")
        conv_moved = sem("conv_moved")
        pe_front, pe_main, pe_tail = sem("pe_front"), sem("pe_main"), sem("pe_tail")
        act_front, act_main, act_tail = sem("act_front"), sem("act_main"), sem("act_tail")
        dve_front, dve_main, dve_tail = sem("dve_front"), sem("dve_main"), sem("dve_tail")
        red_made = sem("red_made")
        tok_turned, tok_moved = sem("tok_turned"), sem("tok_moved")
        ctx_done, ctx_moved = sem("ctx_done"), sem("ctx_moved")
        group_kept = sem("group_kept")
        patch_out = sem("patch_out")
        cls_out = sem("cls_out")
        pre, pre_v = sem("pre"), sem("pre_v")
        cls_exp, cls_moved, cls_gathered = sem("cls_exp"), sem("cls_moved"), sem("cls_gathered")
        ffn_in, pad_zero = sem("ffn_in"), sem("pad_zero")
        h_in = [sem(f"h_in_{i}") for i in range(3)]
        rows_normal = [sem("even_rows_normal"), sem("odd_rows_normal")]
        n_made, hi_rounded, rows_split = sem("n_made"), sem("hi_rounded"), sem("rows_split")
        h_turned, h_turned_moved = sem("h_turned"), sem("h_turned_moved")
        rows_turned, rows_moved = sem("rows_turned"), sem("rows_moved")
        sums_done, sums_masked, max_found = sem("sums_done"), sem("sums_masked"), sem("max_found")
        exped, inverted, weighted = sem("exped"), sem("inverted"), sem("weighted")
        mixed, added = sem("mixed"), sem("added")
        logits_done = sem("logits_done")
        p2v = sem("p2v")
        gate_exp, ranked = sem("gate_exp"), sem("ranked")
        disp_made, disp_done, disp_moved = sem("disp_made"), sem("disp_done"), sem("disp_moved")
        up_done, silu_done, hid_done = sem("up_done"), sem("silu_done"), sem("hid_done")
        down_done, down_moved = sem("down_done"), sem("down_moved")
        comb_made, outs_turned, comb_moved = sem("comb_made"), sem("outs_turned"), sem("comb_moved")
        outs_moved, y_done, y_made = sem("outs_moved"), sem("y_done"), sem("y_made")
        out_sem = [sem("out_even"), sem("out_odd")]

        block = ctx.enter_context(nc.Block())

        def mpn(ap):
            return ap.rearrange("(m p) n -> p m n", p=P)

        LASTW = GW - W0[-2]
        CTX_FILLS = ((0, 0), (0, 1), (0, 2), (1, 0), (1, 1))
        NR = 11
        PF, PM, PT = 5, 5, 4
        AF, AM, AT = 5, 1, 4
        RED_HAT = 1 + 5 + NR + 1
        DF = RED_HAT + 2
        QUAD0 = 4 + 1
        SCORED = NTT + 2 * len(QUADS) + 5 + NR + 1
        SUBTRACTED = SCORED + 2
        SOFTMAXED = SUBTRACTED + 3
        SPREAD = SOFTMAXED + 2
        DM = SPREAD
        LOCAL, PATCHED = 1, 7
        DT = 8
        W_SPLIT = 4
        SQ_DONE = 4 + 2 * 5 + 2 + 5 + 3
        QHAT_DONE = SQ_DONE + 1 + NR + 3
        GQ_DONE = QHAT_DONE + HEADS
        SETUP_V = GQ_DONE + 2
        CLASS_V = SETUP_V + NR
        MASKS = 8 + 8 + 2 + E
        W_DMAS = 8 + len(KEPT_ROWS) + len(SETUP_ROWS) + 1
        LOTS = (range(0, 4), range(4, 12), range(12, NT))
        EARLY_TILES = (NG - 1) * GI // TI
        LATE = 5
        LOT_KNOWN = [sum(2 * len(lot) + 2 + NR for lot in LOTS[:i + 1]) for i in range(len(LOTS))]
        LOT_KNOWN[-1] += 2 * (LATE - 3)
        LN2_DONE = 2 * NT + len(LOTS) * (2 + NR) + 2 * NT + 2 + NR
        GATE_MAX = LN2_DONE + 3
        HOT_DONE = GATE_MAX + 3 + 5 + 1 + 5

        def lot_of(t):
            return next(i for i, lot in enumerate(LOTS) if t in lot)

        def cls_ctx_move(move, k, *args):
            move(ctxv[:, k // 2, :, 64 * (k % 2):64 * (k % 2) + 64].rearrange("p h (g b) -> p g h b", b=GI),
                 ps[:, 1 + k, :].rearrange("p (g h b) -> p g h b", g=NG // 2, h=HEADS), *args).then_inc(cls_moved, 1)

        cls_spread = spread[:, :, :].rearrange("p a w -> p (a w)")[:, 0:NG * HEADS * GI]\
            .rearrange("p (a b) -> p a b", b=GI)

        @block.sync
        def _(sp):
            def load(g, j):
                c, n = BLKS[j]
                if not isinstance(g, int) or g >= 1:
                    sp.wait_ge(lo_made, g * NB - NB + j + 1)
                src = a["x"][g] if isinstance(g, int) else a["x"][bass.ds(g, 1)].rearrange("o k t -> (o k) t")
                sp.dma_start(x_raw[:, 0:KFULL, c:c + n],
                             src[0:KFULL * P, c:c + n].rearrange("(k p) t -> p k t", p=P)).then_inc(raw_in[j], 16)
                sp.dma_start(x_raw[0:KPAD, KFULL, c:c + n], src[KFULL * P:KFULL * P + KPAD, c:c + n])\
                    .then_inc(raw_in[j], 16)

            def store(g):
                sp.wait_ge(dve_tail, g * DT + PATCHED)
                sp.dma_start(scratch_img[bass.ds(g * GI, GI), 1:1 + WIN, :], patch[:, :]).then_inc(patch_out, 16)

            def rows_back(t):
                n = R if t < NT - 1 else LASTR
                sp.dma_start(h_rows[0:n, t, :], scratch[t * R:t * R + n, :]).then_inc(h_in[lot_of(t)], 16)

            for j in range(NB):
                load(0, j)
            sp.dma_start(scratch_img[:, 0:TOK:TOK - 1, :], a["cls_tok"].broadcast_to([IMGS, 2, C]))\
                .then_inc(patch_out, 16)
            for g in (1, 2, 3):
                for j in range(NB):
                    load(g, j)
            with sp.Fori(1, NG - 3) as g:
                store(g - 1)
                for j in range(NB):
                    load(g + 3, j)
            for g in range(NG - 3, NG + 1):
                store(g - 1)
                if g == NG - 1:
                    sp.wait_ge(conv_done, NG * 2 * NB)
                    sp.wait_ge(patch_out, 16 * NG)
                    for t in range(EARLY_TILES):
                        rows_back(t)
            sp.wait_ge(patch_out, 16 + 16 * NG)
            sp.wait_ge(pad_zero, 1)
            for t in range(EARLY_TILES, NT):
                rows_back(t)
            for i, lot in enumerate(LOTS):
                sp.wait_ge(h_in[i], 16 * len(lot))
            sp.wait_ge(pre_v, CLASS_V + 9)
            sp.dma_start(scratch_img[:, 1 + WIN, :], patch[:, :]).then_inc(cls_out, 16)
            sp.wait_ge(cls_out, 16)
            for i, lot in enumerate(LOTS):
                full = [t for t in lot if t < NT - 1 or LASTR == R]
                n = len(full) * TI
                sp.dma_start(h_rows[TOK - 1:R:TOK, full[0]:full[-1] + 1, :],
                             scratch_img[full[0] * TI:full[0] * TI + n, TOK - 1, :].rearrange("(t b) c -> b t c", b=TI))\
                    .then_inc(h_in[i], 16)
                if len(full) < len(lot):
                    sp.dma_start(h_rows[TOK - 1:LASTR:TOK, NT - 1, :], scratch_img[(NT - 1) * TI:IMGS, TOK - 1, :])\
                        .then_inc(h_in[i], 16)
            sp.dma_start(w_gate[:, :, :, :], a["w_gate"].rearrange("e (m p) h -> p e m h", p=P)).then_inc(ffn_in, 16)
            sp.dma_start(w_fc[:, :, :, :], a["w_fc"].rearrange("e (m p) h -> p e m h", p=P)).then_inc(ffn_in, 16)
            sp.dma_start(w_proj[:, :, :], a["w_proj"].rearrange("e h c -> h e c")).then_inc(ffn_in, 16)
            for t in range(NT):
                sp.wait_ge(y_made, t + 1)
                n = R if t < NT - 1 else LASTR
                sp.dma_start(out[t * R:t * R + n, :], y_rows[0:n, t % 2, :]).then_inc(out_sem[t % 2], 16)
            sp.wait_ge(out_sem[0], 16 * ((NT + 1) // 2))
            sp.wait_ge(out_sem[1], 16 * (NT // 2))

        @block.gpsimd
        def _(pool):
            pool.memset(ident[:, :], 0.0).then_inc(masks_made, 1)
            pool.memset(mean_ones[:, :], 1.0 / C).then_inc(masks_made, 1)
            for m in (own_window, own_image, own_seq, same_seq):
                pool.memset(m[:, :], 1.0).then_inc(masks_made, 1)
            pool.memset(gq_block[:, :, :], 0.0).then_inc(masks_made, 1)
            n = 7
            pool.wait_ge(masks_made, n)
            pool.affine_select(out=ident[:, :], in_=ident[:, :], compare_op=ALU.not_equal, fill=1.0, base=0,
                               pattern=[[-1, P]], channel_multiplier=1).then_inc(masks_made, 1)
            n += 1
            for m, size, pat in ((own_window, KEYS, [[-KEYS, TW]]), (own_image, WIN, [[-WIN, GI]]),
                                 (own_seq, TOK, [[-TOK, TI]]), (same_seq, TOK, [[-TOK, TI], [0, TOK]])):
                up = [[-s, k] for s, k in pat]
                pool.affine_select(out=m[:, :], in_=m[:, :], compare_op=ALU.is_ge, fill=0.0, base=0,
                                   pattern=pat, channel_multiplier=1).then_inc(masks_made, 1)
                n += 1
                pool.wait_ge(masks_made, n)
                pool.affine_select(out=m[:, :], in_=m[:, :], compare_op=ALU.is_ge, fill=0.0, base=size - 1,
                                   pattern=up, channel_multiplier=-1).then_inc(masks_made, 1)
                n += 1
                pool.wait_ge(masks_made, n)
            pool.affine_select(out=earlier[:, :], in_=same_seq[:, :], compare_op=ALU.is_ge, fill=0.0, base=-1,
                               pattern=[[1, R]], channel_multiplier=-1).then_inc(masks_made, 1)
            pool.tensor_scalar(neg_mask[:, :], same_seq[:, :], -1.0, NEG, ALU.add, ALU.mult).then_inc(masks_made, 1)
            for e in range(E):
                pool.memset(rank_w[:, e:e + 1], float(E - e)).then_inc(masks_made, 1)
            n += 2 + E
            assert n == MASKS

            def split_lo(g, j):
                c, n = BLKS[j]
                pool.wait_ge(hi_made, g * NB + j + 1)
                pool.tensor_tensor(x_lo[:, 0:KFULL, c:c + n], x_raw[:, 0:KFULL, c:c + n],
                                   x_hi[:, 0:KFULL, c:c + n].bitcast(F32), ALU.subtract)
                pool.tensor_tensor(x_lo[0:KREST, KFULL, c:c + n], x_raw[0:KREST, KFULL, c:c + n],
                                   x_hi[0:KREST, KFULL, c:c + n].bitcast(F32), ALU.subtract).then_inc(lo_made, 1)

            for j in range(NB):
                split_lo(0, j)
            with pool.Fori(1, NG) as g:
                for j in range(NB):
                    split_lo(g, j)
            pool.wait_ge(conv_done, NG * 2 * NB)
            pool.memset(h_rows[:, NT - 1, :], 0.0).then_inc(pad_zero, 1)
            for t in range(0, NT, 2):
                pool.wait_ge(p2v, LOT_KNOWN[lot_of(t)])
                pool.tensor_scalar(n_rows[0:R, t, :], h_rows[0:R, t, :], row_mv[0:R, t, 0:1], row_rstd[0:R, t:t + 1],
                                   ALU.subtract, ALU.mult).then_inc(rows_normal[0], 1)
            for t in range(NT):
                pool.wait_ge(hi_rounded, t + 1)
                if t >= LO_SLOTS:
                    pool.wait_ge(disp_done, t - LO_SLOTS + 1)
                pool.tensor_tensor(n_lo[0:R, t % LO_SLOTS, :], n_rows[0:R, t, :], n_hi[0:R, t, :].bitcast(F32),
                                   ALU.subtract).then_inc(rows_split, 1)

        @block.scalar
        def _(act):
            act.dma_start(w_conv[:, 0:KFULL, :], a["conv_w"][0:KFULL * P, :].rearrange("(k p) c -> p k c", p=P))\
                .then_inc(conv_w_in, 16)
            act.dma_start(w_conv[0:KPAD, KFULL, :], a["conv_w"][KFULL * P:KFULL * P + KPAD, :])\
                .then_inc(conv_w_in, 16)

            def split_hi(g, j):
                c, n = BLKS[j]
                act.wait_ge(raw_in[j], g * 32 + 32)
                if not isinstance(g, int) or g >= 1:
                    act.wait_ge(conv_done, g * 2 * NB - 2 * NB + 2 * j + 2)
                act.activation(x_hi[:, 0:KFULL, c:c + n], x_raw[:, 0:KFULL, c:c + n], ACT.Copy)
                act.activation(x_hi[0:KREST, KFULL, c:c + n], x_raw[0:KREST, KFULL, c:c + n], ACT.Copy)\
                    .then_inc(hi_made, 1)

            def conv_move(g, slot, n):
                c, w = BLKS[n // 2]
                act.wait_ge(conv_done, g * 2 * NB + n + 1)
                act.activation(pe_t[:, slot, n % 2, c:c + w], ps[:, n % 2, 0:w], ACT.Copy).then_inc(conv_moved, 1)

            def front(g):
                act.wait_ge(pe_front, g * PF + 2)
                for m in range(2):
                    act.activation(red_hat_t[:, m, :], ps[:, 3, P * m:P * m + P], ACT.Identity,
                                   bias=cols["la_ln_q_b"][:, m:m + 1], scale=cols["la_ln_q_g"][:, m:m + 1])\
                        .then_inc(act_front, 1)
                act.wait_ge(pe_front, g * PF + 3)
                act.activation(q_t[:, :, :], ps[:, 2, 0:C], ACT.Copy).then_inc(act_front, 1)

            def front_keys(g):
                for i, j in enumerate((0, 2)):
                    act.wait_ge(pe_front, g * PF + 4 + i)
                    act.activation(qk[:, :, j:HEADS:4, :],
                                   ps[:, 2 + j, :].rearrange("p (m h w) -> p m h w", m=2, h=2), ACT.Copy)\
                        .then_inc(act_front, 1)

            def tail_a(g):
                act.wait_ge(pe_tail, g * PT + 2)
                for m in range(2):
                    act.activation(lo_part[:, m, :], ps[:, 7, P * m:P * m + P], ACT.Identity,
                                   bias=cols["la_proj_b"][:, m:m + 1]).then_inc(act_tail, 1)

            def tail_b(g):
                act.wait_ge(pe_tail, g * PT + 3)
                act.activation(lo_all[:, bass.ds(g, 1), :], ps[:, 6, C:2 * C], ACT.Copy).then_inc(group_kept, 1)

            def body(g, slot, tail=True, nxt=True, split=True):
                if tail:
                    tail_a(g - 1)
                for k in range(NTT // 2):
                    act.wait_ge(tok_turned, g * (NTT // 2) + k + 1)
                    act.activation(tok[0:TT, 2 * k:2 * k + 2, :], ps[0:TT, 2 + k % 2, :], ACT.Copy)\
                        .then_inc(tok_moved, 1)
                if nxt:
                    conv_move(g + 1, 1 - slot, 0)
                    if tail:
                        split_hi(g + 1, 2)
                    conv_move(g + 1, 1 - slot, 1)
                    if split:
                        split_hi(g + 2, 0)
                    conv_move(g + 1, 1 - slot, 2)
                act.wait_ge(dve_main, g * DM + SUBTRACTED)
                act.activation(soft[0:TH, :, :], soft[0:TH, :, :], ACT.Exp).then_inc(act_main, 1)
                if nxt:
                    conv_move(g + 1, 1 - slot, 3)
                    if split:
                        split_hi(g + 2, 1)
                    conv_move(g + 1, 1 - slot, 4)
                    conv_move(g + 1, 1 - slot, 5)
                for k, (m, q) in enumerate(CTX_FILLS):
                    act.wait_ge(ctx_done, g * len(CTX_FILLS) + k + 1)
                    n = len(QUADS[q]) * HEADS * TW
                    if q < 2:
                        w = W0[4 * q]
                        act.activation(ctxv[:, m, :, w:w + 4 * TW].rearrange("p h (t w) -> p t h w", w=TW),
                                       ps[:, 4 + k % 2, 0:n].rearrange("p (t h w) -> p t h w", t=4, h=HEADS), ACT.Copy)\
                            .then_inc(ctx_moved, 1)
                    else:
                        act.activation(ctxv[:, :, :, W0[-2]:GW],
                                       ps[:, 4 + k % 2, 0:2 * HEADS * LASTW]
                                       .rearrange("p (m h w) -> p m h w", m=2, h=HEADS), ACT.Copy).then_inc(ctx_moved, 1)
                if tail:
                    tail_b(g - 1)
                if nxt:
                    front(g + 1)
                act.wait_ge(pe_tail, g * PT + 1)
                for m in range(2):
                    act.activation(agg_t[:, m, :], ps[:, 6, P * m:P * m + P], ACT.Identity,
                                   bias=v_bias[:, m:m + 1]).then_inc(act_tail, 1)
                if nxt:
                    front_keys(g + 1)

            split_hi(0, 0)
            for t, n in ((wkv, "la_wkv"), (wq, "la_wq"), (gwkv, "ga_wkv"), (gwq, "ga_wq"), (proj, "la_proj_w"),
                         (gproj, "ga_proj_w"), (mod_w, "mod_w"), (router, "w_router")):
                act.dma_start(t[:, :, 0:a[n].shape[1]], mpn(a[n])).then_inc(weights_in, 16)
            for n in KEPT_ROWS + SETUP_ROWS:
                act.dma_start(rows[n][:, :], a[n].rearrange("(o c) -> o c", o=1).broadcast_to([P, C]))\
                    .then_inc(weights_in, 16)
            act.dma_start(col_vectors[:, :, :], a["cols"]).then_inc(weights_in, 16)
            for j in range(1, NB):
                split_hi(0, j)
            for j in range(NB):
                conv_move(0, 0, 2 * j)
                conv_move(0, 0, 2 * j + 1)
                split_hi(1, j)
            front(0)
            front_keys(0)
            body(0, 0, tail=False)
            with act.Fori(0, NG // 2 - 2) as r:
                body(2 * r + 1, 1)
                body(2 * r + 2, 0)
            body(NG - 3, 1)
            body(NG - 2, 0, split=False)
            body(NG - 1, 1, nxt=False)
            tail_a(NG - 1)
            tail_b(NG - 1)

            act.wait_ge(pre_v, CLASS_V + 3)
            act.activation(s_mat[:, 0:P], s_mat[:, 0:P], ACT.Exp).then_inc(cls_exp, 1)
            for k in (0, 2):
                act.wait_ge(pre, 12 + k)
                cls_ctx_move(act.activation, k, ACT.Copy)
            act.wait_ge(pre, 16)
            for m in range(2):
                act.activation(agg_t[:, m, :], ps[:, 5, P * m:P * m + P], ACT.Identity,
                               bias=gv_bias[:, m:m + 1]).then_inc(cls_gathered, 1)

            def rows_move(t):
                act.wait_ge(rows_turned, t + 1)
                act.activation(nt_t[:, t % 3, :, :], ps[:, t % 2, 0:2 * R], ACT.Copy).then_inc(rows_moved, 1)

            def normal(t):
                act.activation(n_rows[0:R, t, :], h_rows[0:R, t, :], ACT.Identity, bias=row_shift[0:R, t:t + 1],
                               scale=row_rstd[0:R, t:t + 1]).then_inc(rows_normal[1], 1)

            for t in (1, 3):
                act.wait_ge(p2v, LOT_KNOWN[lot_of(t)])
                normal(t)
            for t in range(3):
                rows_move(t)
            for i in range(NT + 5):
                if i % 2 == 0 and i + 5 < NT:
                    act.wait_ge(p2v, LOT_KNOWN[lot_of(i + 5)])
                    normal(i + 5)
                if i + 3 < NT:
                    rows_move(i + 3)
                if 5 <= i:
                    t = i - 5
                    act.wait_ge(h_turned, t + 1)
                    act.activation(h_t[:, t % 3, :, :], ps[:, 6, 0:2 * R], ACT.Copy).then_inc(h_turned_moved, 1)
                if 1 <= i <= NT:
                    t = i - 1
                    act.wait_ge(inverted, t + 1)
                    act.activation(s_slots[0:R, t % 4, :], s_slots[0:R, t % 4, :], ACT.Copy,
                                   scale=soft2[0:R, t % 4, 2:3]).then_inc(weighted, 1)
                if i < NT:
                    act.wait_ge(max_found, i + 1)
                    act.activation(s_slots[0:R, i % 4, :], s_slots[0:R, i % 4, :], ACT.Exp,
                                   bias=soft2[0:R, i % 4, 0:1], accum_out=soft2[0:R, i % 4, 1:2]).then_inc(exped, 1)
            act.wait_ge(p2v, GATE_MAX)
            act.activation(gt1[0:R, :, :], gt1[0:R, :, :], ACT.Exp).then_inc(gate_exp, 1)
            def normal2(t):
                if t < NT:
                    act.activation(n_rows[0:R, t, :], h_rows[0:R, t, :], ACT.Identity, bias=row_shift[0:R, t:t + 1],
                                   scale=row_rstd[0:R, t:t + 1]).then_inc(n_made, 1)
                if 1 <= t <= NT:
                    act.wait_ge(n_made, t)
                    act.activation(n_hi[0:R, t - 1, :], n_rows[0:R, t - 1, :], ACT.Copy).then_inc(hi_rounded, 1)

            for t in range(EARLY_NORMALS):
                normal2(t)
            for t in range(NT):
                act.wait_ge(disp_done, t + 1)
                act.activation(xb[:, :, t, :, :], ps[:, t % 4, 0:2 * ES].rearrange("p (m e s) -> p m e s", m=2, e=E),
                               ACT.Copy).then_inc(disp_moved, 1)
                normal2(t + EARLY_NORMALS)

            def silu(e):
                act.wait_ge(up_done, e + 1)
                if e >= 2:
                    act.wait_ge(hid_done, e - 1)
                act.activation(hid[:, e % 2, 0, :], ps[:, 2 * (e % 2), 0:SLOTS], ACT.Silu).then_inc(silu_done, 1)

            silu(0)
            for e in range(E):
                if e + 1 < E:
                    silu(e + 1)
                act.wait_ge(down_done, e + 1)
                for m in range(2):
                    act.activation(xb[:, m, :, e, :],
                                   ps[:, 4 + 2 * (e % 2) + m, 0:SLOTS].rearrange("p (t s) -> p t s", t=NT), ACT.Copy)\
                        .then_inc(down_moved, 1)
            for t in range(NT):
                act.wait_ge(outs_turned, t + 1)
                if t >= 2:
                    act.wait_ge(y_done, t - 1)
                act.activation(o_rows[0:EH, t % 2, :, :], ps[0:EH, t % 2, :], ACT.Copy).then_inc(outs_moved, 1)

        @block.tensor
        def _(pe):
            def conv_part(g, first, count):
                for u in range(first, first + count):
                    n, i = u // NPR, u % NPR
                    m, j, k, part = n % 2, n // 2, i // 3, i % 3
                    c, w = BLKS[j]
                    if u % (2 * NPR) == 0:
                        pe.wait_ge(lo_made, g * NB + j + 1)
                    if i == 0 and (n >= 2 or not isinstance(g, int) or g >= 1):
                        pe.wait_ge(conv_moved, g * 2 * NB + n - 1)
                    kk = P if k < KFULL else KREST
                    wt, xt = ((w_hi, x_hi), (w_hi, x_lo), (w_lo, x_hi))[part]
                    mm = pe.matmul(ps[:, m, 0:w], wt[0:kk, k, P * m:P * m + P], xt[0:kk, k, c:c + w],
                                   start=(i == 0), stop=(i == NPR - 1))
                    if i == NPR - 1:
                        mm.then_inc(conv_done, 1)

            def turn_window_sums(g, slot):
                pe.wait_ge(red_made, g * 2 * NB + 2 * NB)
                if not isinstance(g, int) or g >= 1:
                    pe.wait_ge(tok_moved, g * (NTT // 2))
                for m in range(2):
                    last = pe.transpose(ps[:, 2, P * m:P * m + P], red_sum[:, slot, m, :], ident[:, :])
                last.then_inc(pe_front, 1)

            def turn_red_hat(g):
                pe.wait_ge(dve_front, g * DF + RED_HAT)
                for m in range(2):
                    last = pe.transpose(ps[:, 3, P * m:P * m + P], red_hat[:, P * m:P * m + P], ident[:, :])
                last.then_inc(pe_front, 1)

            def queries(g):
                pe.wait_ge(act_front, g * AF + 2)
                for hc in range(2):
                    for m in range(2):
                        last = pe.matmul(ps[:, 2, P * hc:P * hc + P], wq[:, m, P * hc:P * hc + P], red_hat_t[:, m, :],
                                         start=(m == 0), stop=(m == 1))
                last.then_inc(pe_front, 1)

            def query_keys(g):
                pe.wait_ge(act_front, g * AF + 3)
                pe.wait_ge(conv_moved, g * 2 * NB + 2 * NB)
                for pair in ((0, 1), (2, 3)):
                    for m in range(2):
                        for hc in range(2):
                            for j in pair:
                                o = P * (2 * m + hc)
                                last = pe.matmul(ps[:, 2 + j, o:o + P], wk_fold[32 * j:32 * j + 32, hc, P * m:P * m + P],
                                                 q_t[32 * j:32 * j + 32, hc, :], start=True, stop=True)
                    last.then_inc(pe_front, 1)

            def gather_values(g, hc):
                if hc == 0:
                    pe.wait_ge(ctx_moved, g * len(CTX_FILLS) + len(CTX_FILLS))
                    if not isinstance(g, int) or g >= 1:
                        pe.wait_ge(group_kept, g)
                for j in range(4):
                    h = 4 * hc + j
                    for m in range(2):
                        last = pe.matmul(ps[32 * j:32 * j + 32, 6, P * hc:P * hc + P],
                                         wv_fold[:, m, DH * h:DH * h + DH], ctxv[:, m, h, :],
                                         start=(m == 0), stop=(m == 1))
                if hc == 1:
                    last.then_inc(pe_tail, 1)

            def project(g):
                pe.wait_ge(act_tail, g * AT + 2)
                for m in range(2):
                    for hc in range(2):
                        last = pe.matmul(ps[:, 7, P * m:P * m + P], proj[:, hc, P * m:P * m + P], agg_t[:, hc, :],
                                         start=(hc == 0), stop=(hc == 1))
                last.then_inc(pe_tail, 1)

            def local_out(g):
                pe.wait_ge(dve_tail, g * DT + LOCAL)
                for m in range(2):
                    last = pe.transpose(ps[:, 6, C + P * m:C + P * m + P], lo_t[:, m, :], ident[:, :])
                last.then_inc(pe_tail, 1)
                for m in range(2):
                    last = pe.matmul(ps[:, 7, 0:C + HEADS], lo_t[:, m, :], mod_w[:, m, :], start=(m == 0), stop=(m == 1))
                last.then_inc(pe_tail, 1)

            def body(g, slot, tail=True, nxt=True, ahead=True):
                at = AHEAD

                def conv(n):
                    nonlocal at
                    if nxt:
                        conv_part(g + 1, at, n)
                        at += n

                if tail:
                    project(g - 1)
                pe.wait_ge(act_front, g * AF + AF)
                pe.wait_ge(dve_front, g * DF + DF)
                for k in range(NTT // 2):
                    if k >= 2:
                        pe.wait_ge(tok_moved, g * (NTT // 2) + k - 1)
                    for t in (2 * k, 2 * k + 1):
                        for m in range(2):
                            o = C * (t % 2) + P * m
                            last = pe.transpose(ps[0:TT, 2 + k % 2, o:o + P],
                                                pe_t[:, slot, m, KEYS * W0[t]:KEYS * W0[t] + TT], ident[:, :])
                    last.then_inc(tok_turned, 1)
                    if k == 4:
                        pe.wait_ge(dve_main, g * DM + QUAD0)
                    for t in (2 * k, 2 * k + 1):
                        for m in range(2):
                            o = HEADS * TW * (t % 4)
                            last = pe.matmul(ps[0:TT, 4 + (t // 4) % 2, o:o + HEADS * TW],
                                             pe_t[:, slot, m, KEYS * W0[t]:KEYS * W0[t] + TT],
                                             qk[:, m, :, W0[t]:W0[t] + TW], start=(m == 0), stop=(m == 1))
                    if k in (1, 3, 4):
                        last.then_inc(pe_main, 1)
                    conv(2)
                conv(CONV_C)
                pe.wait_ge(dve_main, g * DM + SCORED)
                pe.transpose(ps[0:TH, 6, 0:TT], score[0:TT, :, :], ident[0:TT, 0:TT]).then_inc(pe_main, 1)
                conv(CONV_D)
                pe.wait_ge(dve_main, g * DM + SOFTMAXED)
                if tail:
                    pe.wait_ge(dve_tail, g * DT - DT + LOCAL)
                pe.transpose(ps[0:TT, 7, 0:TH], soft[0:TH, :, :], ident[0:TH, 0:TH]).then_inc(pe_main, 1)
                conv(2 * NB * NPR - AHEAD - CONV_D - CONV_C - NTT)
                assert not nxt or at == 2 * NB * NPR, at
                pe.wait_ge(dve_main, g * DM + SPREAD)
                pe.wait_ge(tok_moved, g * (NTT // 2) + NTT // 2)

                def weigh(dst, m, t, windows):
                    return pe.matmul(dst, tok[0:TT, t, P * m:P * m + P],
                                     spread[0:TT, HEADS * t:HEADS * t + HEADS, 0:windows], start=True, stop=True)

                for k, (m, q) in enumerate(CTX_FILLS):
                    if k >= 2:
                        pe.wait_ge(ctx_moved, g * len(CTX_FILLS) + k - 1)
                    bank = ps[:, 4 + k % 2, :]
                    if q < 2:
                        for t in QUADS[q]:
                            o = HEADS * TW * (t % 4)
                            last = weigh(bank[:, o:o + HEADS * TW], m, t, TW)
                    else:
                        w = W0[-1] - W0[-2]
                        for m in range(2):
                            o = HEADS * LASTW * m
                            both = bank[:, o:o + HEADS * LASTW].rearrange("p (h w) -> p h w", h=HEADS)
                            weigh(both[:, :, 0:w], m, NTT - 2, w)
                            last = weigh(both[:, :, w:LASTW], m, NTT - 1, TW)
                    last.then_inc(ctx_done, 1)
                    if nxt and k == 1:
                        turn_window_sums(g + 1, 1 - slot)
                if tail:
                    local_out(g - 1)
                if nxt and ahead:
                    conv_part(g + 2, 0, AHEAD // 2)
                if nxt:
                    turn_red_hat(g + 1)
                gather_values(g, 0)
                gather_values(g, 1)
                if nxt:
                    queries(g + 1)
                    if ahead:
                        conv_part(g + 2, AHEAD // 2, AHEAD - AHEAD // 2)
                if nxt:
                    query_keys(g + 1)
                if tail:
                    pe.wait_ge(dve_tail, g * DT)

            pe.wait_ge(w_split, W_SPLIT)
            pe.wait_ge(masks_made, MASKS)
            conv_part(0, 0, 30)
            pe.wait_ge(weights_in, 16 * W_DMAS)
            for b, w in enumerate((wkv, gwkv)):
                for hc in range(2):
                    for m in range(2):
                        last = pe.transpose(ps[:, 6 + b, C * hc + P * m:C * hc + P * m + P], w[:, m, P * hc:P * hc + P],
                                            ident[:, :])
                last.then_inc(pre, 1)
            pe.wait_ge(pre_v, 4)
            for b, w in enumerate((wv_fold, gwv_fold)):
                for m in range(2):
                    last = pe.matmul(ps[:, 2 + b, 0:C], mean_ones[:, :], w[:, m, :], start=(m == 0), stop=(m == 1))
                last.then_inc(pre, 1)
            for i, (w, bc) in enumerate(((wkv, "la_ln_kv_b"), (gwkv, "ga_ln_kv_b"))):
                for hc in range(2):
                    for m in range(2):
                        last = pe.matmul(ps[:, 4, 2 * i + hc:2 * i + hc + 1], w[:, m, C + P * hc:C + P * hc + P],
                                         cols[bc][:, m:m + 1], start=(m == 0), stop=(m == 1))
            for m in range(2):
                last = pe.matmul(ps[:, 4, E:2 * E], mean_ones[:, :], router[:, m, :], start=(m == 0), stop=(m == 1))
            last.then_inc(pre, 1)
            for m in range(2):
                last = pe.matmul(ps[:, 5, 0:1], mean_ones[:, :], cols["class_emb"][:, m:m + 1],
                                 start=(m == 0), stop=(m == 1))
            last.then_inc(pre, 1)
            conv_part(0, 30, 35)
            pe.wait_ge(pre_v, SQ_DONE)
            for m in range(2):
                last = pe.matmul(ps[:, 5, 1:2], mean_ones[:, :], small[:, 4 + m:5 + m], start=(m == 0), stop=(m == 1))
            last.then_inc(pre, 1)
            conv_part(0, 65, 15)
            pe.wait_ge(pre_v, QHAT_DONE)
            for hc in range(2):
                for m in range(2):
                    last = pe.matmul(ps[:, 5, 2 + hc:3 + hc], gwq[:, m, P * hc:P * hc + P], small[:, 8 + m:9 + m],
                                     start=(m == 0), stop=(m == 1))
            last.then_inc(pre, 1)
            conv_part(0, 80, 10)
            pe.wait_ge(pre_v, GQ_DONE)
            for m in range(2):
                for hc in range(2):
                    last = pe.matmul(ps[:, 5, 8 + 8 * m:16 + 8 * m], gwk_fold[:, hc, P * m:P * m + P],
                                     gq_block[:, hc, :], start=(hc == 0), stop=(hc == 1))
            last.then_inc(pre, 1)
            pe.wait_ge(pre_v, SETUP_V)
            turn_window_sums(0, 0)
            turn_red_hat(0)
            queries(0)
            conv_part(1, 0, AHEAD)
            query_keys(0)
            body(0, 0, tail=False)
            with pe.Fori(0, NG // 2 - 2) as r:
                body(2 * r + 1, 1)
                body(2 * r + 2, 0)
            body(NG - 3, 1)
            body(NG - 2, 0, ahead=False)
            body(NG - 1, 1, nxt=False)
            project(NG - 1)
            local_out(NG - 1)

            pe.wait_ge(pre_v, CLASS_V + 1)
            pe.transpose(ps[:, 0, 0:P], gs_all[:, :, :], ident[:, :]).then_inc(pre, 1)
            pe.wait_ge(pre_v, CLASS_V + 6)
            pe.transpose(ps[:, 0, P:2 * P], s_mat[:, 0:P], ident[:, :]).then_inc(pre, 1)
            pe.wait_ge(pre_v, CLASS_V + 8)
            pe.wait_ge(group_kept, NG)
            for k in range(4):
                m = k // 2
                for i in range(NG // 2):
                    g = NG // 2 * (k % 2) + i
                    last = pe.matmul(ps[:, 1 + k, HEADS * GI * i:HEADS * GI * i + HEADS * GI],
                                     lo_all[:, g, P * m:P * m + P], cls_spread[:, HEADS * g:HEADS * g + HEADS, :],
                                     start=True, stop=True)
                last.then_inc(pre, 1)
            pe.wait_ge(cls_moved, 4)
            for hc in range(2):
                for j in range(4):
                    h = 4 * hc + j
                    for m in range(2):
                        last = pe.matmul(ps[32 * j:32 * j + 32, 5, P * hc:P * hc + P],
                                         gwv_fold[:, m, DH * h:DH * h + DH], ctxv[:, m, h, :],
                                         start=(m == 0), stop=(m == 1))
            last.then_inc(pre, 1)
            pe.wait_ge(cls_gathered, 2)
            for hc in range(2):
                last = pe.matmul(ps[:, 6, 0:C], agg_t[:, hc, :], gproj[:, hc, :], start=(hc == 0), stop=(hc == 1))
            last.then_inc(pre, 1)

            def turn_rows(t):
                pe.wait_ge(rows_normal[t % 2], t // 2 + 1)
                if t >= 2:
                    pe.wait_ge(rows_moved, t - 1)
                for m in range(2):
                    last = pe.transpose(ps[:, t % 2, R * m:R * m + R], n_rows[0:R, t, P * m:P * m + P],
                                        ident[0:R, 0:R])
                last.then_inc(rows_turned, 1)

            def products(t):
                pe.wait_ge(rows_moved, t + 1)
                if t >= 2:
                    pe.wait_ge(sums_masked, t - 1)
                for m in range(2):
                    last = pe.matmul(ps[0:R, 2 + t % 2, 0:R], nt_t[:, t % 3, m, :], nt_t[:, t % 3, m, :],
                                     start=(m == 0), stop=(m == 1))
                last.then_inc(sums_done, 1)

            def mix(t):
                pe.wait_ge(weighted, t + 1)
                if t >= 2:
                    pe.wait_ge(added, t - 1)
                pe.matmul(ps[0:R, 4 + t % 2, 0:C], s_slots[0:R, t % 4, :], n_rows[0:R, t, :],
                          start=True, stop=True).then_inc(mixed, 1)

            def turn_h(t):
                pe.wait_ge(added, t + 1)
                if t >= 1:
                    pe.wait_ge(h_turned_moved, t)
                for m in range(2):
                    last = pe.transpose(ps[:, 6, R * m:R * m + R], h_rows[0:R, t, P * m:P * m + P], ident[0:R, 0:R])
                last.then_inc(h_turned, 1)

            def route(t):
                pe.wait_ge(h_turned_moved, t + 1)
                for m in range(2):
                    last = pe.matmul(ps[0:R, 7, E * t:E * t + E], h_t[:, t % 3, m, :], router[:, m, :],
                                     start=(m == 0), stop=(m == 1))
                last.then_inc(logits_done, 1)

            for t in range(3):
                turn_rows(t)
            for t in range(2):
                products(t)
            for i in range(NT + 6):
                if i + 3 < NT:
                    turn_rows(i + 3)
                if i + 2 < NT:
                    products(i + 2)
                for stage, ago in ((mix, 2), (turn_h, 4), (route, 6)):
                    if 0 <= i - ago < NT:
                        stage(i - ago)
            pe.wait_ge(p2v, HOT_DONE)
            pe.matmul(ps[0:R, 4, 0:NT * E], earlier_r[0:R, :], hot[0:R, 0, :, :], start=True, stop=True)
            pe.matmul(ps[0:R, 5, 0:NT * E], same_seq_r[0:R, :], hot[0:R, 0, :, :], start=True, stop=False)
            pe.matmul(ps[0:R, 5, 0:NT * E], earlier_r[0:R, :], hot[0:R, 1, :, :], start=False, stop=True)\
                .then_inc(ranked, 1)
            for t in range(NT):
                pe.wait_ge(rows_split, t + 1)
                pe.wait_ge(disp_made, t + 1)
                if t >= 4:
                    pe.wait_ge(disp_moved, t - 3)
                for m in range(2):
                    for n, first_part in ((n_hi[0:R, t, P * m:P * m + P], True),
                                          (n_lo[0:R, t % LO_SLOTS, P * m:P * m + P], False)):
                        last = pe.matmul(ps[:, t % 4, ES * m:ES * m + ES], n, disp[0:R, t % 2, :, :, :],
                                         start=first_part, stop=not first_part)
                last.then_inc(disp_done, 1)

            def up(e):
                if e == 0:
                    pe.wait_ge(ffn_in, 48)
                    pe.wait_ge(disp_moved, NT)
                if e >= 2:
                    pe.wait_ge(hid_done, e - 1)
                for i, w in enumerate((w_gate, w_fc)):
                    for m in range(2):
                        last = pe.matmul(ps[:, 2 * (e % 2) + i, 0:SLOTS], w[:, e, m, :], xb[:, m, :, e, :],
                                         start=(m == 0), stop=(m == 1))
                last.then_inc(up_done, 1)

            up(0)
            for e in range(E):
                if e + 1 < E:
                    up(e + 1)
                pe.wait_ge(hid_done, e + 1)
                if e >= 2:
                    pe.wait_ge(down_moved, 2 * e - 2)
                for m in range(2):
                    last = pe.matmul(ps[:, 4 + 2 * (e % 2) + m, 0:SLOTS], w_proj[:, e, P * m:P * m + P],
                                     hid[:, e % 2, 1, :], start=True, stop=True)
                last.then_inc(down_done, 1)

            def turn_outs(t):
                if t == 0:
                    pe.wait_ge(down_moved, 2 * E)
                if t >= 2:
                    pe.wait_ge(outs_moved, t - 1)
                for half in range(2):
                    for m in range(2):
                        pe.transpose(ps[0:EH, t % 2, C * half + P * m:C * half + P * m + P],
                                     xb[:, m, t, 8 * half:8 * half + 8, :], ident[:, :])
                pe.wait_ge(comb_made, t + 1)
                if t >= 2:
                    pe.wait_ge(comb_moved, t - 1)
                for half in range(2):
                    last = pe.transpose(ps[0:EH, 2 + t % 2, P * half:P * half + R],
                                        comb[0:R, t % 2, 8 * half:8 * half + 8, :, :], ident[0:R, 0:R])
                last.then_inc(outs_turned, 1)

            turn_outs(0)
            for t in range(NT):
                if t + 1 < NT:
                    turn_outs(t + 1)
                pe.wait_ge(comb_moved, t + 1)
                pe.wait_ge(outs_moved, t + 1)
                if t >= 2:
                    pe.wait_ge(y_made, t - 1)
                for half in range(2):
                    last = pe.matmul(ps[0:R, 4 + t % 2, 0:C], comb_t[0:EH, t % 2, half, :],
                                     o_rows[0:EH, t % 2, half, :], start=(half == 0), stop=(half == 1))
                last.then_inc(y_done, 1)

        @block.vector
        def _(dve):
            def rsqrt(step, settled, v, y, n):
                p = v.shape[0]
                a, b = newton[0:p, 0, 0:n], newton[0:p, 1, 0:n]
                step(dve.tensor_scalar(a.bitcast(I32), v.bitcast(I32), 1, None, ALU.logical_shift_right))
                settled()
                step(dve.tensor_scalar(y.bitcast(I32), a.bitcast(I32), -1.0, float(0x5f3759df), ALU.mult, ALU.add))
                for _ in range(3):
                    settled()
                    step(dve.tensor_tensor(a, y, y, ALU.mult))
                    settled()
                    step(dve.scalar_tensor_tensor(out=b, in0=a, scalar=-0.5, in1=v, op0=ALU.mult, op1=ALU.mult))
                    settled()
                    step(dve.scalar_tensor_tensor(out=y, in0=b, scalar=1.5, in1=y, op0=ALU.add, op1=ALU.mult))

            made = 0

            def first(ins):
                nonlocal made
                made += 1
                ins.then_inc(pre_v, 1)

            def first_settled():
                dve.wait_ge(pre_v, made)

            def window_sums(g, slot, n):
                c, w = BLKS[n // 2]
                dve.wait_ge(conv_moved, g * 2 * NB + n + 1)
                dve.tensor_reduce(red_sum[:, slot, n % 2, c // KEYS:(c + w) // KEYS],
                                  pe_t[:, slot, n % 2, c:c + w].rearrange("p (w k) -> p w k", k=KEYS), AX_X, ALU.add)\
                    .then_inc(red_made, 1)

            dve.wait_ge(conv_w_in, 32)
            for kk, k0, k1 in ((P, 0, KFULL), (KREST, KFULL, KFULL + 1)):
                dve.tensor_copy(w_hi[0:kk, k0:k1, :], w_conv[0:kk, k0:k1, :]).then_inc(w_split, 1)
            dve.wait_ge(w_split, 2)
            for kk, k0, k1 in ((P, 0, KFULL), (KREST, KFULL, KFULL + 1)):
                dve.tensor_tensor(w_lo[0:kk, k0:k1, :], w_conv[0:kk, k0:k1, :], w_hi[0:kk, k0:k1, :].bitcast(F32),
                                  ALU.subtract).then_inc(w_split, 1)
            dve.wait_ge(masks_made, MASKS)
            dve.wait_ge(weights_in, 16 * W_DMAS)
            for w, f, gn in ((wkv, wv_fold, "la_ln_kv_g"), (gwkv, gwv_fold, "ga_ln_kv_g")):
                for m in range(2):
                    first(dve.tensor_scalar(f[:, m, :], w[:, m, C:2 * C], cols[gn][:, m:m + 1], None, ALU.mult))
            for b, (f, gn) in enumerate(((wk_fold, "la_ln_kv_g"), (gwk_fold, "ga_ln_kv_g"))):
                dve.wait_ge(pre, b + 1)
                first(dve.tensor_tensor(f[:, :, :], ps[:, 6 + b, :].rearrange("p (h c) -> p h c", h=2),
                                        rows[gn][:, :].unsqueeze(1).broadcast_to([P, 2, C]), ALU.mult))
                dve.wait_ge(pre_v, made)
                first(dve.tensor_reduce(small[:, 0:2], f[:, :, :], AX_X, ALU.add))
                dve.wait_ge(pre_v, made)
                first(dve.tensor_scalar(small[:, 2:4], small[:, 0:2], -1.0 / C, None, ALU.mult))
                dve.wait_ge(pre_v, made)
                for hc in range(2):
                    first(dve.tensor_scalar(f[:, hc, :], f[:, hc, :], small[:, 2 + hc:3 + hc], SCALE,
                                            ALU.add, ALU.mult))
            for b, f in enumerate((wv_fold, gwv_fold)):
                dve.wait_ge(pre, 3 + b)
                first(dve.tensor_tensor(f[:, :, :], f[:, :, :],
                                        ps[:, 2 + b, 0:C].unsqueeze(1).broadcast_to([P, 2, C]), ALU.subtract))
            dve.wait_ge(pre, 5)
            first(dve.tensor_copy(v_bias[:, :], ps[:, 4, 0:2]))
            first(dve.tensor_copy(gv_bias[:, :], ps[:, 4, 2:4]))
            first(dve.tensor_copy(earlier_r[:, :], earlier[:, :]))
            first(dve.tensor_copy(same_seq_r[:, :], same_seq[:, :]))
            first(dve.tensor_tensor(router[:, :, :], router[:, :, :],
                                    ps[:, 4, E:2 * E].unsqueeze(1).broadcast_to([P, 2, E]), ALU.subtract))
            dve.wait_ge(pre, 6)
            dve.wait_ge(pre_v, made)
            first(dve.tensor_copy(small[:, 0:1], ps[:, 5, 0:1]))
            dve.wait_ge(pre_v, made)
            first(dve.tensor_scalar(small[:, 2:4], cols["class_emb"][:, :], small[:, 0:1], None, ALU.subtract))
            dve.wait_ge(pre_v, made)
            first(dve.tensor_tensor(small[:, 4:6], small[:, 2:4], small[:, 2:4], ALU.mult))
            assert made == SQ_DONE
            dve.wait_ge(pre, 7)
            first(dve.tensor_scalar(small[:, 12:13], ps[:, 5, 1:2], EPS, None, ALU.add))
            dve.wait_ge(pre_v, made)
            rsqrt(first, first_settled, small[:, 12:13], small[:, 6:7], 1)
            dve.wait_ge(pre_v, made)
            first(dve.tensor_scalar(small[:, 8:10], small[:, 2:4], small[:, 6:7], None, ALU.mult))
            dve.wait_ge(pre_v, made)
            first(dve.tensor_tensor(small[:, 10:12], small[:, 8:10], cols["ga_ln_q_g"][:, :], ALU.mult))
            dve.wait_ge(pre_v, made)
            first(dve.tensor_tensor(small[:, 8:10], small[:, 10:12], cols["ga_ln_q_b"][:, :], ALU.add))
            assert made == QHAT_DONE
            for i in range(4):
                window_sums(0, 0, i)
            dve.wait_ge(pre, 8)
            for h in range(HEADS):
                j, hc = h % 4, h // 4
                first(dve.tensor_copy(gq_block[32 * j:32 * j + 32, hc, h:h + 1],
                                      ps[32 * j:32 * j + 32, 5, 2 + hc:3 + hc]))
            assert made == GQ_DONE
            dve.wait_ge(pre, 9)
            first(dve.tensor_copy(mod_w[:, :, C:C + HEADS], ps[:, 5, 8:24].rearrange("p (m h) -> p m h", m=2)))
            dve.wait_ge(pre_v, made)
            first(dve.tensor_tensor(rows["class_emb"][:, :], rows["class_emb"][:, :], rows["ga_proj_b"][:, :], ALU.add))
            assert made == SETUP_V, made

            def variance(step, settled, st, eps, dst, v):
                step(dve.tensor_scalar(v[:, 1:2], st[:, 1:2], st[:, 4:5], None, ALU.subtract))
                step(dve.tensor_scalar(v[:, 2:3], st[:, 2:3], st[:, 5:6], 4.0 / C, ALU.add, ALU.mult))
                settled()
                step(dve.scalar_tensor_tensor(out=v[:, 3:4], in0=v[:, 1:2], scalar=v[:, 1:2], in1=v[:, 2:3],
                                              op0=ALU.mult, op1=ALU.add))
                settled()
                step(dve.tensor_scalar(dst, v[:, 3:4], 0.25, eps, ALU.mult, ALU.add))

            def front(g, between=None):
                n = 0

                def step(ins):
                    nonlocal n
                    n += 1
                    ins.then_inc(dve_front, 1)

                def settled():
                    dve.wait_ge(dve_front, g * DF + n)

                dve.wait_ge(pe_front, g * PF + 1)
                step(dve.bn_stats(st6[:, 0, :], ps[:, 2, 0:C]))
                settled()
                step(dve.tensor_scalar(mv[:, 0:1], st6[:, 0, 1:2], st6[:, 0, 4:5], 0.5, ALU.add, ALU.mult))
                variance(step, settled, st6[:, 0, :], KEYS * KEYS * EPS, var[:, 0:1], var)
                settled()
                rsqrt(step, settled, var[:, 0:1], mv[:, 1:2], 1)
                settled()
                step(dve.tensor_scalar(red_hat[:, :], ps[:, 2, 0:C], mv[:, 0:1], mv[:, 1:2], ALU.subtract, ALU.mult))
                assert n == RED_HAT
                if between:
                    between()
                for i, j in enumerate((1, 3)):
                    dve.wait_ge(pe_front, g * PF + 4 + i)
                    step(dve.tensor_copy(qk[:, :, j:HEADS:4, :],
                                         ps[:, 2 + j, :].rearrange("p (m h w) -> p m h w", m=2, h=2)))
                assert n == DF

            tail_n = 0

            def tail_step(ins):
                nonlocal tail_n
                tail_n += 1
                ins.then_inc(dve_tail, 1)

            def tail_local(g, slot):
                nonlocal tail_n
                tail_n = 0
                dve.wait_ge(act_tail, g * AT + 4)
                tail_step(dve.scalar_tensor_tensor(out=lo_t[:, :, :], in0=red_sum[:, slot, :, :], scalar=1.0 / KEYS,
                                                   in1=lo_part[:, :, :], op0=ALU.mult, op1=ALU.add))

            def tail_stats(g):
                dve.wait_ge(group_kept, g + 1)
                tail_step(dve.bn_stats(st6[:, 1, :], lo_all[:, bass.ds(g, 1), :]))
                settled = lambda: dve.wait_ge(dve_tail, g * DT + tail_n)
                settled()
                variance(tail_step, settled, st6[:, 1, :], EPS, lo_var[:, bass.ds(g, 1)], var[:, 8:16])
                dve.wait_ge(pe_tail, g * PT + 4)
                dve.wait_ge(patch_out, g * 16 + 16)
                tail_step(dve.tensor_tensor(patch[:, :], ps[:, 7, 0:C], rows["mod_b"][:, :], ALU.add))
                assert tail_n == PATCHED

                tail_step(dve.tensor_copy(gs_all[:, bass.ds(g, 1), :], ps[:, 7, C:C + HEADS]))
                assert tail_n == DT

            def body(g, slot, tail=True, nxt=True):
                n = 0

                def step(ins):
                    nonlocal n
                    n += 1
                    ins.then_inc(dve_main, 1)

                def settled():
                    dve.wait_ge(dve_main, g * DM + n)

                def sums(i):
                    if nxt:
                        window_sums(g + 1, 1 - slot, i)

                made_at = {}

                def mask(q):
                    dve.wait_ge(pe_main, g * PM + 1 + q)
                    a = HEADS * len(QUADS[q])
                    step(dve.tensor_tensor(masked[0:TT, q % 2, 0:a, :],
                                           ps[0:TT, 4 + q % 2, 0:a * TW].rearrange("p (a w) -> p a w", w=TW),
                                           own_window[0:TT, :].unsqueeze(1).broadcast_to([TT, a, TW]), ALU.mult))
                    made_at[q] = n

                def reduce(q):
                    dve.wait_ge(dve_main, g * DM + made_at[q])
                    a = HEADS * len(QUADS[q])
                    step(dve.tensor_reduce(score[0:TT, 4 * q:4 * q + len(QUADS[q]), :], masked[0:TT, q % 2, 0:a, :],
                                           AX_X, ALU.add))

                for t in range(NTT):
                    if t % 2 == 0:
                        dve.wait_ge(tok_moved, g * (NTT // 2) + t // 2 + 1)
                    step(dve.bn_stats(stats[0:TT, t, :], tok[0:TT, t, :]))
                    if tail and t == 1:
                        tail_local(g - 1, 1 - slot)
                    if t == 3:
                        mask(0)
                    if t == 4:
                        reduce(0)
                    if t == 7:
                        mask(1)
                    if t == 8:
                        reduce(1)
                settled()
                s = stats[0:TT, :, :]
                v0, v1, v2 = (tok_var[0:TT, i, :] for i in range(3))
                step(dve.tensor_tensor(v0, s[:, :, 1], s[:, :, 4], ALU.subtract))
                step(dve.tensor_tensor(v1, s[:, :, 2], s[:, :, 5], ALU.add))
                mask(2)
                dve.wait_ge(dve_main, g * DM + made_at[2] - 1)
                step(dve.scalar_tensor_tensor(out=v2, in0=v0, scalar=C / 4, in1=v0, op0=ALU.mult, op1=ALU.mult))
                settled()
                reduce(2)
                step(dve.tensor_tensor(v0, v1, v2, ALU.add))
                settled()
                step(dve.tensor_scalar(v1, v0, 1.0 / C, EPS, ALU.mult, ALU.add))
                settled()
                rsqrt(step, settled, v1, rstd[0:TT, :], NTT)
                settled()
                by_rstd = rstd[0:TT, :].unsqueeze(2).broadcast_to([TT, NTT, HEADS])
                step(dve.tensor_tensor(score[0:TT, :, :], score[0:TT, :, :], by_rstd, ALU.mult))
                assert n == SCORED, (n, SCORED)
                sums(0)
                sums(1)
                dve.wait_ge(pe_main, g * PM + 4)
                sp_ = ps[0:TH, 6, 0:TT].rearrange("p (w k) -> p w k", k=KEYS)
                top, total = soft_max[0:TH, :], soft_sum[0:TH, :]
                per_window = top.unsqueeze(2).broadcast_to([TH, TW, KEYS])
                step(dve.tensor_reduce(top, sp_, AX_X, ALU.max))
                settled()
                step(dve.tensor_tensor(soft[0:TH, :, :], sp_, per_window, ALU.subtract))
                assert n == SUBTRACTED, n
                sums(2)
                dve.wait_ge(act_main, g * AM + 1)
                step(dve.tensor_reduce(total, soft[0:TH, :, :], AX_X, ALU.add))
                settled()
                step(dve.reciprocal(top, total))
                settled()
                step(dve.tensor_tensor(soft[0:TH, :, :], soft[0:TH, :, :], per_window, ALU.mult))
                assert n == SOFTMAXED, n
                sums(3)
                dve.wait_ge(pe_main, g * PM + 5)
                step(dve.tensor_tensor(attn[0:TT, :, :], ps[0:TT, 7, 0:TH].rearrange("p (t h) -> p t h", h=HEADS),
                                       by_rstd, ALU.mult))
                settled()
                step(dve.tensor_tensor(spread[0:TT, :, :],
                                       attn[0:TT, :, :].rearrange("p t h -> p (t h)").unsqueeze(2)
                                       .broadcast_to([TT, TH, TW]),
                                       own_window[0:TT, :].unsqueeze(1).broadcast_to([TT, TH, TW]), ALU.mult))
                assert n == DM, n
                sums(4)
                sums(5)
                last_stats = (lambda: tail_stats(g - 1)) if tail else None
                if nxt:
                    front(g + 1, last_stats)
                elif tail:
                    last_stats()

            for i in range(4, 2 * NB):
                window_sums(0, 0, i)
            front(0)
            body(0, 0, tail=False)
            with dve.Fori(0, NG // 2 - 1) as r:
                body(2 * r + 1, 1)
                body(2 * r + 2, 0)
            body(NG - 1, 1, nxt=False)
            tail_local(NG - 1, 1)
            tail_stats(NG - 1)

            dve.wait_ge(dve_tail, NG * DT)
            top = soft_max[:, 0:GI]
            rsqrt(first, first_settled, lo_var[:, :], lo_rstd[:, :], NG)
            dve.wait_ge(pre_v, made)
            by_lo = lo_rstd[:, :].unsqueeze(2).broadcast_to([P, NG, HEADS])
            first(dve.tensor_tensor(gs_all[:, :, :], gs_all[:, :, :], by_lo, ALU.mult))
            dve.wait_ge(pre, 10)
            gsp = ps[:, 0, 0:P].rearrange("p (b w) -> p b w", w=WIN)
            first(dve.tensor_reduce(top, gsp, AX_X, ALU.max))
            dve.wait_ge(pre_v, made)
            gsm = s_mat[:, 0:P].rearrange("p (b w) -> p b w", w=WIN)
            first(dve.tensor_tensor(gsm, gsp, top.unsqueeze(2).broadcast_to([P, GI, WIN]), ALU.subtract))
            dve.wait_ge(cls_exp, 1)
            first(dve.tensor_reduce(soft_sum[:, 0:GI], gsm, AX_X, ALU.add))
            dve.wait_ge(pre_v, made)
            first(dve.reciprocal(top, soft_sum[:, 0:GI]))
            dve.wait_ge(pre_v, made)
            first(dve.tensor_tensor(gsm, gsm, top.unsqueeze(2).broadcast_to([P, GI, WIN]), ALU.mult))
            dve.wait_ge(pre, 11)
            first(dve.tensor_tensor(gs_all[:, :, :], ps[:, 0, P:2 * P].rearrange("p (g h) -> p g h", g=NG), by_lo,
                                    ALU.mult))
            dve.wait_ge(pre_v, made)
            first(dve.tensor_tensor(cls_spread, gs_all[:, :, :].rearrange("p g h -> p (g h)").unsqueeze(2)
                                    .broadcast_to([P, NG * HEADS, GI]),
                                    own_image[:, :].unsqueeze(1).broadcast_to([P, NG * HEADS, GI]), ALU.mult))
            assert made == CLASS_V + 8
            for k in (1, 3):
                dve.wait_ge(pre, 12 + k)
                cls_ctx_move(dve.tensor_copy, k)
            dve.wait_ge(pre, 17)
            dve.wait_ge(patch_out, 16 + 16 * NG)
            first(dve.tensor_tensor(patch[:, :], ps[:, 6, 0:C], rows["class_emb"][:, :], ALU.add))

            n2 = 0

            def step(ins):
                nonlocal n2
                n2 += 1
                ins.then_inc(p2v, 1)

            def settled():
                dve.wait_ge(p2v, n2)

            def row_stats(t):
                step(dve.bn_stats(stat6[0:R, t, :], h_rows[0:R, t, :]))
                dve.wait_ge(p2v, n2)
                step(dve.bn_aggr(row_mv[0:R, t, :], stat6[0:R, t, :]))

            def find_rstd(tiles):
                lo, hi = tiles[0], tiles[-1] + 1
                settled()
                step(dve.tensor_scalar(row_var[0:R, lo:hi], row_mv[0:R, lo:hi, 1], EPS, None, ALU.add))
                settled()
                rsqrt(step, settled, row_var[0:R, lo:hi], row_rstd[0:R, lo:hi], hi - lo)
                settled()
                step(dve.scalar_tensor_tensor(out=row_shift[0:R, lo:hi], in0=row_mv[0:R, lo:hi, 0], scalar=-1.0,
                                              in1=row_rstd[0:R, lo:hi], op0=ALU.mult, op1=ALU.mult))

            def lot_stats(i):
                dve.wait_ge(h_in[i], 16 * (len(LOTS[i]) + 1 + (NT - 1 in LOTS[i] and LASTR < R)))
                for t in LOTS[i]:
                    step(dve.bn_stats(stat6[0:R, t, :], h_rows[0:R, t, :]))
                settled()
                for t in LOTS[i]:
                    step(dve.bn_aggr(row_mv[0:R, t, :], stat6[0:R, t, :]))
                find_rstd(LOTS[i])
                assert n2 == LOT_KNOWN[i]

            dve.wait_ge(pad_zero, 1)
            lot_stats(0)
            lot_stats(1)
            for i in range(NT + 3):
                if i == LATE:
                    lot_stats(2)
                if i < NT:
                    dve.wait_ge(sums_done, i + 1)
                    if i >= 4:
                        dve.wait_ge(mixed, i - 3)
                    dve.tensor_tensor(s_slots[0:R, i % 4, :], ps[0:R, 2 + i % 2, 0:R], neg_mask[0:R, :], ALU.add)\
                        .then_inc(sums_masked, 1)
                if 1 <= i <= NT:
                    t = i - 1
                    dve.wait_ge(exped, t + 1)
                    dve.reciprocal(soft2[0:R, t % 4, 2:3], soft2[0:R, t % 4, 1:2]).then_inc(inverted, 1)
                if i < NT:
                    dve.wait_ge(sums_masked, i + 1)
                    dve.tensor_reduce(soft2[0:R, i % 4, 0:1], s_slots[0:R, i % 4, :], AX_X, ALU.max, negate=True)\
                        .then_inc(max_found, 1)
                if i >= 3:
                    t = i - 3
                    dve.wait_ge(mixed, t + 1)
                    dve.tensor_tensor(h_rows[0:R, t, :], h_rows[0:R, t, :], ps[0:R, 4 + t % 2, 0:C], ALU.add)\
                        .then_inc(added, 1)
                    dve.wait_ge(added, t + 1)
                    row_stats(t)
            find_rstd(range(NT))
            assert n2 == LN2_DONE, n2
            lg = logit[0:R, :, :]

            def wide(col):
                return col.unsqueeze(2).broadcast_to([R, NT, E])

            dve.wait_ge(logits_done, NT)
            settled()
            step(dve.tensor_tensor(lg, ps[0:R, 7, 0:NT * E].rearrange("p (t e) -> p t e", t=NT),
                                   wide(row_rstd[0:R, :]), ALU.mult))
            settled()
            step(dve.tensor_reduce(gate_col[0:R, :], lg, AX_X, ALU.max))
            settled()
            step(dve.tensor_tensor(gt1[0:R, :, :], lg, wide(gate_col[0:R, :]), ALU.subtract))
            assert n2 == GATE_MAX
            dve.wait_ge(gate_exp, 1)
            step(dve.tensor_reduce(gate_col[0:R, :], gt1[0:R, :, :], AX_X, ALU.add))
            settled()
            step(dve.reciprocal(gate_col[0:R, :], gate_col[0:R, :]))
            settled()
            step(dve.tensor_tensor(lg, gt1[0:R, :, :], wide(gate_col[0:R, :]), ALU.mult))
            settled()
            rw = rank_w[0:R, :].unsqueeze(1).broadcast_to([R, NT, E])
            for k in range(2):
                left = lg if k == 0 else gt1[0:R, :, :]
                step(dve.tensor_reduce(gate_col[0:R, :], left, AX_X, ALU.max))
                settled()
                step(dve.tensor_tensor(gt2[0:R, :, :], left, wide(gate_col[0:R, :]), ALU.is_equal))
                settled()
                step(dve.tensor_tensor(gt2[0:R, :, :], gt2[0:R, :, :], rw, ALU.mult))
                settled()
                step(dve.tensor_reduce(gate_col[0:R, :], gt2[0:R, :, :], AX_X, ALU.max))
                settled()
                step(dve.tensor_tensor(hot[0:R, k, :, :], gt2[0:R, :, :], wide(gate_col[0:R, :]), ALU.is_equal))
                settled()
                if k == 0:
                    step(dve.scalar_tensor_tensor(out=gt1[0:R, :, :], in0=hot[0:R, 0, :, :].bitcast(F32), scalar=-2.0,
                                                  in1=lg, op0=ALU.mult, op1=ALU.add))
                    settled()
            assert n2 == HOT_DONE, (n2, HOT_DONE)
            dve.wait_ge(ranked, 1)
            first_hot, second_hot = hot[0:R, 0, :, :].bitcast(F32), hot[0:R, 1, :, :].bitcast(F32)
            r1 = ps[0:R, 4, 0:NT * E].rearrange("p (t e) -> p t e", t=NT)
            r2 = ps[0:R, 5, 0:NT * E].rearrange("p (t e) -> p t e", t=NT)
            tk = take[0:R, :, :].rearrange("p (t e) s -> p t e s", t=NT)
            gi = give[0:R, :, :].rearrange("p (t e) s -> p t e s", t=NT)
            for s in range(2):
                step(dve.scalar_tensor_tensor(out=gt1[0:R, :, :], in0=r1, scalar=float(s), in1=first_hot,
                                              op0=ALU.is_equal, op1=ALU.mult))
                step(dve.scalar_tensor_tensor(out=gt2[0:R, :, :], in0=r2, scalar=float(s), in1=second_hot,
                                              op0=ALU.is_equal, op1=ALU.mult))
                settled()
                step(dve.tensor_tensor(tk[:, :, :, s], gt1[0:R, :, :], gt2[0:R, :, :], ALU.add))
                settled()
            by_seq = own_seq[0:R, :].unsqueeze(1).unsqueeze(3).broadcast_to([R, E, TI, CAP])

            def per_slot(dst, src, t, made_sem):
                dve.tensor_tensor(dst[0:R, t % 2, :, :, :],
                                  src[0:R, E * t:E * t + E, :].unsqueeze(2).broadcast_to([R, E, TI, CAP]),
                                  by_seq, ALU.mult).then_inc(made_sem, 1)

            for t in range(NT):
                if t >= 2:
                    dve.wait_ge(disp_done, t - 1)
                per_slot(disp, take, t, disp_made)
            step(dve.tensor_tensor(gi[:, :, :, 0], tk[:, :, :, 0], lg, ALU.mult))
            step(dve.tensor_tensor(gt3[0:R, :, :], first_hot, second_hot, ALU.add))
            settled()
            step(dve.tensor_tensor(gt2[0:R, :, :], gt3[0:R, :, :], lg, ALU.mult))
            settled()
            step(dve.tensor_tensor(gi[:, :, :, 1], gt2[0:R, :, :], gi[:, :, :, 0], ALU.subtract))
            settled()
            for e in range(E):
                b = e % 2
                dve.wait_ge(silu_done, e + 1)
                if e >= 2:
                    dve.wait_ge(down_done, e - 1)
                dve.tensor_tensor(hid[:, b, 1, :], hid[:, b, 0, :], ps[:, 2 * b + 1, 0:SLOTS], ALU.mult)\
                    .then_inc(hid_done, 1)

            def comb_move(t):
                b = t % 2
                dve.wait_ge(outs_turned, t + 1)
                if t >= 2:
                    dve.wait_ge(y_done, t - 1)
                dve.tensor_copy(comb_t[0:EH, b, :, :],
                                ps[0:EH, 2 + b, 0:C].rearrange("p (k r) -> p k r", k=2)[:, :, 0:R])\
                    .then_inc(comb_moved, 1)

            per_slot(comb, give, 0, comb_made)
            per_slot(comb, give, 1, comb_made)
            comb_move(0)
            for t in range(NT):
                b = t % 2
                if t + 2 < NT:
                    dve.wait_ge(outs_turned, t + 1)
                    per_slot(comb, give, t + 2, comb_made)
                if t + 1 < NT:
                    comb_move(t + 1)
                dve.wait_ge(y_done, t + 1)
                if t >= 2:
                    dve.wait_ge(out_sem[b], 16 * (t // 2))
                dve.tensor_tensor(y_rows[0:R, b, :], ps[0:R, 4 + b, 0:C], h_rows[0:R, t, :], ALU.add)\
                    .then_inc(y_made, 1)


def kernel(**inputs):
    import numpy as _np
    import concourse.bacc as _bacc
    from concourse.bass_utils import run_bass_kernel_spmd as _run

    v = {n: _np.asarray(x) for n, x in inputs.items()}
    pad = KFULL * P + KPAD - PIX
    x = v["x"].reshape(NG, GI, CH, SIDE, CS, PS, SIDE, CS, PS).transpose(0, 2, 5, 8, 1, 3, 6, 4, 7)
    x = _np.concatenate([x.reshape(NG, PIX, GT), _np.zeros((NG, pad, GT), _np.float32)], axis=1)
    conv_w = v["L0_tok_conv_w"].reshape(C, PIX).T
    conv_w = _np.concatenate([conv_w, _np.zeros((pad, C), _np.float32)], axis=0)
    arrays = {"x": x, "conv_w": _np.ascontiguousarray(conv_w), "cls_tok": v["cls_tok"]}
    for n in ("class_emb", "la_ln_q_g", "la_ln_q_b", "la_wq", "la_ln_kv_g", "la_ln_kv_b", "la_wkv", "la_proj_w",
              "la_proj_b", "ga_ln_q_g", "ga_ln_q_b", "ga_wq", "ga_ln_kv_g", "ga_ln_kv_b", "ga_wkv", "ga_proj_w",
              "ga_proj_b", "mod_w", "mod_b"):
        arrays[n] = v["L0_tok_" + n]
    for n in ("w_router", "w_fc", "w_gate", "w_proj"):
        arrays[n] = v["L0_ffn_" + n]
    arrays["cols"] = _np.stack([v["L0_tok_" + n].reshape(2, P) for n in COLS]).transpose(2, 0, 1)
    arrays = {n: _np.ascontiguousarray(x) for n, x in arrays.items()}
    nc = _bacc.Bacc("TRN2", target_bir_lowering=False, num_devices=1)
    aps = {n: nc.dram_tensor("in_" + n, x.shape, F32, kind="ExternalInput").ap() for n, x in arrays.items()}
    out = nc.dram_tensor("out_rows", (IMGS * TOK, C), F32, kind="ExternalOutput").ap()
    tower(nc, aps, out)
    r = _run(nc, [{"in_" + n: x for n, x in arrays.items()}], core_ids=[0])
    return r.results[0]["out_rows"].reshape(IMGS, TOK, C)
```
